# Optimizing a Trainium2 kernel written in Bass

```python
import numpy as np
import jax
import jax.numpy as jnp

def _softmax(x, axis=-1):
    return jax.nn.softmax(x, axis=axis)

def _gelu(x):
    return jax.nn.gelu(x, approximate=True)

def _silu(x):
    return jax.nn.silu(x)

def _sigmoid(x):
    return jax.nn.sigmoid(x)

def _layernorm(x, axis=-1, eps=1e-05):
    m = jnp.mean(x, axis=axis, keepdims=True)
    v = jnp.var(x, axis=axis, keepdims=True)
    return (x - m) / jnp.sqrt(v + eps)

def _scatter_add(tgt, idx, src, axis=0):
    return tgt.at[idx].add(src)

def _segment_sum(src, seg, n):
    return jax.ops.segment_sum(src, seg, n)
kernel_name = 'mk_adaln_d4_jaxref_r8_eef339'

def setup_inputs(seed: int=0):
    np.random.seed(seed)
    _w = jnp.asarray

    def _L0_attn_setup():
        import jax, jax.numpy as jnp
        import numpy as np
        N_HEAD = 16
        LATENT = 32

        def _rotate_half(x):
            xe = x[..., ::2]
            xo = x[..., 1::2]
            return jnp.stack((-xo, xe), axis=-1).reshape(x.shape)

        def _rope_tables(T, latent_dim, dtype):
            inv_freq = 1.0 / 10000.0 ** (jnp.arange(0, latent_dim, 2, dtype=jnp.float32) / latent_dim)
            t = jnp.arange(T, dtype=jnp.float32)
            freqs = jnp.outer(t, inv_freq)
            cos = jnp.repeat(jnp.cos(freqs), 2, axis=-1)[:, :latent_dim]
            sin = jnp.repeat(jnp.sin(freqs), 2, axis=-1)[:, :latent_dim]
            return (cos.astype(dtype), sin.astype(dtype))
        key = jax.random.key(seed)
        ks = jax.random.split(key, 14)
        C = 128
        hd = C // N_HEAD
        L = LATENT
        s = 0.02
        return {'x': jax.random.normal(ks[0], (4, 256, C), jnp.float32), 'c_attn_w': jax.random.normal(ks[1], (3 * C, C), jnp.float32) * s, 'c_attn_b': jnp.zeros((3 * C,), jnp.float32), 'q2l_w': jax.random.normal(ks[2], (L, hd), jnp.float32) * s, 'q2l_b': jnp.zeros((L,), jnp.float32), 'kv2l_w': jax.random.normal(ks[3], (L, hd), jnp.float32) * s, 'kv2l_b': jnp.zeros((L,), jnp.float32), 'l2o_w': jax.random.normal(ks[4], (hd, L), jnp.float32) * s, 'l2o_b': jnp.zeros((hd,), jnp.float32), 'wqk_w': jax.random.normal(ks[5], (L, L), jnp.float32) * s, 'wqk_b': jnp.zeros((L,), jnp.float32), 'cproj_w': jax.random.normal(ks[6], (C, C), jnp.float32) * s, 'cproj_b': jnp.zeros((C,), jnp.float32)}
    _L0_attn_in = _L0_attn_setup()

    def _L0_ffn_setup():
        import jax, jax.numpy as jnp
        import numpy as np
        HIDDEN = 128
        NUM_EXPERTS = 8
        TOP_K = 2
        key = jax.random.key(seed)
        k_x, k_r, k_w1, k_w2 = jax.random.split(key, 4)
        x = jax.random.normal(k_x, (4, 256, HIDDEN), dtype=jnp.float32)
        router_w = jax.random.normal(k_r, (NUM_EXPERTS, HIDDEN), dtype=jnp.float32) * HIDDEN ** (-0.5)
        w1 = jax.random.normal(k_w1, (NUM_EXPERTS, HIDDEN, 2 * HIDDEN), dtype=jnp.float32) * HIDDEN ** (-0.5)
        w2 = jax.random.normal(k_w2, (NUM_EXPERTS, 2 * HIDDEN, HIDDEN), dtype=jnp.float32) * (2 * HIDDEN) ** (-0.5)
        return {'x': x, 'router_w': router_w, 'w1': w1, 'w2': w2}
    _L0_ffn_in = _L0_ffn_setup()
    _L0_c = _w((lambda *s: np.random.randn(*s).astype(np.float32) * 0.05)(4, 128))
    _L0_wmod = _w((lambda *s: np.random.randn(*s).astype(np.float32) * 0.05)(128, 6 * 128) * 128 ** (-0.5))

    def _L1_attn_setup():
        import jax, jax.numpy as jnp
        import numpy as np
        B, T, D, H = (8, 512, 128, 64)
        key = jax.random.key(seed)
        ks = jax.random.split(key, 16)
        s = 0.02
        return {'x': jax.random.normal(ks[0], (B, T, D), jnp.float32), 'norm_w': jnp.ones((D,), jnp.float32), 'W1': jax.random.normal(ks[1], (D, D), jnp.float32) * s, 'W2': jax.random.normal(ks[2], (D, D), jnp.float32) * s, 'Wlast': jax.random.normal(ks[3], (D, D), jnp.float32) * s, 'conv_w': jax.random.normal(ks[4], (D, 3), jnp.float32) * s, 'conv_b': jnp.zeros((D,), jnp.float32), 'A': jnp.log(jnp.arange(1, H + 1, dtype=jnp.float32)), 'Bw': jax.random.normal(ks[5], (H, D), jnp.float32) * s, 'Bb': jnp.zeros((H,), jnp.float32), 'Cw': jax.random.normal(ks[6], (D, H), jnp.float32) * s, 'Cb': jnp.zeros((D,), jnp.float32), 'Dw': jax.random.normal(ks[7], (D, D), jnp.float32) * s, 'Db': jnp.zeros((D,), jnp.float32), 'dw': jax.random.normal(ks[8], (H, D), jnp.float32) * s, 'db': jnp.zeros((H,), jnp.float32)}
    _L1_attn_in = _L1_attn_setup()

    def _L1_ffn_setup():
        import jax, jax.numpy as jnp
        import numpy as np
        B, SEQ, D, E, F = (4, 128, 128, 8, 512)
        CAPACITY = 2
        key = jax.random.key(seed)
        ks = jax.random.split(key, 8)
        x = jax.random.normal(ks[0], (B, SEQ, D), jnp.float32)
        gate_weight = jax.random.normal(ks[1], (E, D), jnp.float32) * 0.006
        W1 = jax.random.normal(ks[2], (E, D, F), jnp.float32) * (1.0 / np.sqrt(D))
        b1 = jnp.zeros((E, F), jnp.float32)
        W2 = jax.random.normal(ks[3], (E, F, D), jnp.float32) * (1.0 / np.sqrt(F))
        b2 = jnp.zeros((E, D), jnp.float32)
        Ws1 = jax.random.normal(ks[4], (D, F), jnp.float32) * (1.0 / np.sqrt(D))
        bs1 = jnp.zeros((F,), jnp.float32)
        Ws2 = jax.random.normal(ks[5], (F, D), jnp.float32) * (1.0 / np.sqrt(F))
        bs2 = jnp.zeros((D,), jnp.float32)
        return {'x': x, 'gate_weight': gate_weight, 'W1': W1, 'b1': b1, 'W2': W2, 'b2': b2, 'Ws1': Ws1, 'bs1': bs1, 'Ws2': Ws2, 'bs2': bs2}
    _L1_ffn_in = _L1_ffn_setup()
    _L1_c = _w((lambda *s: np.random.randn(*s).astype(np.float32) * 0.05)(4, 128))
    _L1_wmod = _w((lambda *s: np.random.randn(*s).astype(np.float32) * 0.05)(128, 6 * 128) * 128 ** (-0.5))

    def _L2_attn_setup():
        import jax, jax.numpy as jnp
        import numpy as np
        B, L, IN_DIM = (4, 256, 128)
        H, D = (16, 64)
        OUT_DIM = 128
        key = jax.random.key(seed)
        k1, k2, k3 = jax.random.split(key, 3)
        inputs = jax.random.normal(k1, (B, L, IN_DIM), dtype=jnp.float32)
        W_qkv = jax.random.normal(k2, (IN_DIM, 3 * H * D), dtype=jnp.float32) * IN_DIM ** (-0.5)
        W_out = jax.random.normal(k3, (H * D, OUT_DIM), dtype=jnp.float32) * (H * D) ** (-0.5)
        return {'inputs': inputs, 'W_qkv': W_qkv, 'W_out': W_out}
    _L2_attn_in = _L2_attn_setup()

    def _L2_ffn_setup():
        import jax, jax.numpy as jnp
        import numpy as np
        import math
        BETA = 0.9
        THRESHOLD = 1.0
        NUM_STEPS = 5
        ALPHA = 2.0

        @jax.custom_vjp
        def spike_fn(u):
            return (u > 0).astype(u.dtype)

        def _spike_fwd(u):
            return (spike_fn(u), u)

        def _spike_bwd(u, g):
            s = jnp.pi / 2.0 * ALPHA * u
            return (g * (ALPHA / 2.0) / (1.0 + s * s),)
        spike_fn.defvjp(_spike_fwd, _spike_bwd)
        key = jax.random.key(seed)
        k1, k2, k3 = jax.random.split(key, 3)
        n_embd = 128
        x = jax.random.normal(k1, (4, 256, n_embd), dtype=jnp.float32)
        W_fc = jax.random.normal(k2, (4 * n_embd, n_embd), dtype=jnp.float32) / math.sqrt(n_embd)
        W_proj = jax.random.normal(k3, (n_embd, 4 * n_embd), dtype=jnp.float32) / math.sqrt(4 * n_embd)
        return {'x': x, 'W_fc': W_fc, 'W_proj': W_proj}
    _L2_ffn_in = _L2_ffn_setup()
    _L2_c = _w((lambda *s: np.random.randn(*s).astype(np.float32) * 0.05)(4, 128))
    _L2_wmod = _w((lambda *s: np.random.randn(*s).astype(np.float32) * 0.05)(128, 6 * 128) * 128 ** (-0.5))

    def _L3_attn_setup():
        import jax, jax.numpy as jnp
        import numpy as np
        HIDDEN = 128
        NUM_HEADS = 16
        HEAD_DIM = 64
        NUM_KV_HEADS = 4

        def _xavier(key, out_dim, in_dim):
            limit = jnp.sqrt(6.0 / (in_dim + out_dim)).astype(jnp.float32)
            return jax.random.uniform(key, (out_dim, in_dim), jnp.float32, -limit, limit)
        key = jax.random.key(seed)
        kx, kq, kk, kv, ko = jax.random.split(key, 5)
        return {'hidden_states': jax.random.normal(kx, (2, 256, HIDDEN), jnp.float32), 'Wq': _xavier(kq, NUM_HEADS * HEAD_DIM, HIDDEN), 'Wk': _xavier(kk, NUM_KV_HEADS * HEAD_DIM, HIDDEN), 'Wv': _xavier(kv, NUM_KV_HEADS * HEAD_DIM, HIDDEN), 'Wo': _xavier(ko, HIDDEN, NUM_HEADS * HEAD_DIM)}
    _L3_attn_in = _L3_attn_setup()

    def _L3_ffn_setup():
        import jax, jax.numpy as jnp
        import numpy as np
        D_MODEL = 128
        key = jax.random.key(seed)
        k_x, k_w, k_a1, k_a2 = jax.random.split(key, 4)
        x = jax.random.normal(k_x, (4, 256, D_MODEL), dtype=jnp.float32)
        weight = jax.random.normal(k_w, (D_MODEL, D_MODEL), dtype=jnp.float32) * 0.02
        aux_weight1 = jax.random.normal(k_a1, (D_MODEL, D_MODEL), dtype=jnp.float32) * 0.02
        aux_weight2 = jax.random.normal(k_a2, (D_MODEL, D_MODEL), dtype=jnp.float32) * 0.02
        bias = jnp.zeros((D_MODEL,), dtype=jnp.float32)
        return {'x': x, 'weight': weight, 'aux_weight1': aux_weight1, 'aux_weight2': aux_weight2, 'bias': bias}
    _L3_ffn_in = _L3_ffn_setup()
    _L3_c = _w((lambda *s: np.random.randn(*s).astype(np.float32) * 0.05)(4, 128))
    _L3_wmod = _w((lambda *s: np.random.randn(*s).astype(np.float32) * 0.05)(128, 6 * 128) * 128 ** (-0.5))
    _d = {'L0_attn_x': _L0_attn_in['x'], 'L0_attn_c_attn_w': _L0_attn_in['c_attn_w'], 'L0_attn_c_attn_b': _L0_attn_in['c_attn_b'], 'L0_attn_q2l_w': _L0_attn_in['q2l_w'], 'L0_attn_q2l_b': _L0_attn_in['q2l_b'], 'L0_attn_kv2l_w': _L0_attn_in['kv2l_w'], 'L0_attn_kv2l_b': _L0_attn_in['kv2l_b'], 'L0_attn_l2o_w': _L0_attn_in['l2o_w'], 'L0_attn_l2o_b': _L0_attn_in['l2o_b'], 'L0_attn_wqk_w': _L0_attn_in['wqk_w'], 'L0_attn_wqk_b': _L0_attn_in['wqk_b'], 'L0_attn_cproj_w': _L0_attn_in['cproj_w'], 'L0_attn_cproj_b': _L0_attn_in['cproj_b'], 'L0_ffn_router_w': _L0_ffn_in['router_w'], 'L0_ffn_w1': _L0_ffn_in['w1'], 'L0_ffn_w2': _L0_ffn_in['w2'], 'L0_c': _L0_c, 'L0_wmod': _L0_wmod, 'L1_attn_norm_w': _L1_attn_in['norm_w'], 'L1_attn_W1': _L1_attn_in['W1'], 'L1_attn_W2': _L1_attn_in['W2'], 'L1_attn_Wlast': _L1_attn_in['Wlast'], 'L1_attn_conv_w': _L1_attn_in['conv_w'], 'L1_attn_conv_b': _L1_attn_in['conv_b'], 'L1_attn_A': _L1_attn_in['A'], 'L1_attn_Bw': _L1_attn_in['Bw'], 'L1_attn_Bb': _L1_attn_in['Bb'], 'L1_attn_Cw': _L1_attn_in['Cw'], 'L1_attn_Cb': _L1_attn_in['Cb'], 'L1_attn_Dw': _L1_attn_in['Dw'], 'L1_attn_Db': _L1_attn_in['Db'], 'L1_attn_dw': _L1_attn_in['dw'], 'L1_attn_db': _L1_attn_in['db'], 'L1_ffn_gate_weight': _L1_ffn_in['gate_weight'], 'L1_ffn_W1': _L1_ffn_in['W1'], 'L1_ffn_b1': _L1_ffn_in['b1'], 'L1_ffn_W2': _L1_ffn_in['W2'], 'L1_ffn_b2': _L1_ffn_in['b2'], 'L1_ffn_Ws1': _L1_ffn_in['Ws1'], 'L1_ffn_bs1': _L1_ffn_in['bs1'], 'L1_ffn_Ws2': _L1_ffn_in['Ws2'], 'L1_ffn_bs2': _L1_ffn_in['bs2'], 'L1_c': _L1_c, 'L1_wmod': _L1_wmod, 'L2_attn_W_qkv': _L2_attn_in['W_qkv'], 'L2_attn_W_out': _L2_attn_in['W_out'], 'L2_ffn_W_fc': _L2_ffn_in['W_fc'], 'L2_ffn_W_proj': _L2_ffn_in['W_proj'], 'L2_c': _L2_c, 'L2_wmod': _L2_wmod, 'L3_attn_Wq': _L3_attn_in['Wq'], 'L3_attn_Wk': _L3_attn_in['Wk'], 'L3_attn_Wv': _L3_attn_in['Wv'], 'L3_attn_Wo': _L3_attn_in['Wo'], 'L3_ffn_weight': _L3_ffn_in['weight'], 'L3_ffn_aux_weight1': _L3_ffn_in['aux_weight1'], 'L3_ffn_aux_weight2': _L3_ffn_in['aux_weight2'], 'L3_ffn_bias': _L3_ffn_in['bias'], 'L3_c': _L3_c, 'L3_wmod': _L3_wmod}
    _x0 = _d['L0_attn_x']
    _d['L0_attn_x'] = jax.random.normal(jax.random.fold_in(jax.random.key(seed), 1), (4, 1024, 128), dtype=_x0.dtype)
    del _x0
    return _d

def reference(L0_attn_x, L0_attn_c_attn_w, L0_attn_c_attn_b, L0_attn_q2l_w, L0_attn_q2l_b, L0_attn_kv2l_w, L0_attn_kv2l_b, L0_attn_l2o_w, L0_attn_l2o_b, L0_attn_wqk_w, L0_attn_wqk_b, L0_attn_cproj_w, L0_attn_cproj_b, L0_ffn_router_w, L0_ffn_w1, L0_ffn_w2, L0_c, L0_wmod, L1_attn_norm_w, L1_attn_W1, L1_attn_W2, L1_attn_Wlast, L1_attn_conv_w, L1_attn_conv_b, L1_attn_A, L1_attn_Bw, L1_attn_Bb, L1_attn_Cw, L1_attn_Cb, L1_attn_Dw, L1_attn_Db, L1_attn_dw, L1_attn_db, L1_ffn_gate_weight, L1_ffn_W1, L1_ffn_b1, L1_ffn_W2, L1_ffn_b2, L1_ffn_Ws1, L1_ffn_bs1, L1_ffn_Ws2, L1_ffn_bs2, L1_c, L1_wmod, L2_attn_W_qkv, L2_attn_W_out, L2_ffn_W_fc, L2_ffn_W_proj, L2_c, L2_wmod, L3_attn_Wq, L3_attn_Wk, L3_attn_Wv, L3_attn_Wo, L3_ffn_weight, L3_ffn_aux_weight1, L3_ffn_aux_weight2, L3_ffn_bias, L3_c, L3_wmod):

    def _L0_attn_ref(x, c_attn_w, c_attn_b, q2l_w, q2l_b, kv2l_w, kv2l_b, l2o_w, l2o_b, wqk_w, wqk_b, cproj_w, cproj_b):
        import jax, jax.numpy as jnp
        import numpy as np
        N_HEAD = 16
        LATENT = 32

        def _rotate_half(x):
            xe = x[..., ::2]
            xo = x[..., 1::2]
            return jnp.stack((-xo, xe), axis=-1).reshape(x.shape)

        def _rope_tables(T, latent_dim, dtype):
            inv_freq = 1.0 / 10000.0 ** (jnp.arange(0, latent_dim, 2, dtype=jnp.float32) / latent_dim)
            t = jnp.arange(T, dtype=jnp.float32)
            freqs = jnp.outer(t, inv_freq)
            cos = jnp.repeat(jnp.cos(freqs), 2, axis=-1)[:, :latent_dim]
            sin = jnp.repeat(jnp.sin(freqs), 2, axis=-1)[:, :latent_dim]
            return (cos.astype(dtype), sin.astype(dtype))
        B, T, C = x.shape
        H = N_HEAD
        hd = C // H
        L = q2l_w.shape[0]
        qkv = x @ c_attn_w.T + c_attn_b
        q, k, v = jnp.split(qkv, 3, axis=2)

        def heads(t):
            return t.reshape(B, T, H, hd).transpose(0, 2, 1, 3)
        q, k, v = (heads(q), heads(k), heads(v))
        q_lat = q @ q2l_w.T + q2l_b
        k_lat = k @ kv2l_w.T + kv2l_b
        v_lat = v @ kv2l_w.T + kv2l_b
        cos, sin = _rope_tables(T, L, x.dtype)
        cos = cos[None, None]
        sin = sin[None, None]
        q_lat = q_lat * cos + _rotate_half(q_lat) * sin
        k_lat = k_lat * cos + _rotate_half(k_lat) * sin
        q_for_k = q_lat @ wqk_w.T + wqk_b
        att = jnp.einsum('bhql,bhkl->bhqk', q_for_k, k_lat) * L ** (-0.5)
        causal = jnp.tril(jnp.ones((T, T), dtype=bool))
        att = jnp.where(causal[None, None], att, -jnp.inf)
        att = jax.nn.softmax(att, axis=-1)
        y_lat = jnp.einsum('bhqk,bhkl->bhql', att, v_lat)
        y = y_lat @ l2o_w.T + l2o_b
        y = y.transpose(0, 2, 1, 3).reshape(B, T, C)
        return y @ cproj_w.T + cproj_b

    def _L0_ffn_ref(x, router_w, w1, w2):
        import jax, jax.numpy as jnp
        import numpy as np
        HIDDEN = 128
        NUM_EXPERTS = 8
        TOP_K = 2
        bsz, seq, hidden = x.shape
        tokens = x.reshape(-1, hidden)
        logits = tokens @ router_w.T
        topk_vals, topk_idx = jax.lax.top_k(logits, TOP_K)
        weights = jax.nn.softmax(topk_vals, axis=-1)
        h = jnp.einsum('td,edf->etf', tokens, w1)
        h = jax.nn.gelu(h, approximate=False)
        out_all = jnp.einsum('etf,efd->etd', h, w2)
        out_ted = jnp.transpose(out_all, (1, 0, 2))
        gathered = jnp.take_along_axis(out_ted, topk_idx[:, :, None], axis=1)
        output = jnp.sum(weights[:, :, None] * gathered, axis=1)
        return output.reshape(bsz, seq, hidden)

    def _L1_attn_ref(x, norm_w, W1, W2, Wlast, conv_w, conv_b, A, Bw, Bb, Cw, Cb, Dw, Db, dw, db):
        import jax, jax.numpy as jnp
        import numpy as np
        B, T, D, H = (8, 512, 128, 64)
        eps = jnp.finfo(x.dtype).eps
        res = x
        xn = x * jax.lax.rsqrt(jnp.mean(x * x, axis=-1, keepdims=True) + eps) * norm_w
        x_b = xn @ W1.T
        z = xn @ W2.T
        xp = jnp.pad(x_b, ((0, 0), (2, 0), (0, 0)))
        xc = xp[:, :-2] * conv_w[:, 0] + xp[:, 1:-1] * conv_w[:, 1] + xp[:, 2:] * conv_w[:, 2] + conv_b
        xc = jax.nn.silu(xc)
        delta = jax.nn.softplus(xc @ dw.T + db)
        A_log = -jax.nn.softplus(A)
        A_bar_log = delta * A_log
        B_bar = delta * (xc @ Bw.T + Bb)
        A_cum = jnp.clip(jnp.cumsum(A_bar_log, axis=1), -20.0, 20.0)
        A_shift = jnp.concatenate([jnp.zeros_like(A_cum[:, :1]), A_cum[:, :-1]], axis=1)
        h = jnp.exp(A_cum) * jnp.cumsum(B_bar * jnp.exp(-A_shift), axis=1)
        y = h @ Cw.T + Cb + (xc @ Dw.T + Db)
        out = y * jax.nn.silu(z) @ Wlast.T + res
        return out

    def _L1_ffn_ref(x, gate_weight, W1, b1, W2, b2, Ws1, bs1, Ws2, bs2):
        import jax, jax.numpy as jnp
        import numpy as np
        B, SEQ, D, E, F = (4, 128, 128, 8, 512)
        CAPACITY = 2
        Bb, s, Dd = x.shape
        Ee = gate_weight.shape[0]
        xf = x.reshape(-1, Dd)
        S = xf.shape[0]
        logits = xf @ gate_weight.T
        scores = jax.nn.softmax(logits, axis=-1).T
        k = S * CAPACITY
        vals, idx = jax.lax.top_k(scores.reshape(-1), k)
        eidx = idx // S
        tidx = idx % S
        gate = jnp.zeros((Ee, S), x.dtype).at[eidx, tidx].add(vals)
        h = jax.nn.gelu(jnp.einsum('sd,edf->esf', xf, W1) + b1[:, None, :], approximate=True)
        y = jnp.einsum('esf,efd->esd', h, W2) + b2[:, None, :]
        out = jnp.einsum('es,esd->sd', gate, y)
        shared = jax.nn.gelu(xf @ Ws1 + bs1, approximate=True) @ Ws2 + bs2
        out = out + shared
        return out.reshape(Bb, s, Dd)

    def _L2_attn_ref(inputs, W_qkv, W_out):
        import jax, jax.numpy as jnp
        import numpy as np
        B, L, IN_DIM = (4, 256, 128)
        H, D = (16, 64)
        OUT_DIM = 128
        b, l, _ = inputs.shape
        qkv = inputs @ W_qkv
        q, k, v = jnp.split(qkv, 3, axis=-1)
        q = q.reshape(b, l, H, D)
        k = k.reshape(b, l, H, D)
        v = v.reshape(b, l, H, D)
        score = jnp.einsum('bihd,bjhd->bijh', q, k) / D ** 0.5
        mask = jnp.tril(jnp.ones((l, l), dtype=score.dtype))[None, :, :, None]
        masked_score = score * mask + 1e+30 * (mask - 1.0)
        wmat = jax.nn.softmax(masked_score, axis=2)
        out = jnp.einsum('bijh,bjhd->bihd', wmat, v).reshape(b, l, H * D)
        return out @ W_out

    def _L2_ffn_ref(x, W_fc, W_proj):
        import jax, jax.numpy as jnp
        import numpy as np
        import math
        BETA = 0.9
        THRESHOLD = 1.0
        NUM_STEPS = 5
        ALPHA = 2.0

        @jax.custom_vjp
        def spike_fn(u):
            return (u > 0).astype(u.dtype)

        def _spike_fwd(u):
            return (spike_fn(u), u)

        def _spike_bwd(u, g):
            s = jnp.pi / 2.0 * ALPHA * u
            return (g * (ALPHA / 2.0) / (1.0 + s * s),)
        spike_fn.defvjp(_spike_fwd, _spike_bwd)
        h = jnp.square(jax.nn.relu(jnp.einsum('bsd,fd->bsf', x, W_fc)))
        y = jnp.einsum('bsf,df->bsd', h, W_proj)

        def step(mem, _):
            reset = jax.lax.stop_gradient(spike_fn(mem - THRESHOLD))
            mem_new = BETA * mem + y - reset * THRESHOLD
            spk = spike_fn(mem_new - THRESHOLD)
            return (mem_new, spk)
        mem0 = jnp.zeros_like(y)
        _, spks = jax.lax.scan(step, mem0, None, length=NUM_STEPS)
        return jnp.sum(spks, axis=0) / NUM_STEPS

    def _L3_attn_ref(hidden_states, Wq, Wk, Wv, Wo):
        import jax, jax.numpy as jnp
        import numpy as np
        HIDDEN = 128
        NUM_HEADS = 16
        HEAD_DIM = 64
        NUM_KV_HEADS = 4

        def _xavier(key, out_dim, in_dim):
            limit = jnp.sqrt(6.0 / (in_dim + out_dim)).astype(jnp.float32)
            return jax.random.uniform(key, (out_dim, in_dim), jnp.float32, -limit, limit)
        B, S, _ = hidden_states.shape
        q = (hidden_states @ Wq.T).reshape(B, S, NUM_HEADS, HEAD_DIM).transpose(0, 2, 1, 3)
        k = (hidden_states @ Wk.T).reshape(B, S, NUM_KV_HEADS, HEAD_DIM).transpose(0, 2, 1, 3)
        v = (hidden_states @ Wv.T).reshape(B, S, NUM_KV_HEADS, HEAD_DIM).transpose(0, 2, 1, 3)
        n_rep = NUM_HEADS // NUM_KV_HEADS
        if n_rep > 1:
            k = jnp.repeat(k, n_rep, axis=1)
            v = jnp.repeat(v, n_rep, axis=1)
        scale = HEAD_DIM ** (-0.5)
        scores = jnp.einsum('bhqd,bhkd->bhqk', q, k) * scale
        causal = jnp.triu(jnp.full((S, S), -jnp.inf, dtype=scores.dtype), k=1)
        scores = scores + causal[None, None]
        probs = jax.nn.softmax(scores, axis=-1)
        out = jnp.einsum('bhqk,bhkd->bhqd', probs, v)
        out = out.transpose(0, 2, 1, 3).reshape(B, S, NUM_HEADS * HEAD_DIM)
        return out @ Wo.T

    def _L3_ffn_ref(x, weight, aux_weight1, aux_weight2, bias):
        import jax, jax.numpy as jnp
        import numpy as np
        D_MODEL = 128
        h = jnp.einsum('btc,cd->btd', x, weight)
        h = jnp.einsum('btc,cd->btd', h, aux_weight1)
        h = jnp.einsum('btc,cd->btd', h, aux_weight2)
        return jnp.tanh(h + bias)
    x = L0_attn_x
    mod = (_silu(L0_c) @ L0_wmod).reshape(L0_c.shape[0], 6, 1, -1)
    sa, ca, ga, sb, cb, gb = (mod[:, 0], mod[:, 1], mod[:, 2], mod[:, 3], mod[:, 4], mod[:, 5])
    ga = (2 * (ga >= 0) - 1) * jnp.maximum(jnp.abs(ga), 0.25)
    gb = (2 * (gb >= 0) - 1) * jnp.maximum(jnp.abs(gb), 0.25)
    h = _layernorm(x, axis=-1) * (1 + ca) + sa
    x = x + ga * _L0_attn_ref(h, L0_attn_c_attn_w, L0_attn_c_attn_b, L0_attn_q2l_w, L0_attn_q2l_b, L0_attn_kv2l_w, L0_attn_kv2l_b, L0_attn_l2o_w, L0_attn_l2o_b, L0_attn_wqk_w, L0_attn_wqk_b, L0_attn_cproj_w, L0_attn_cproj_b)
    h = _layernorm(x, axis=-1) * (1 + cb) + sb
    x = x + gb * _L0_ffn_ref(h, L0_ffn_router_w, L0_ffn_w1, L0_ffn_w2)
    mod = (_silu(L1_c) @ L1_wmod).reshape(L1_c.shape[0], 6, 1, -1)
    sa, ca, ga, sb, cb, gb = (mod[:, 0], mod[:, 1], mod[:, 2], mod[:, 3], mod[:, 4], mod[:, 5])
    ga = (2 * (ga >= 0) - 1) * jnp.maximum(jnp.abs(ga), 0.25)
    gb = (2 * (gb >= 0) - 1) * jnp.maximum(jnp.abs(gb), 0.25)
    h = _layernorm(x, axis=-1) * (1 + ca) + sa
    x = x + ga * _L1_attn_ref(h, L1_attn_norm_w, L1_attn_W1, L1_attn_W2, L1_attn_Wlast, L1_attn_conv_w, L1_attn_conv_b, L1_attn_A, L1_attn_Bw, L1_attn_Bb, L1_attn_Cw, L1_attn_Cb, L1_attn_Dw, L1_attn_Db, L1_attn_dw, L1_attn_db)
    h = _layernorm(x, axis=-1) * (1 + cb) + sb
    x = x + gb * _L1_ffn_ref(h, L1_ffn_gate_weight, L1_ffn_W1, L1_ffn_b1, L1_ffn_W2, L1_ffn_b2, L1_ffn_Ws1, L1_ffn_bs1, L1_ffn_Ws2, L1_ffn_bs2)
    mod = (_silu(L2_c) @ L2_wmod).reshape(L2_c.shape[0], 6, 1, -1)
    sa, ca, ga, sb, cb, gb = (mod[:, 0], mod[:, 1], mod[:, 2], mod[:, 3], mod[:, 4], mod[:, 5])
    ga = (2 * (ga >= 0) - 1) * jnp.maximum(jnp.abs(ga), 0.25)
    gb = (2 * (gb >= 0) - 1) * jnp.maximum(jnp.abs(gb), 0.25)
    h = _layernorm(x, axis=-1) * (1 + ca) + sa
    x = x + ga * _L2_attn_ref(h, L2_attn_W_qkv, L2_attn_W_out)
    h = _layernorm(x, axis=-1) * (1 + cb) + sb
    x = x + gb * _L2_ffn_ref(h, L2_ffn_W_fc, L2_ffn_W_proj)
    mod = (_silu(L3_c) @ L3_wmod).reshape(L3_c.shape[0], 6, 1, -1)
    sa, ca, ga, sb, cb, gb = (mod[:, 0], mod[:, 1], mod[:, 2], mod[:, 3], mod[:, 4], mod[:, 5])
    ga = (2 * (ga >= 0) - 1) * jnp.maximum(jnp.abs(ga), 0.25)
    gb = (2 * (gb >= 0) - 1) * jnp.maximum(jnp.abs(gb), 0.25)
    h = _layernorm(x, axis=-1) * (1 + ca) + sa
    x = x + ga * _L3_attn_ref(h, L3_attn_Wq, L3_attn_Wk, L3_attn_Wv, L3_attn_Wo)
    h = _layernorm(x, axis=-1) * (1 + cb) + sb
    x = x + gb * _L3_ffn_ref(h, L3_ffn_weight, L3_ffn_aux_weight1, L3_ffn_aux_weight2, L3_ffn_bias)
    return x

_drawn_inputs = setup_inputs


def setup_inputs(seed=0):
    import zlib

    import numpy as np

    out = dict(_drawn_inputs(seed))
    spreads = {'L0_attn_c_attn_b': (0.0, 0.8),
     'L0_attn_q2l_b': (0.0, 0.8),
     'L0_attn_kv2l_b': (0.0, 0.8),
     'L0_attn_l2o_b': (0.0, 0.673),
     'L0_attn_wqk_b': (0.0, 0.8),
     'L0_attn_cproj_b': (0.0, 0.1),
     'L1_attn_norm_w': (1.0, 0.6),
     'L1_attn_conv_b': (0.0, 0.8),
     'L1_attn_Bb': (0.0, 0.1),
     'L1_attn_Cb': (0.0, 2.0),
     'L1_attn_Db': (0.0, 2.0),
     'L1_attn_db': (0.0, 0.8),
     'L1_ffn_b1': (0.0, 2.0),
     'L1_ffn_b2': (0.0, 0.8),
     'L1_ffn_bs1': (0.0, 0.464),
     'L1_ffn_bs2': (0.0, 0.343),
     'L3_ffn_bias': (0.0, 1.752)}
    factors = {'L0_attn_c_attn_w': 8.0,
     'L0_attn_q2l_w': 8.0,
     'L0_attn_kv2l_w': 8.0,
     'L0_attn_l2o_w': 8.0,
     'L0_attn_wqk_w': 8.0,
     'L0_attn_cproj_w': 5.429,
     'L1_attn_W1': 8.0,
     'L1_attn_conv_w': 8.0,
     'L1_attn_A': 64.0,
     'L1_attn_Bw': 8.0,
     'L1_attn_Dw': 40.947,
     'L1_attn_dw': 8.0,
     'L3_attn_Wq': 4.586,
     'L3_attn_Wk': 4.583,
     'L3_ffn_weight': 8.0,
     'L3_ffn_aux_weight1': 8.0,
     'L3_ffn_aux_weight2': 8.0}
    for name, (base, spread) in spreads.items():
        noise = np.random.default_rng([zlib.crc32(name.encode()), seed]).standard_normal(out[name].shape)
        drawn = base * np.exp(spread * noise) if base else spread * noise
        out[name] = jnp.asarray(drawn.astype(out[name].dtype))
    for name, factor in factors.items():
        out[name] = (out[name] * factor).astype(out[name].dtype)
    return out
```

```python
from contextlib import ExitStack

import numpy as np

import concourse.bass as bass
from concourse import mybir

F32, BF16, I32, U32, F32R = (mybir.dt.float32, mybir.dt.bfloat16, mybir.dt.int32, mybir.dt.uint32,
                             mybir.dt.float32r)
ALU, ACT, AX = mybir.AluOpType, mybir.ActivationFunctionType, mybir.AxisListType.X
ds = bass.ds

P = 128
B, T, C = 4, 1024, 128
NT = T // P
NTILES = B * NT
CHUNK = 512
NCH = T // CHUNK
LAYERS = 4
DEBUG = False
SA, CA, GA, SB, CB, GB = range(6)
LN_EPS = 1e-5
RMS_EPS = float(np.finfo(np.float32).eps)
EXPERTS = 8
TOPK_ALL = B * T * 2
MASKED = 1e30
LATENT_DIM = 32
SEQ_STEPS = 5


class Ctx(dict):
    def __getattr__(self, name):
        return self[name]


def open_sb(nc, ctx, t, **shapes):
    for name, (shape, dt) in shapes.items():
        t[name] = ctx.enter_context(nc.sbuf_tensor(name, shape, dt))


def open_sems(nc, ctx, t, prefix, names):
    for n in names.split():
        t[n] = ctx.enter_context(nc.semaphore(prefix + n))
        t.finished.append(t[n])


def bc_tiles(row, n):
    return row.unsqueeze(1).to_broadcast([P, n, row.shape[-1]])


def bc_last(col, n):
    return col.unsqueeze(2).to_broadcast([P, col.shape[-1], n])


def await_loads(eng, t, names):
    for sem, count in {str(t.loads[n][0]): t.loads[n] for n in names.split()}.values():
        eng.wait_ge(sem, count)


APART = {}


def wait_apart(eng, sem, value):
    eng.wait_ge(sem, value)
    eng.sem_inc(APART["sem"], 1)


LN_SEMS = "ln_stats ln_aggr ln_eps ln_rstd ln_xn ln_tr hT_ready"


def open_ln(nc, ctx, t, tag):
    open_sb(nc, ctx, t, **{
        "ln_st" + tag: ([P, NT, 6], F32), "ln_mv" + tag: ([P, NT, 2], F32), "ln_ve" + tag: ([P, NT], F32),
        "ln_rs" + tag: ([P, NT], F32), "xn" + tag: ([P, NT, C], F32)})
    for n in ("ln_st", "ln_mv", "ln_ve", "ln_rs", "xn"):
        t[n] = t[n + tag]


def ln_vector_normalise(nc, dve, t, b):
    for j in range(NT):
        nc.vector.bn_stats(t.ln_st[:, j, :], t.x[:, ds(b * NT + j, 1), :]).then_inc(t.ln_stats, 1)
    wait_apart(dve, t.ln_stats, b * NT + NT)
    for j in range(NT):
        nc.vector.bn_aggr(t.ln_mv[:, j, :], t.ln_st[:, j, :]).then_inc(t.ln_aggr, 1)
    dve.wait_ge(t.ln_rstd, b + 1)
    for j in range(NT):
        nc.vector.tensor_scalar(t.xn[:, j, :], t.x[:, ds(b * NT + j, 1), :], t.ln_mv[:, j, 0:1],
                                t.ln_rs[:, j:j + 1], ALU.subtract, ALU.mult).then_inc(t.ln_xn, 1)


def ln_pool_rstd(nc, pool, t, b):
    wait_apart(pool, t.ln_aggr, b * NT + NT)
    nc.gpsimd.tensor_scalar(t.ln_ve[:, :], t.ln_mv[:, :, 1], LN_EPS, None, ALU.add).then_inc(t.ln_eps, 1)
    pool.wait_ge(t.ln_eps, b + 1)
    nc.gpsimd.tensor_tensor(t.ln_rs[:, :], t.ln_ve[:, :], t.minus_half[:, 0:NT], ALU.pow).then_inc(t.ln_rstd, 1)


def ln_tensor_transpose(nc, pe, t, b):
    for j in range(NT):
        if j % 4 == 0:
            pe.wait_ge(t.ln_xn, b * NT + (j + 4))
        mm = nc.tensor.transpose(t.ps_t[j // 4][:, (j % 4) * P:(j % 4 + 1) * P], t.xn[:, j, :], t.ident[:, :])
        if j % 4 == 3:
            mm.then_inc(t.ln_tr, 1)


def ln_vector_modulate(nc, dve, t, b, layer, scale, shift, hT):
    for c in range(NCH):
        dve.wait_ge(t.ln_tr, b * NCH + (c + 1))
        nc.vector.tensor_scalar(hT[c], t.ps_t[c][:, :], t.modT[:, ds(b + (layer * 6 + scale) * B, 1)],
                                t.modT[:, ds(b + (layer * 6 + shift) * B, 1)], ALU.mult, ALU.add)\
            .then_inc(t.hT_ready, 1)


def setup(nc, t, dram, weights):
    with ExitStack() as ctx:
        open_sb(nc, ctx, t, cT=([P, LAYERS * B], F32), sil=([P, LAYERS * B], F32),
                wmod=([P, LAYERS, 6 * C], F32), sil_rep=([P, LAYERS * B, P], F32),
                g_sign=([P, 2 * C], F32), g_abs=([P, 2 * C], F32))
        open_sems(nc, ctx, t, "setup_", "c_loaded wmod_loaded sil_done rep_done const_done id_zero id_done "
                  "mod_ps rows_ps mod_done sign_done abs_done rows_done")
        with nc.Block() as block:
            @block.sync
            def _(sp):
                sp.dma_start(t.cT[:, :], dram["cT"]).then_inc(t.c_loaded, 16)
                sp.dma_start(t.wmod[:, :, :], dram["wmod"].rearrange("l p n -> p l n")).then_inc(t.wmod_loaded, 16)
                sp.dma_start(t.x[:, :, :], dram["x"].rearrange("(n p) c -> p n c", p=P)).then_inc(t.x_loaded, 16)
                for name, dst, src in weights:
                    sp.dma_start(dst, src).then_inc(t.loads[name][0], 16)
                if DEBUG:
                    await_loads(sp, t, " ".join(name for name, _, _ in weights))
                    sp.wait_ge(t.x_loaded, 16)

            @block.gpsimd
            def _(pool):
                nc.gpsimd.memset(t.minus_half[:, :], -0.5).then_inc(t.id_zero, 1)
                nc.gpsimd.memset(t.ones[:, :], 1.0).then_inc(t.id_zero, 1)
                for m in (t.ident, t.ident16, t.maskp, t.tri):
                    nc.gpsimd.memset(m[:, :], 0.0).then_inc(t.id_zero, 1)
                pool.wait_ge(t.id_zero, 6)
                for m in (t.ident, t.ident16):
                    nc.gpsimd.affine_select(out=m[:, :], in_=m[:, :], compare_op=ALU.not_equal, fill=1.0, base=0,
                                            pattern=[[-1, P]], channel_multiplier=1).then_inc(t.id_done, 1)
                nc.gpsimd.affine_select(out=t.maskp[:, :], in_=t.maskp[:, :], compare_op=ALU.is_ge, fill=MASKED,
                                        base=0, pattern=[[-1, P]], channel_multiplier=1).then_inc(t.id_done, 1)
                nc.gpsimd.affine_select(out=t.tri[:, :], in_=t.tri[:, :], compare_op=ALU.is_ge, fill=1.0,
                                        base=0, pattern=[[-1, P]], channel_multiplier=1).then_inc(t.id_done, 1)

            @block.scalar
            def _(act):
                act.wait_ge(t.c_loaded, 16)
                nc.scalar.activation(t.sil[:, :], t.cT[:, :], ACT.Silu).then_inc(t.sil_done, 1)

            @block.tensor
            def _(pe):
                pe.wait_ge(t.sil_done, 1)
                pe.wait_ge(t.wmod_loaded, 16)
                for l in range(LAYERS):
                    for j in range(6):
                        at = (l * 6 + j) * B
                        mm = nc.tensor.matmul(t.ps_o[0][:, at:at + B], t.wmod[:, l, j * C:(j + 1) * C],
                                              t.sil[:, l * B:(l + 1) * B], start=True, stop=True)
                mm.then_inc(t.mod_ps, 1)
                pe.wait_ge(t.rep_done, LAYERS * B)
                for n in range(LAYERS * B):
                    l = n // B
                    if n >= 2:
                        pe.wait_ge(t.rows_done, n - 1)
                    ps = t.ps_t[n % 2]
                    for i, j in enumerate((GA, GB) + ((SA, CA) if l == 1 else ())):
                        mm = nc.tensor.matmul(ps[:, i * C:(i + 1) * C], t.sil_rep[:, n, :],
                                              t.wmod[:, l, j * C:(j + 1) * C], start=True, stop=True)
                    mm.then_inc(t.rows_ps, 1)

            @block.vector
            def _(dve):
                dve.wait_ge(t.sil_done, 1)
                for n in range(LAYERS * B):
                    nc.vector.tensor_copy(t.sil_rep[:, n, :], t.sil[:, n:n + 1].to_broadcast([P, P]))\
                        .then_inc(t.rep_done, 1)
                dve.wait_ge(t.mod_ps, 1)
                for l in range(LAYERS):
                    for j in range(6):
                        at = (l * 6 + j) * B
                        nc.vector.tensor_scalar(t.modT[:, at:at + B], t.ps_o[0][:, at:at + B],
                                                1.0 if j in (CA, CB) else 0.0, None, ALU.add).then_inc(t.mod_done, 1)
                for n in range(LAYERS * B):
                    l, b = n // B, n % B
                    ps = t.ps_t[n % 2]
                    dve.wait_ge(t.rows_ps, n + 1)
                    if n >= 1:
                        dve.wait_ge(t.rows_done, n)
                    nc.vector.tensor_scalar(t.g_sign[:, :], ps[:, 0:2 * C], 0.0, 2.0, ALU.is_ge, ALU.mult)\
                        .then_inc(t.sign_done, 1)
                    dve.wait_ge(t.sign_done, 2 * n + 1)
                    nc.vector.tensor_scalar(t.g_sign[:, :], t.g_sign[:, :], -1.0, None, ALU.add).then_inc(t.sign_done, 1)
                    dve.wait_ge(t.sign_done, 2 * n + 2)
                    nc.vector.tensor_tensor(t.g_abs[:, :], ps[:, 0:2 * C], t.g_sign[:, :], ALU.mult).then_inc(t.abs_done, 1)
                    if l == 1:
                        nc.vector.tensor_copy(t.sa_rows[:, b, :], ps[:, 2 * C:3 * C]).then_inc(t.mod_done, 1)
                        nc.vector.tensor_scalar(t.ca_rows[:, b, :], ps[:, 3 * C:4 * C], 1.0, None, ALU.add)\
                            .then_inc(t.mod_done, 1)
                    dve.wait_ge(t.abs_done, n + 1)
                    nc.vector.scalar_tensor_tensor(out=t.gate_rows[:, n, :], in0=t.g_abs[:, :], scalar=0.25,
                                                   in1=t.g_sign[:, :], op0=ALU.max, op1=ALU.mult)\
                        .then_inc(t.rows_done, 1)


def attention(nc, t, layer, groups, heads, project, w_stage, before=None):
    D = C // heads
    STEPS = heads * NT
    tag = f"_L{layer}"
    chunks = []
    of_step = []
    for s in range(STEPS):
        n = s % NT + 1
        of_step.append([])
        for k in range(0, n, 4):
            of_step[s].append(len(chunks))
            chunks.append((s, k, min(4, n - k)))
    NCK = len(chunks)
    on = [int(c % 6 != 0) for c in range(NCK)]
    until = [on.count(e) for e in (0, 1)]
    OCH = (groups + 3) // 4
    SETS = NT * OCH // 2

    def seen(c):
        return on[:c + 1].count(on[c])

    with ExitStack() as ctx:
        open_ln(nc, ctx, t, tag)
        open_sb(nc, ctx, t, **{
            "hT" + tag: ([P, T], F32), "wbuf" + tag: ([P, project.w_cols], F32),
            "qs" + tag: ([P, heads, T], F32R), "ks" + tag: ([P, project.k_heads, project.k_parts, T], F32R), "vv" + tag: ([P, NT, C], F32), "pp" + tag: ([P, 2, T], F32),
            "pT" + tag: ([P, 2, T], F32), "nmax" + tag: ([P, 4], F32), "rsum" + tag: ([P, 4], F32),
            "rinv" + tag: ([P, 4], F32), "o_all" + tag: ([P, NT, groups * C], F32),
            "oT" + tag: ([P, 2, groups * C], F32), "att_out" + tag: ([P, C], F32)})
        for n in ("hT", "wbuf", "qs", "ks", "vv", "pp", "pT", "nmax", "rsum", "rinv", "o_all", "oT", "att_out"):
            t[n] = t[n + tag]
        open_sems(nc, ctx, t, f"att{layer}_", LN_SEMS + " w_here v_done q_done k_done q_hi k_hi q_ready k_ready v_ready "
                  "s_done max_done exp_done tr_done evac0 evac1 av_done rinv_done o_done "
                  "otr_done oevac0 oevac1 out_done scaled_done x_done" + project.sems)
        evac = (t.evac0, t.evac1)
        oevac = (t.oevac0, t.oevac1)
        if before:
            before(nc, t)
        with nc.Block() as block:
            w_stage(nc, block, t, groups)

            def copy_chunk(eng, copy, n, c):
                s, k, m = chunks[c]
                eng.wait_ge(t.tr_done, n * NCK + (c + 1))
                if s >= 2:
                    eng.wait_ge(t.av_done, n * STEPS + (s - 1))
                copy(t.pT[:, s % 2, k * P:(k + m) * P], t.ps_t[c % 2][:, 0:m * P]).then_inc(evac[on[c]], 1)

            def copy_out_chunk(eng, copy, b, i, u):
                c = i * OCH + u
                m = min(4, groups - 4 * u)
                eng.wait_ge(t.otr_done, b * NT * OCH + (c + 1))
                if i >= 2:
                    eng.wait_ge(t.out_done, b * NT + (i - 1))
                copy(t.oT[:, i % 2, u * 4 * P:(u * 4 + m) * P], t.ps_t[c % 2][:, 0:m * P]).then_inc(oevac[c % 2], 1)

            @block.tensor
            def _(pe):
                def scores(n, s):
                    a, i = s // NT, s % NT
                    w = (i + 1) * P
                    if s >= 2:
                        pe.wait_ge(t.exp_done, n * STEPS + (s - 1))
                    ps = t.ps_s[s % 2]
                    for k0 in range(0, w, CHUNK):
                        k1 = min(w, k0 + CHUNK)
                        for part in range(project.k_parts):
                            nc.tensor.matmul(ps[:, k0:k1], t.qs[:, a, i * P:(i + 1) * P],
                                             t.ks[:, a % project.k_heads, part, k0:k1], start=(part == 0),
                                             stop=(k1 < w and part == project.k_parts - 1))
                    nc.tensor.matmul(ps[:, i * P:w], t.ident16[:, :], t.maskp[:, :],
                                     start=False, stop=True).then_inc(t.s_done, 1)

                def transposes(n, s):
                    pe.wait_ge(t.exp_done, n * STEPS + (s + 1))
                    for c in of_step[s]:
                        _, k, m = chunks[c]
                        if c >= 2:
                            pe.wait_ge(evac[on[c - 2]], n * until[on[c - 2]] + seen(c - 2))
                        for q in range(m):
                            mm = nc.tensor.transpose(t.ps_t[c % 2][:, q * P:(q + 1) * P],
                                                     t.pp[:, s % 2, (k + q) * P:(k + q + 1) * P], t.ident[:, :])
                        mm.then_inc(t.tr_done, 1)

                def values(n, s):
                    a, i = s // NT, s % NT
                    for c in of_step[s]:
                        pe.wait_ge(evac[on[c]], n * until[on[c]] + seen(c))
                    if s >= 2:
                        pe.wait_ge(t.o_done, n * STEPS + (s - 1))
                    for k in range(i + 1):
                        mm = nc.tensor.matmul(t.ps_o[s % 2][:, 0:D], t.pT[:, s % 2, k * P:(k + 1) * P],
                                              t.vv[:, k, a * D:(a + 1) * D], start=(k == 0), stop=(k == i))
                    mm.then_inc(t.av_done, 1)

                with pe.Fori(0, B) as b:
                    ln_tensor_transpose(nc, pe, t, b)
                    wait_apart(pe, t.hT_ready, b * NCH + NCH)
                    with pe.Fori(0, groups) as g:
                        n = b * groups + g
                        project.tensor(nc, pe, t, n)
                        pe.wait_ge(t.q_ready, n * heads + heads)
                        pe.wait_ge(t.k_ready, n * project.k_heads + project.k_heads)
                        pe.wait_ge(t.v_ready, n * NCH + (NCH + 1))
                        scores(n, 0)
                        for s in range(STEPS + 2):
                            if s + 1 < STEPS:
                                scores(n, s + 1)
                            if 1 <= s <= STEPS:
                                transposes(n, s - 1)
                            if s >= 2:
                                values(n, s - 2)
                    pe.wait_ge(t.o_done, b * (groups * STEPS) + groups * STEPS)
                    await_loads(pe, t, f"w_out{layer}")

                    def out_transposes(i):
                        for u in range(OCH):
                            c = i * OCH + u
                            if c >= 2:
                                pe.wait_ge(oevac[c % 2], b * SETS + c // 2)
                            for q in range(min(4, groups - 4 * u)):
                                mm = nc.tensor.transpose(t.ps_t[c % 2][:, q * P:(q + 1) * P],
                                                         t.o_all[:, i, (4 * u + q) * P:(4 * u + q + 1) * P],
                                                         t.ident[:, :])
                            mm.then_inc(t.otr_done, 1)

                    def out_product(i):
                        for u in range(OCH):
                            c = i * OCH + u
                            pe.wait_ge(oevac[c % 2], b * SETS + (c // 2 + 1))
                        if i >= 2:
                            pe.wait_ge(t.scaled_done, b * NT + (i - 1))
                        for q in range(groups):
                            mm = nc.tensor.matmul(t.ps_o[i % 2][:, 0:C], t.oT[:, i % 2, q * P:(q + 1) * P],
                                                  t.w_out[layer][:, q, :], start=(q == 0), stop=(q == groups - 1))
                        mm.then_inc(t.out_done, 1)

                    out_transposes(0)
                    for i in range(NT):
                        if i + 1 < NT:
                            out_transposes(i + 1)
                        out_product(i)

            @block.vector
            def _(dve):
                def row_max(n, s):
                    w = (s % NT + 1) * P
                    dve.wait_ge(t.s_done, n * STEPS + (s + 1))
                    nc.vector.tensor_reduce(t.nmax[:, s % 4:s % 4 + 1], t.ps_s[s % 2][:, 0:w], AX, ALU.min)\
                        .then_inc(t.max_done, 1)

                def row_scale(n, s):
                    dve.wait_ge(t.exp_done, n * STEPS + (s + 1))
                    nc.vector.reciprocal(t.rinv[:, s % 4:s % 4 + 1], t.rsum[:, s % 4:s % 4 + 1]).then_inc(t.rinv_done, 1)

                def head_out(n, g, s):
                    a, i = s // NT, s % NT
                    dve.wait_ge(t.av_done, n * STEPS + (s + 1))
                    dve.wait_ge(t.rinv_done, n * STEPS + (s + 1))
                    nc.vector.tensor_scalar(t.o_all[:, i, ds(g * C + a * D, D)], t.ps_o[s % 2][:, 0:D],
                                            t.rinv[:, s % 4:s % 4 + 1], None, ALU.mult).then_inc(t.o_done, 1)

                def evacuate(n, s):
                    for c in of_step[s]:
                        if on[c] == 0:
                            copy_chunk(dve, nc.vector.tensor_copy, n, c)

                def attention_residual(b, i):
                    dve.wait_ge(t.out_done, b * NT + (i + 1))
                    src = t.ps_o[i % 2][:, 0:C]
                    if project.out_bias is not None:
                        nc.vector.tensor_tensor(t.att_out[:, :], src, project.out_bias(t), ALU.add)\
                            .then_inc(t.c3, 1)
                        dve.wait_ge(t.c3, b * NT + (i + 1))
                        src = t.att_out[:, :]
                    nc.vector.tensor_tensor(t.att_out[:, :], src, t.gate_rows[:, ds(b + layer * B, 1), 0:C], ALU.mult)\
                        .then_inc(t.scaled_done, 1)
                    dve.wait_ge(t.scaled_done, b * NT + (i + 1))
                    nc.vector.tensor_tensor(t.x[:, ds(b * NT + i, 1), :], t.x[:, ds(b * NT + i, 1), :],
                                            t.att_out[:, :].unsqueeze(1), ALU.add).then_inc(t.x_done, 1)
                    dve.wait_ge(t.x_done, b * NT + (i + 1))

                if layer == 0:
                    dve.wait_ge(t.x_loaded, 16)
                project.vector_start(nc, dve, t)
                with dve.Fori(0, B) as b:
                    ln_vector_normalise(nc, dve, t, b)
                    ln_vector_modulate(nc, dve, t, b, layer, CA, SA,
                                       [t.hT[:, c * CHUNK:(c + 1) * CHUNK] for c in range(NCH)])
                    with dve.Fori(0, groups) as g:
                        n = b * groups + g
                        project.vector(nc, dve, t, n, g)
                        for s in range(STEPS + 3):
                            if s < STEPS:
                                row_max(n, s)
                            if 2 <= s <= STEPS + 1:
                                row_scale(n, s - 2)
                                evacuate(n, s - 2)
                            if s >= 3:
                                head_out(n, g, s - 3)
                    for i in range(NT):
                        for u in range(OCH):
                            if (i * OCH + u) % 2 == 0:
                                copy_out_chunk(dve, nc.vector.tensor_copy, b, i, u)
                        if i >= 1:
                            attention_residual(b, i - 1)
                    attention_residual(b, NT - 1)


            @block.scalar
            def _(act):
                def exponential(n, s):
                    w = (s % NT + 1) * P
                    act.wait_ge(t.max_done, n * STEPS + (s + 1))
                    if s >= 2:
                        act.wait_ge(t.tr_done, n * NCK + (of_step[s - 2][-1] + 1))
                    nc.scalar.activation(t.pp[:, s % 2, 0:w], t.ps_s[s % 2][:, 0:w], ACT.Exp,
                                         bias=t.nmax[:, s % 4:s % 4 + 1], scale=-1.0,
                                         accum_out=t.rsum[:, s % 4:s % 4 + 1]).then_inc(t.exp_done, 1)

                def evacuate(n, s):
                    for c in of_step[s]:
                        if on[c] == 1:
                            copy_chunk(act, nc.scalar.copy, n, c)

                with act.Fori(0, B) as b:
                    with act.Fori(0, groups) as g:
                        n = b * groups + g
                        project.scalar(nc, act, t, n, g)
                        for s in range(STEPS + 2):
                            if s < STEPS:
                                exponential(n, s)
                            if s >= 2:
                                evacuate(n, s - 2)
                    for i in range(NT):
                        for u in range(OCH):
                            if (i * OCH + u) % 2 == 1:
                                copy_out_chunk(act, nc.scalar.copy, b, i, u)

            @block.gpsimd
            def _(pool):
                with pool.Fori(0, B) as b:
                    ln_pool_rstd(nc, pool, t, b)
                    project.pool(nc, pool, t, b, groups)


class PlainProjection:
    out_bias = None
    sems = ""
    k_parts = 2

    def __init__(self, head_dim, q_heads, k_heads):
        self.scale, self.D = head_dim ** -0.5, head_dim
        self.heads, self.k_heads = q_heads, k_heads
        self.w_cols = (q_heads + k_heads + 1) * C

    def vector_start(self, nc, dve, t):
        pass

    def pool(self, nc, pool, t, b, groups):
        pass

    def tensor(self, nc, pe, t, n):
        pe.wait_ge(t.w_here, n * 16 + 16)
        for a in range(self.heads):
            if a:
                pe.wait_ge(t.q_ready, n * self.heads + a)
            channel_projection(nc, t, t.ps_s[0], a).then_inc(t.q_done, 1)
            if a < self.k_heads:
                if a:
                    pe.wait_ge(t.k_ready, n * self.k_heads + a)
                channel_projection(nc, t, t.ps_s[1], self.heads + a).then_inc(t.k_done, 1)
            if a == self.heads - 1:
                token_projection(nc, t, self.heads + self.k_heads)

    def vector(self, nc, dve, t, n, g):
        for a in range(self.heads):
            dve.wait_ge(t.q_hi, n * self.heads + (a + 1))
            lo = t.qs[self.D:P, a, :]
            nc.vector.scalar_tensor_tensor(out=lo, in0=t.ps_s[0][self.D:P, :], scalar=-self.scale, in1=lo.bitcast(F32),
                                           op0=ALU.mult, op1=ALU.subtract).then_inc(t.q_ready, 1)
            if a < self.k_heads:
                dve.wait_ge(t.k_hi, n * self.k_heads + (a + 1))
                nc.vector.tensor_tensor(t.ks[:, a, 1, :], t.ps_s[1][:, :], t.ks[:, a, 0, :].bitcast(F32), ALU.subtract)\
                    .then_inc(t.k_ready, 1)
            if a == self.heads - 1:
                dve.wait_ge(t.v_done, n * NCH + 1)
                nc.vector.tensor_copy(t.vv[:, 0:4, :], t.ps_t[0][:, :].rearrange("p (j c) -> p j c", c=C)).then_inc(t.v_ready, 1)

    def scalar(self, nc, act, t, n, g):
        for a in range(self.heads):
            act.wait_ge(t.q_done, n * self.heads + (a + 1))
            nc.scalar.mul(t.qs[:, a, :], t.ps_s[0][:, :], -self.scale).then_inc(t.q_hi, 1)
            if a < self.k_heads:
                act.wait_ge(t.k_done, n * self.k_heads + (a + 1))
                nc.scalar.copy(t.ks[:, a, 0, :], t.ps_s[1][:, :]).then_inc(t.k_hi, 1)
            if a == self.heads - 1:
                act.wait_ge(t.v_done, n * NCH + 2)
                nc.scalar.copy(t.vv[:, 4:8, :], t.ps_t[1][:, :].rearrange("p (j c) -> p j c", c=C)).then_inc(t.v_ready, 1)


def channel_projection(nc, t, ps, block):
    for c in range(NCH):
        mm = nc.tensor.matmul(ps[:, c * CHUNK:(c + 1) * CHUNK], t.wbuf[:, block * C:(block + 1) * C],
                              t.hT[:, c * CHUNK:(c + 1) * CHUNK], start=True, stop=True)
    return mm


def token_projection(nc, t, block):
    for j in range(NT):
        mm = nc.tensor.matmul(t.ps_t[j // 4][:, (j % 4) * C:(j % 4 + 1) * C], t.hT[:, j * P:(j + 1) * P],
                              t.wbuf[:, block * C:(block + 1) * C], start=True, stop=True)
        if j % 4 == 3:
            mm.then_inc(t.v_done, 1)


def stage_from_dram(w_dram):
    def stage(nc, block, t, groups):
        @block.sync
        def _(sp):
            sp.sem_inc(t.v_ready, 1)
            with sp.Fori(0, B) as b:
                with sp.Fori(0, groups) as g:
                    n = b * groups + g
                    sp.wait_ge(t.v_ready, n * NCH + 1)
                    sp.dma_start(t.wbuf[:, :], w_dram[ds(g, 1), :, :].rearrange("a p n -> (a p) n"))\
                        .then_inc(t.w_here, 16)
    return stage


class LatentProjection:
    sems = " lat_q lat_k rot_done sin_q sin_k cos_q cos_k rope_q rope_k const_ready c1 c2 c3"
    k_parts, w_cols = 1, 3 * C

    def __init__(self, latent):
        self.scale, self.L = latent ** -0.5, latent
        self.heads = self.k_heads = P // latent

    def out_bias(self, t):
        return t.out_b_rows[:, :]

    def vector_start(self, nc, dve, t):
        pass

    def tensor(self, nc, pe, t, n):
        H = self.heads
        pe.wait_ge(t.w_here, n + 1)
        channel_projection(nc, t, t.ps_s[0], 0).then_inc(t.q_done, 1)
        channel_projection(nc, t, t.ps_s[1], 1).then_inc(t.k_done, 1)
        token_projection(nc, t, 2)
        for part, ready in ((0, t.lat_q), (1, t.lat_k)):
            pe.wait_ge(ready, n + 1)
            for c in range(NCH):
                mm = nc.tensor.matmul(t.ps_s[part][:, c * CHUNK:(c + 1) * CHUNK], t.rot[:, :],
                                      t.pp[:, part, c * CHUNK:(c + 1) * CHUNK], start=True, stop=True)
            mm.then_inc(t.rot_done, 1)
        for a in range(H):
            for part, rope, ready, done, w in ((0, t.rope_q, t.q_ready, t.q_done, t.wqk_rep),
                                               (1, t.rope_k, t.k_ready, t.k_done, t.sel_rep)):
                if a == 0:
                    pe.wait_ge(rope, n + 1)
                else:
                    pe.wait_ge(ready, n * H + a)
                for c in range(NCH):
                    mm = nc.tensor.matmul(t.ps_s[part][:, c * CHUNK:(c + 1) * CHUNK], w[:, a, :],
                                          t.pT[:, part, c * CHUNK:(c + 1) * CHUNK], start=True, stop=True)
                mm.then_inc(done, 1)

    def vector(self, nc, dve, t, n, g):
        H, L = self.heads, self.L
        dve.wait_ge(t.k_done, n * (H + 1) + 1)
        nc.vector.tensor_scalar(t.pp[:, 1, :], t.ps_s[1][:, :], t.lat_b[:, ds(g + 4, 1)], None, ALU.add)\
            .then_inc(t.lat_k, 1)
        for c in range(NCH):
            dve.wait_ge(t.v_done, n * NCH + (c + 1))
            row = t.v_b_rows[:, ds(g, 1), :].to_broadcast([P, 4, C])
            nc.vector.tensor_tensor(t.vv[:, 4 * c:4 * c + 4, :], t.ps_t[c][:, :].rearrange("p (j c) -> p j c", c=C),
                                    row, ALU.add).then_inc(t.v_ready, 1)
        for part, cos, sin in ((0, t.cos_q, t.sin_q), (1, t.cos_k, t.sin_k)):
            dve.wait_ge(t.rot_done, n * 2 + (part + 1))
            dve.wait_ge(cos, n + 1)
            nc.vector.tensor_tensor(t.pp[:, part, :], t.ps_s[part][:, :], t.sin[:, :], ALU.mult).then_inc(sin, 1)
        for part, sin, rope in ((0, t.sin_q, t.rope_q), (1, t.sin_k, t.rope_k)):
            dve.wait_ge(sin, n + 1)
            nc.vector.tensor_tensor(t.pT[:, part, :], t.pT[:, part, :], t.pp[:, part, :], ALU.add).then_inc(rope, 1)
        for a in range(H):
            dve.wait_ge(t.q_hi, n * H + (a + 1))
            lo = t.qs[2 * L:P, a, :]
            nc.vector.scalar_tensor_tensor(out=lo, in0=t.ps_s[0][2 * L:P, :], scalar=t.wqk_b[2 * L:P, 0:1],
                                           in1=lo.bitcast(F32), op0=ALU.add, op1=ALU.subtract).then_inc(t.q_ready, 1)
            dve.wait_ge(t.k_hi, n * H + (a + 1))
            for copy in (1, 3):
                lo = t.ks[copy * L:(copy + 1) * L, a, 0, :]
                last = nc.vector.tensor_tensor(lo, t.ps_s[1][copy * L:(copy + 1) * L, :], lo.bitcast(F32), ALU.subtract)
            last.then_inc(t.k_ready, 1)

    def scalar(self, nc, act, t, n, g):
        H = self.heads
        act.wait_ge(t.q_done, n * (H + 1) + 1)
        nc.scalar.activation(t.pp[:, 0, :], t.ps_s[0][:, :], ACT.Identity, bias=t.lat_b[:, ds(g, 1)])\
            .then_inc(t.lat_q, 1)
        for a in range(H):
            act.wait_ge(t.q_done, n * (H + 1) + (a + 2))
            nc.scalar.activation(t.qs[:, a, :], t.ps_s[0][:, :], ACT.Identity, bias=t.wqk_b[:, 0:1]).then_inc(t.q_hi, 1)
            act.wait_ge(t.k_done, n * (H + 1) + (a + 2))
            nc.scalar.copy(t.ks[:, a, 0, :], t.ps_s[1][:, :]).then_inc(t.k_hi, 1)

    def pool(self, nc, pool, t, b, groups):
        with pool.Fori(0, groups) as g:
            n = b * groups + g
            pool.wait_ge(t.v_ready, n * NCH + 1)
            nc.gpsimd.tensor_copy(t.wbuf[:, :], t.w_lat[:, ds(g, 1), :].rearrange("p a n -> p (a n)"))\
                .then_inc(t.w_here, 1)
            for part, ready, done in ((0, t.lat_q, t.cos_q), (1, t.lat_k, t.cos_k)):
                pool.wait_ge(ready, n + 1)
                nc.gpsimd.tensor_tensor(t.pT[:, part, :], t.pp[:, part, :], t.cos[:, :], ALU.mult).then_inc(done, 1)


def stage_on_chip(nc, block, t, groups):
    @block.sync
    def _(sp):
        sp.sem_inc(t.v_ready, 1)


LATENT_WEIGHTS = "ca_w ca_b bd_q bd_kv bd_o rot wqk_rep sel_rep qlb kvlb_col kvlb_rows wqk_b l2ob cprojT cpb_rows cos sin"


def compose_latent(nc, t):
    H = 4
    with nc.Block() as block:
        @block.vector
        def _(dve):
            await_loads(dve, t, LATENT_WEIGHTS)
            nc.vector.tensor_copy(t.pp[:, 0, 0:P], t.ca_b[:, 2:3].to_broadcast([P, P])).then_inc(t.c1, 1)
            nc.vector.tensor_copy(t.pp[:, 0, P:2 * P], t.l2ob[:, 0:1].to_broadcast([P, P])).then_inc(t.c1, 1)
            for w in (t.wqk_rep[:, :, :], t.wqk_b[:, :]):
                nc.vector.tensor_scalar(w, w, -LATENT_DIM ** -0.5, None, ALU.mult).then_inc(t.const_ready, 1)
            dve.wait_ge(t.c2, 1)
            for part in range(3):
                src = t.ps_s[part // 2][:, (part % 2) * CHUNK:(part % 2 + 1) * CHUNK]
                nc.vector.tensor_copy(t.w_lat[:, :, part * C:(part + 1) * C],
                                      src.rearrange("p (g c) -> p g c", c=C)).then_inc(t.const_ready, 1)
            nc.vector.tensor_scalar(t.lat_b[:, 0:4], t.ps_o[0][:, 0:4], t.qlb[:, 0:1], None, ALU.add)\
                .then_inc(t.const_ready, 1)
            nc.vector.tensor_scalar(t.lat_b[:, 4:8], t.ps_o[0][:, 4:8], t.kvlb_col[:, 0:1], None, ALU.add)\
                .then_inc(t.const_ready, 1)
            nc.vector.tensor_tensor(t.v_b_rows[:, :, :], t.ps_o[1][:, :].rearrange("p (g c) -> p g c", c=C),
                                    t.kvlb_rows[:, :].rearrange("p (g c) -> p g c", c=C), ALU.add).then_inc(t.const_ready, 1)
            nc.vector.tensor_copy(t.w_out[0][:, :, :], t.ps_t[0][:, :].rearrange("p (g c) -> p g c", c=C))\
                .then_inc(t.loads["w_out0"][0], 1)
            nc.vector.tensor_tensor(t.out_b_rows[:, :], t.ps_t[1][:, 0:C], t.cpb_rows[:, :], ALU.add)\
                .then_inc(t.const_ready, 1)

        @block.tensor
        def _(pe):
            pe.wait_ge(t.c1, 2)
            for part in range(3):
                nc.tensor.matmul(t.ps_s[part // 2][:, (part % 2) * CHUNK:(part % 2 + 1) * CHUNK], t.ca_w[:, part, :],
                                 (t.bd_q if part == 0 else t.bd_kv)[:, :], start=True, stop=True)
            for part, bd in ((0, t.bd_q), (1, t.bd_kv)):
                for g in range(H):
                    nc.tensor.matmul(t.ps_o[0][:, part * H + g:part * H + g + 1], bd[:, g * P:(g + 1) * P],
                                     t.ca_b[:, part:part + 1], start=True, stop=True)
            nc.tensor.matmul(t.ps_o[1][:, :], t.pp[:, 0, 0:P], t.bd_kv[:, :], start=True, stop=True)
            for g in range(H):
                nc.tensor.matmul(t.ps_t[0][:, g * C:(g + 1) * C], t.bd_o[:, g * P:(g + 1) * P], t.cprojT[:, :],
                                 start=True, stop=True)
            nc.tensor.matmul(t.ps_t[1][:, 0:C], t.pp[:, 0, P:2 * P], t.cprojT[:, :],
                             start=True, stop=True).then_inc(t.c2, 1)


def experts_tensor(nc, pe, t, b, w1, w2, hT, nf, units, extra=None):
    per_b = len(units)

    def hidden(u):
        c, e = units[u]
        for f in range(nf):
            i = u * nf + f
            if i >= 4:
                pe.wait_ge(t.act_done, b * (per_b * nf) + (i - 3))
            nc.tensor.matmul(t.ps_h[i % 4], w1(e, f), hT(c), start=True, stop=True).then_inc(t.h_done, 1)

    def product(u):
        c, e = units[u]
        pe.wait_ge(t.act_done, b * (per_b * nf) + (u + 1) * nf)
        if u >= 2:
            pe.wait_ge(t.acc_done, (b * per_b + (u - 1)) * 4)
        for j in range(4):
            more = extra is not None and e == 0
            for f in range(nf):
                mm = nc.tensor.matmul(t.ps_y[u % 2][:, j * C:(j + 1) * C], t.hid[:, u % 2, f, j * P:(j + 1) * P],
                                      w2(e, f), start=(f == 0), stop=(f == nf - 1 and not more))
            if more:
                mm = extra(c, j, t.ps_y[u % 2][:, j * C:(j + 1) * C])
        mm.then_inc(t.y_done, 1)

    hidden(0)
    for u in range(per_b):
        if u + 1 < per_b:
            hidden(u + 1)
        product(u)


def experts_scalar(nc, act, t, b, nf, units, func, bias):
    per_b = len(units)
    for u, (c, e) in enumerate(units):
        if u >= 2:
            act.wait_ge(t.y_done, b * per_b + (u - 1))
        for f in range(nf):
            i = u * nf + f
            act.wait_ge(t.h_done, b * (per_b * nf) + (i + 1))
            nc.scalar.activation(t.hid[:, u % 2, f, :], t.ps_h[i % 4], func, bias=bias(e, f)).then_inc(t.act_done, 1)


def experts_vector(nc, dve, t, b, units, weight, layer, ne):
    per_b = len(units)
    for u, (c, e) in enumerate(units):
        first, last = e == units[0][1], (u + 1 == per_b or units[u + 1][0] != c)
        dve.wait_ge(t.y_done, b * per_b + (u + 1))
        for j in range(4):
            src = t.ps_y[u % 2][:, j * C:(j + 1) * C]
            w = weight(b, c, j, e)
            if first:
                if w is None:
                    op = nc.vector.tensor_copy(t.acc[:, j, :], src)
                else:
                    op = nc.vector.tensor_scalar(t.acc[:, j, :], src, w, None, ALU.mult)
            else:
                dve.wait_ge(t.acc_done, (b * per_b + (u - 1)) * 4 + (j + 1))
                op = nc.vector.scalar_tensor_tensor(out=t.acc[:, j, :], in0=src, scalar=w, in1=t.acc[:, j, :],
                                                    op0=ALU.mult, op1=ALU.add)
            op.then_inc(t.acc_done, 1)
        if last:
            dve.wait_ge(t.acc_done, (b * per_b + (u + 1)) * 4)
            ffn_residual(nc, dve, t, b, c, layer)


def ffn_residual(nc, dve, t, b, c, layer):
    k = b * NCH + (c + 1)
    nc.vector.tensor_tensor(t.acc[:, :, :], t.acc[:, :, :],
                            t.gate_rows[:, ds(b + layer * B, 1), C:2 * C].to_broadcast([P, 4, C]), ALU.mult)\
        .then_inc(t.gated_done, 1)
    dve.wait_ge(t.gated_done, k)
    xs = t.x[:, ds(b * NT + 4 * c, 4), :]
    nc.vector.tensor_tensor(xs, xs, t.acc[:, :, :], ALU.add).then_inc(t.x_done, 1)
    dve.wait_ge(t.x_done, k)


FFN_SEMS = LN_SEMS + " h_done act_done y_done acc_done gated_done x_done"


def open_ffn(nc, ctx, t, layer, nf):
    tag = f"_F{layer}"
    open_ln(nc, ctx, t, tag)
    open_sb(nc, ctx, t, **{"hid" + tag: ([P, 2, nf, CHUNK], F32), "acc" + tag: ([P, 4, C], F32)})
    t["hid"], t["acc"] = t["hid" + tag], t["acc" + tag]
    t["ps_h"] = [t.ps_s[i // 2][:, (i % 2) * CHUNK:(i % 2 + 1) * CHUNK] for i in range(4)]
    t["ps_y"] = t.ps_o


def moe_top2(nc, t):
    F, NF = 256, 2
    units = [(c, e) for c in range(NCH) for e in range(EXPERTS)]
    E8 = EXPERTS
    with ExitStack() as ctx:
        open_ffn(nc, ctx, t, 0, NF)
        open_sb(nc, ctx, t, f0_hT=([P, T], F32), lg=([P, NT, E8], F32), top=([P, NT, E8], F32),
                topi=([P, NT, E8], U32), topf=([P, NT, 2], F32), gap=([P, NT], F32), eg=([P, NT], F32),
                den=([P, NT], F32), pw=([P, NT, 2], F32), hot=([P, 2, NT, E8], F32), gw=([P, NT, E8], F32))
        open_sems(nc, ctx, t, "moe0_", FFN_SEMS + " lg_ps lg_done top_done idx_done step exp_done gw_done")
        with nc.Block() as block:
            @block.tensor
            def _(pe):
                await_loads(pe, t, "f0_w1 f0_w2 router")
                with pe.Fori(0, B) as b:
                    ln_tensor_transpose(nc, pe, t, b)
                    pe.wait_ge(t.hT_ready, b * NCH + NCH)
                    for j in range(NT):
                        mm = nc.tensor.matmul(t.ps_o[0][:, j * E8:(j + 1) * E8], t.f0_hT[:, j * P:(j + 1) * P],
                                              t.router[:, :], start=True, stop=True)
                    mm.then_inc(t.lg_ps, 1)
                    pe.wait_ge(t.lg_done, b + 1)
                    experts_tensor(nc, pe, t, b, lambda e, f: t.f0_w1[:, e, f * P:(f + 1) * P],
                                   lambda e, f: t.f0_w2[:, e, f, :],
                                   lambda c: t.f0_hT[:, c * CHUNK:(c + 1) * CHUNK], NF, units)

            @block.vector
            def _(dve):
                STEP = 8
                await_loads(dve, t, "iota8")
                with dve.Fori(0, B) as b:
                    ln_vector_normalise(nc, dve, t, b)
                    ln_vector_modulate(nc, dve, t, b, 0, CB, SB,
                                       [t.f0_hT[:, c * CHUNK:(c + 1) * CHUNK] for c in range(NCH)])
                    dve.wait_ge(t.lg_ps, b + 1)
                    nc.vector.tensor_copy(t.lg[:, :, :], t.ps_o[0][:, 0:NT * E8].rearrange("p (j e) -> p j e", e=E8))\
                        .then_inc(t.lg_done, 1)
                    wait_apart(dve, t.lg_done, b + 1)
                    for j in range(NT):
                        nc.vector.max(t.top[:, j, :], t.lg[:, j, :]).then_inc(t.top_done, 1)
                    wait_apart(dve, t.top_done, b * NT + NT)
                    for j in range(NT):
                        nc.vector.max_index(t.topi[:, j, :], t.top[:, j, :], t.lg[:, j, :]).then_inc(t.idx_done, 1)
                    nc.vector.tensor_tensor(t.gap[:, :], t.top[:, :, 1], t.top[:, :, 0], ALU.subtract).then_inc(t.step, 1)
                    dve.wait_ge(t.idx_done, b * NT + NT)
                    nc.vector.tensor_copy(t.topf[:, :, :], t.topi[:, :, 0:2]).then_inc(t.step, 1)
                    dve.wait_ge(t.exp_done, b + 1)
                    nc.vector.tensor_scalar(t.den[:, :], t.eg[:, :], 1.0, None, ALU.add).then_inc(t.step, 1)
                    dve.wait_ge(t.step, b * STEP + 3)
                    nc.vector.reciprocal(t.pw[:, :, 0], t.den[:, :]).then_inc(t.step, 1)
                    dve.wait_ge(t.step, b * STEP + 4)
                    nc.vector.tensor_tensor(t.pw[:, :, 1], t.pw[:, :, 0], t.eg[:, :], ALU.mult).then_inc(t.step, 1)
                    for k in range(2):
                        nc.vector.tensor_tensor(t.hot[:, k, :, :], bc_tiles(t.iota8[:, :], NT),
                                                bc_last(t.topf[:, :, k], E8), ALU.is_equal).then_inc(t.step, 1)
                    dve.wait_ge(t.step, b * STEP + 7)
                    for k in range(2):
                        nc.vector.tensor_tensor(t.hot[:, k, :, :], t.hot[:, k, :, :], bc_last(t.pw[:, :, k], E8),
                                                ALU.mult).then_inc(t.gw_done, 1)
                    dve.wait_ge(t.gw_done, b * 2 + 2)
                    nc.vector.tensor_tensor(t.gw[:, :, :], t.hot[:, 0, :, :], t.hot[:, 1, :, :], ALU.add)\
                        .then_inc(t.step, 1)
                    dve.wait_ge(t.step, b * STEP + STEP)
                    experts_vector(nc, dve, t, b, units, lambda b, c, j, e: t.gw[:, 4 * c + j, e:e + 1], 0, E8)

            @block.scalar
            def _(act):
                with act.Fori(0, B) as b:
                    act.wait_ge(t.step, b * STEP0 + 1)
                    nc.scalar.activation(t.eg[:, :], t.gap[:, :], ACT.Exp).then_inc(t.exp_done, 1)
                    experts_scalar(nc, act, t, b, NF, units, ACT.Gelu, lambda e, f: 0.0)

            @block.gpsimd
            def _(pool):
                with pool.Fori(0, B) as b:
                    ln_pool_rstd(nc, pool, t, b)


STEP0 = 8


def gated_scan(nc, t):
    H = 64
    with ExitStack() as ctx:
        open_ln(nc, ctx, t, "_S")
        open_sb(nc, ctx, t, s_sq=([P, NT, C], F32), s_ms=([P, NT], F32), s_me=([P, NT], F32), s_rr=([P, NT], F32),
                s_xn=([P, NT, C], F32), s_xnT=([P, T], F32), s_xb=([P, 2 + T], F32), s_cv=([P, T], F32),
                s_xc=([P, T], F32), s_sz=([P, T], F32), s_v=([H, T], F32), s_a=([H, T], F32), s_e=([H, T], F32),
                s_l=([H, T], F32), s_dl=([H, T], F32), s_bb=([H, T], F32), s_cum=([H, 1 + T], F32),
                s_e1=([H, T], F32), s_e2=([H, T], F32), s_ones=([H, T], F32), s_g=([P, T], F32),
                s_out=([P, NT, C], F32), s_negA=([H, 4], F32), s_yb=([P, 1], F32))
        open_sems(nc, ctx, t, "scan_", LN_SEMS + " v p mm sc a0 a1 const_done")
        VN, SN, MN = 24, 6, 6
        with nc.Block() as block:
            @block.scalar
            def _(act):
                act.wait_ge(t.a0, 1)
                nc.scalar.activation(t.s_negA[:, 1:2], t.s_negA[:, 0:1], ACT.Exp).then_inc(t.a1, 1)
                act.wait_ge(t.a1, 1)
                nc.scalar.activation(t.s_negA[:, 2:3], t.s_negA[:, 1:2], ACT.Ln, bias=1.0).then_inc(t.a1, 1)
                with act.Fori(0, B) as b:
                    s0 = b * SN
                    act.wait_ge(t.mm, b * MN + 2)
                    nc.scalar.activation(t.s_sz[:, :], t.ps_s[1][:, :], ACT.Silu).then_inc(t.sc, 1)
                    act.wait_ge(t.v, b * VN + 9)
                    nc.scalar.activation(t.s_xc[:, :], t.s_cv[:, :], ACT.Silu, bias=t.conv_b[:, 0:1]).then_inc(t.sc, 1)
                    act.wait_ge(t.v, b * VN + 11)
                    nc.scalar.activation(t.s_e[:, :], t.s_a[:, :], ACT.Exp).then_inc(t.sc, 1)
                    act.wait_ge(t.sc, s0 + 3)
                    nc.scalar.activation(t.s_l[:, :], t.s_e[:, :], ACT.Ln, bias=1.0).then_inc(t.sc, 1)
                    act.wait_ge(t.v, b * VN + 17)
                    nc.scalar.activation(t.s_e1[:, :], t.s_cum[:, 1:1 + T], ACT.Exp).then_inc(t.sc, 1)
                    nc.scalar.activation(t.s_e2[:, :], t.s_cum[:, 0:T], ACT.Exp, scale=-1.0).then_inc(t.sc, 1)

            @block.gpsimd
            def _(pool):
                with pool.Fori(0, B) as b:
                    ln_pool_rstd(nc, pool, t, b)
                    wait_apart(pool, t.v, b * VN + 4)
                    nc.gpsimd.tensor_scalar(t.s_me[:, :], t.s_ms[:, :], 1.0 / C, RMS_EPS, ALU.mult, ALU.add).then_inc(t.p, 1)
                    pool.wait_ge(t.p, b * 2 + 1)
                    nc.gpsimd.tensor_tensor(t.s_rr[:, :], t.s_me[:, :], t.minus_half[:, 0:NT], ALU.pow).then_inc(t.p, 1)

            @block.tensor
            def _(pe):
                await_loads(pe, t, "W1T W2T WlT BwT CwT DwT dwT")

                def pair(out, w, src, start, stop):
                    for c in range(NCH):
                        mm = nc.tensor.matmul(out(c), w, src(c), start=start, stop=stop)
                    return mm

                def cols(a):
                    return lambda c: a[:, c * CHUNK:(c + 1) * CHUNK]
                with pe.Fori(0, B) as b:
                    pe.wait_ge(t.v, b * VN + 5)
                    for j in range(NT):
                        mm = nc.tensor.transpose(t.ps_t[j // 4][:, (j % 4) * P:(j % 4 + 1) * P], t.s_xn[:, j, :], t.ident[:, :])
                    mm.then_inc(t.ln_tr, 1)
                    pe.wait_ge(t.v, b * VN + 6)
                    pair(cols(t.ps_s[0]), t.W1T[:, :], cols(t.s_xnT), True, True).then_inc(t.mm, 1)
                    pair(cols(t.ps_s[1]), t.W2T[:, :], cols(t.s_xnT), True, True).then_inc(t.mm, 1)
                    pe.wait_ge(t.sc, b * SN + 2)
                    pair(lambda c: t.ps_s[0][0:H, c * CHUNK:(c + 1) * CHUNK], t.dwT[:, :], cols(t.s_xc), True, True)\
                        .then_inc(t.mm, 1)
                    pair(lambda c: t.ps_s[1][0:H, c * CHUNK:(c + 1) * CHUNK], t.BwT[:, :], cols(t.s_xc), True, True)\
                        .then_inc(t.mm, 1)
                    pe.wait_ge(t.v, b * VN + 20)
                    for c in range(NCH):
                        nc.tensor.matmul(t.ps_s[0][:, c * CHUNK:(c + 1) * CHUNK], t.DwT[:, :],
                                         t.s_xc[:, c * CHUNK:(c + 1) * CHUNK], start=True, stop=False)
                        mm = nc.tensor.matmul(t.ps_s[0][:, c * CHUNK:(c + 1) * CHUNK], t.CwT[:, :],
                                              t.s_bb[:, c * CHUNK:(c + 1) * CHUNK], start=False, stop=True)
                    mm.then_inc(t.mm, 1)
                    pe.wait_ge(t.v, b * VN + 21)
                    for j in range(NT):
                        mm = nc.tensor.matmul(t.ps_s[1][:, j * C:(j + 1) * C], t.s_g[:, j * P:(j + 1) * P], t.WlT[:, :],
                                              start=True, stop=True)
                    mm.then_inc(t.mm, 1)

            @block.vector
            def _(dve):
                await_loads(dve, t, "conv_w conv_b norm_w Avec Bb Cb Db db")
                nc.vector.memset(t.s_ones[:, :], 1.0).then_inc(t.const_done, 1)
                nc.vector.memset(t.s_xb[:, 0:2], 0.0).then_inc(t.const_done, 1)
                nc.vector.memset(t.s_cum[:, 0:1], 0.0).then_inc(t.const_done, 1)
                nc.vector.tensor_tensor(t.s_yb[:, :], t.Cb[:, :], t.Db[:, :], ALU.add).then_inc(t.const_done, 1)
                nc.vector.scalar_tensor_tensor(out=t.s_negA[:, 0:1], in0=t.Avec[:, :], scalar=-1.0, in1=t.Avec[:, :],
                                               op0=ALU.mult, op1=ALU.min).then_inc(t.a0, 1)
                dve.wait_ge(t.a1, 2)
                nc.vector.scalar_tensor_tensor(out=t.s_negA[:, 3:4], in0=t.Avec[:, :], scalar=0.0, in1=t.s_negA[:, 2:3],
                                               op0=ALU.max, op1=ALU.add).then_inc(t.const_done, 1)
                dve.wait_ge(t.const_done, 5)
                nc.vector.tensor_scalar(t.s_negA[:, 0:1], t.s_negA[:, 3:4], -1.0, None, ALU.mult).then_inc(t.const_done, 1)
                dve.wait_ge(t.const_done, 6)
                with dve.Fori(0, B) as b:
                    v0 = b * VN
                    step = [0]

                    def does(ins, wait=True):
                        step[0] += 1
                        ins.then_inc(t.v, 1)
                        if wait:
                            dve.wait_ge(t.v, v0 + step[0])
                    ln_vector_normalise(nc, dve, t, b)
                    dve.wait_ge(t.ln_xn, b * NT + NT)
                    does(nc.vector.tensor_tensor(t.xn[:, :, :], t.xn[:, :, :],
                                                 t.ca_rows[:, ds(b, 1), :].to_broadcast([P, NT, C]), ALU.mult))
                    does(nc.vector.tensor_tensor(t.xn[:, :, :], t.xn[:, :, :],
                                                 t.sa_rows[:, ds(b, 1), :].to_broadcast([P, NT, C]), ALU.add))
                    does(nc.vector.tensor_tensor(t.s_sq[:, :, :], t.xn[:, :, :], t.xn[:, :, :], ALU.mult))
                    does(nc.vector.tensor_reduce(t.s_ms[:, :], t.s_sq[:, :, :], AX, ALU.add))
                    dve.wait_ge(t.p, b * 2 + 2)
                    does(nc.vector.tensor_tensor(t.s_xn[:, :, :], t.xn[:, :, :], bc_last(t.s_rr[:, :], C), ALU.mult))
                    assert step[0] == 5
                    dve.wait_ge(t.ln_tr, b + 1)
                    nc.vector.tensor_scalar(t.s_xnT[:, 0:CHUNK], t.ps_t[0][:, :], t.norm_w[:, 0:1], None, ALU.mult)\
                        .then_inc(t.hT_ready, 1)
                    dve.wait_ge(t.hT_ready, b + 1)
                    does(nc.vector.tensor_scalar(t.s_xnT[:, CHUNK:T], t.ps_t[1][:, :], t.norm_w[:, 0:1], None, ALU.mult))
                    assert step[0] == 6
                    dve.wait_ge(t.mm, b * MN + 1)
                    does(nc.vector.tensor_copy(t.s_xb[:, 2:2 + T], t.ps_s[0][:, :]))
                    does(nc.vector.tensor_scalar(t.s_cv[:, :], t.s_xb[:, 2:2 + T], t.conv_w[:, 2:3], None, ALU.mult))
                    tap = nc.vector.scalar_tensor_tensor(out=t.s_g[:, :], in0=t.s_xb[:, 1:1 + T], scalar=t.conv_w[:, 1:2],
                                                         in1=t.s_cv[:, :], op0=ALU.mult, op1=ALU.add)
                    tap.then_inc(t.a0, 1)
                    dve.wait_ge(t.a0, b + 2)
                    does(nc.vector.scalar_tensor_tensor(out=t.s_cv[:, :], in0=t.s_xb[:, 0:T], scalar=t.conv_w[:, 0:1],
                                                        in1=t.s_g[:, :], op0=ALU.mult, op1=ALU.add))
                    assert step[0] == 9
                    dve.wait_ge(t.mm, b * MN + 3)
                    does(nc.vector.tensor_scalar(t.s_v[:, :], t.ps_s[0][0:H, :], t.db[:, 0:1], None, ALU.add))
                    does(nc.vector.scalar_tensor_tensor(out=t.s_a[:, :], in0=t.s_v[:, :], scalar=-1.0, in1=t.s_v[:, :],
                                                        op0=ALU.mult, op1=ALU.min))
                    assert step[0] == 11
                    dve.wait_ge(t.sc, b * SN + 4)
                    does(nc.vector.scalar_tensor_tensor(out=t.s_dl[:, :], in0=t.s_v[:, :], scalar=0.0, in1=t.s_l[:, :],
                                                        op0=ALU.max, op1=ALU.add))
                    does(nc.vector.tensor_scalar(t.s_a[:, :], t.s_dl[:, :], t.s_negA[:, 0:1], None, ALU.mult))
                    dve.wait_ge(t.mm, b * MN + 4)
                    does(nc.vector.scalar_tensor_tensor(out=t.s_v[:, :], in0=t.ps_s[1][0:H, :], scalar=t.Bb[:, 0:1],
                                                        in1=t.s_dl[:, :], op0=ALU.add, op1=ALU.mult))
                    does(nc.vector.tensor_tensor_scan(t.s_cum[:, 1:1 + T], t.s_ones[:, :], t.s_a[:, :], 0.0, ALU.mult, ALU.add))
                    does(nc.vector.tensor_scalar(t.s_cum[:, 1:1 + T], t.s_cum[:, 1:1 + T], -20.0, 20.0, ALU.max, ALU.min))
                    does(nc.vector.memset(t.s_cum[:, 0:1], 0.0))
                    assert step[0] == 17
                    dve.wait_ge(t.sc, b * SN + 6)
                    does(nc.vector.tensor_tensor(t.s_a[:, :], t.s_v[:, :], t.s_e2[:, :], ALU.mult))
                    does(nc.vector.tensor_tensor_scan(t.s_dl[:, :], t.s_ones[:, :], t.s_a[:, :], 0.0, ALU.mult, ALU.add))
                    does(nc.vector.tensor_tensor(t.s_bb[:, :], t.s_dl[:, :], t.s_e1[:, :], ALU.mult))
                    assert step[0] == 20
                    dve.wait_ge(t.mm, b * MN + 5)
                    does(nc.vector.scalar_tensor_tensor(out=t.s_g[:, :], in0=t.ps_s[0][:, :], scalar=t.s_yb[:, 0:1],
                                                        in1=t.s_sz[:, :], op0=ALU.add, op1=ALU.mult))
                    assert step[0] == 21
                    dve.wait_ge(t.mm, b * MN + 6)
                    does(nc.vector.tensor_tensor(t.s_out[:, :, :], t.ps_s[1][:, :].rearrange("p (j c) -> p j c", c=C),
                                                 t.xn[:, :, :], ALU.add))
                    does(nc.vector.tensor_tensor(t.s_out[:, :, :], t.s_out[:, :, :],
                                                 t.gate_rows[:, ds(b + B, 1), 0:C].to_broadcast([P, NT, C]), ALU.mult))
                    xs = t.x[:, ds(b * NT, NT), :]
                    does(nc.vector.tensor_tensor(xs, xs, t.s_out[:, :, :], ALU.add))
                    assert step[0] == 24


def moe_global(nc, t):
    F, NF = 512, 4
    NE = EXPERTS + 1
    units = [(c, e) for c in range(NCH) for e in range(NE)]
    E8 = EXPERTS
    BITS = 30
    with ExitStack() as ctx:
        open_ffn(nc, ctx, t, 1, NF)
        open_sb(nc, ctx, t, g_hT=([P, B * T], F32), sc=([P, NTILES, E8], F32), sc_mx=([P, NTILES], F32),
                sc_sum=([P, NTILES], F32), sc_e=([P, E8, NTILES], F32), gate=([P, NTILES, NE], F32),
                gateT=([NE, B * T], F32), thr=([P, 1], I32), cand=([P, 1], I32), inc=([P, 1], I32),
                cnt=([P, 2], F32), flag=([P, E8 * NTILES], F32), rank=([P, E8 * NTILES], F32),
                tot=([P, E8 * NTILES], F32), room=([P, 1], F32), ones256=([P, E8 * NTILES], F32))
        open_sems(nc, ctx, t, "moe1_", FFN_SEMS + " lg_ps lg_done v mm gate_tr gate_ready s_exp m1")
        with nc.Block("gates") as block:
            @block.tensor
            def _(pe):
                await_loads(pe, t, "gwT")
                with pe.Fori(0, B) as b:
                    ln_tensor_transpose(nc, pe, t, b)
                    pe.wait_ge(t.hT_ready, b * NCH + NCH)
                    for c in range(NCH):
                        for j in range(4):
                            k = c * 4 + j
                            mm = nc.tensor.matmul(t.ps_o[0][:, k * E8:(k + 1) * E8], t.hid[:, 0, c, j * P:(j + 1) * P],
                                                  t.gwT[:, :], start=True, stop=True)
                    mm.then_inc(t.lg_ps, 1)
                for i in range(BITS):
                    pe.wait_ge(t.v, 7 + 3 * i)
                    nc.tensor.matmul(t.ps_o[1][:, 0:2], t.ones[:, :], t.cnt[:, :], start=True, stop=True).then_inc(t.mm, 1)
                V = 7 + 3 * BITS
                pe.wait_ge(t.v, V + 1)
                nc.tensor.matmul(t.ps_o[1][:, 0:2], t.ones[:, :], t.cnt[:, :], start=True, stop=True)
                nc.tensor.matmul(t.ps_s[0][:, 0:E8 * NTILES], t.tri[:, :], t.flag[:, :], start=True, stop=True)
                nc.tensor.matmul(t.ps_s[1][:, 0:E8 * NTILES], t.ones[:, :], t.flag[:, :], start=True, stop=True)\
                    .then_inc(t.mm, 1)
                pe.wait_ge(t.gate_ready, 1)
                for k in range(NTILES):
                    if k % 4 == 0 and k >= 8:
                        pe.wait_ge(t.m1, k // 4 - 1)
                    mm = nc.tensor.transpose(t.ps_t[k // 4 % 2][0:NE, (k % 4) * P:(k % 4 + 1) * P], t.gate[:, k, :],
                                             t.ident[:, :])
                    if k % 4 == 3:
                        mm.then_inc(t.gate_tr, 1)

            @block.vector
            def _(dve):
                n = [0]

                def does(ins):
                    n[0] += 1
                    ins.then_inc(t.v, 1)
                    dve.wait_ge(t.v, n[0])
                with dve.Fori(0, B) as b:
                    ln_vector_normalise(nc, dve, t, b)
                    ln_vector_modulate(nc, dve, t, b, 1, CB, SB, [t.hid[:, 0, c, :] for c in range(NCH)])
                    for c in range(NCH):
                        dve.wait_ge(t.hT_ready, b * NCH + (c + 1))
                        nc.vector.tensor_copy(t.g_hT[:, ds(b * T + c * CHUNK, CHUNK)], t.hid[:, 0, c, :]).then_inc(t.h_done, 1)
                    dve.wait_ge(t.lg_ps, b + 1)
                    nc.vector.tensor_copy(t.sc[:, ds(b * NT, NT), :],
                                          t.ps_o[0][:, 0:NT * E8].rearrange("p (j e) -> p j e", e=E8)).then_inc(t.lg_done, 1)
                dve.wait_ge(t.lg_done, B)
                dve.wait_ge(t.h_done, B * NCH)
                does(nc.vector.tensor_reduce(t.sc_mx[:, :], t.sc[:, :, :], AX, ALU.max))
                does(nc.vector.tensor_tensor(t.sc[:, :, :], t.sc[:, :, :], bc_last(t.sc_mx[:, :], E8), ALU.subtract))
                dve.wait_ge(t.s_exp, 1)
                does(nc.vector.tensor_reduce(t.sc_sum[:, :], t.sc[:, :, :], AX, ALU.add))
                does(nc.vector.reciprocal(t.sc_mx[:, :], t.sc_sum[:, :]))
                does(nc.vector.tensor_tensor(t.sc_e[:, :, :].rearrange("p e n -> p n e"), t.sc[:, :, :],
                                             bc_last(t.sc_mx[:, :], E8), ALU.mult))
                does(nc.vector.memset(t.cnt[:, :], 0.0))
                flat = t.sc_e[:, :, :].rearrange("p e n -> p (e n)")
                nc.vector.memset(t.ones256[:, :], 1.0).then_inc(t.act_done, 1)
                nc.vector.memset(t.thr[:, :], 0).then_inc(t.act_done, 1)
                nc.vector.memset(t.cand[:, :], 1 << (BITS - 1)).then_inc(t.act_done, 1)
                dve.wait_ge(t.act_done, 3)
                for i in range(BITS):
                    bit = 1 << (BITS - 1 - i)
                    does(nc.vector.tensor_scalar(t.flag[:, :], flat, t.cand[:, :].bitcast(F32), None, ALU.is_ge, ALU.add,
                                                 accum_out=t.cnt[:, 0:1]))
                    assert n[0] == 7 + 3 * i
                    dve.wait_ge(t.mm, i + 1)
                    does(nc.vector.tensor_scalar(t.inc[:, :], t.ps_o[1][:, 0:1], float(TOPK_ALL), float(bit),
                                                 ALU.is_ge, ALU.mult))
                    nc.vector.scalar_tensor_tensor(out=t.cand[:, :], in0=t.inc[:, :], scalar=bit >> 1, in1=t.thr[:, :],
                                                   op0=ALU.bitwise_or, op1=ALU.bitwise_or).then_inc(t.y_done, 1)
                    dve.wait_ge(t.y_done, i + 1)
                    does(nc.vector.tensor_tensor(t.thr[:, :], t.inc[:, :], t.thr[:, :], ALU.bitwise_or))
                thr = t.thr[:, :].bitcast(F32)
                does(nc.vector.tensor_scalar(t.rank[:, :], flat, thr, None, ALU.is_gt, ALU.add, accum_out=t.cnt[:, 0:1]))
                does(nc.vector.tensor_scalar(t.flag[:, :], flat, thr, None, ALU.is_equal))
                assert n[0] == 8 + 3 * BITS
                dve.wait_ge(t.mm, BITS + 1)
                does(nc.vector.tensor_scalar(t.room[:, :], t.ps_o[1][:, 0:1], -1.0, float(TOPK_ALL), ALU.mult, ALU.add))
                does(nc.vector.tensor_copy(t.tot[:, :], t.ps_s[1][:, 0:E8 * NTILES]))
                does(nc.vector.tensor_tensor_scan(t.ones256[:, :], t.ones256[:, :], t.tot[:, :], 0.0, ALU.mult, ALU.add))
                does(nc.vector.tensor_tensor(t.tot[:, :], t.ones256[:, :], t.tot[:, :], ALU.subtract))
                does(nc.vector.tensor_tensor(t.tot[:, :], t.ps_s[0][:, 0:E8 * NTILES], t.tot[:, :], ALU.add))
                does(nc.vector.scalar_tensor_tensor(out=t.tot[:, :], in0=t.tot[:, :], scalar=t.room[:, 0:1], in1=t.flag[:, :],
                                                    op0=ALU.is_lt, op1=ALU.mult))
                does(nc.vector.tensor_tensor(t.rank[:, :], t.rank[:, :], t.tot[:, :], ALU.add))
                does(nc.vector.memset(t.gate[:, :, 0:1], 1.0))
                nc.vector.tensor_tensor(t.gate[:, :, 1:NE], t.rank[:, :].rearrange("p (e n) -> p n e", e=E8),
                                        t.sc_e[:, :, :].rearrange("p e n -> p n e"), ALU.mult).then_inc(t.gate_ready, 1)
                for k in range(NTILES // 4):
                    dve.wait_ge(t.gate_tr, k + 1)
                    nc.vector.tensor_copy(t.gateT[:, k * CHUNK:(k + 1) * CHUNK], t.ps_t[k % 2][0:NE, :]).then_inc(t.m1, 1)

            @block.scalar
            def _(act):
                act.wait_ge(t.v, 2)
                nc.scalar.activation(t.sc[:, :, :], t.sc[:, :, :], ACT.Exp).then_inc(t.s_exp, 1)

            @block.gpsimd
            def _(pool):
                with pool.Fori(0, B) as b:
                    ln_pool_rstd(nc, pool, t, b)

        open_sems(nc, ctx, t, "moe1b_", "h_done act_done y_done acc_done gated_done x_done gT_here")
        open_sb(nc, ctx, t, gT=([NE, T], F32), e_hT=([P, T], F32), gb=([P, NT, NE], F32))
        with nc.Block("experts") as block:
            @block.tensor
            def _(pe):
                await_loads(pe, t, "f1_w1 f1_w2 b2_rows")

                def biases(c, j, out):
                    return nc.tensor.matmul(out, t.gT[:, c * CHUNK + j * P:c * CHUNK + (j + 1) * P], t.b2_rows[:, :],
                                            start=False, stop=True)
                with pe.Fori(0, B) as b:
                    pe.wait_ge(t.gT_here, b + 1)
                    experts_tensor(nc, pe, t, b, lambda e, f: t.f1_w1[:, e, f * P:(f + 1) * P],
                                   lambda e, f: t.f1_w2[:, e, f, :],
                                   lambda c: t.g_hT[:, ds(b * T + c * CHUNK, CHUNK)], NF, units, biases)

            @block.vector
            def _(dve):
                with dve.Fori(0, B) as b:
                    nc.vector.tensor_copy(t.gT[:, :], t.gateT[:, ds(b * T, T)]).then_inc(t.gT_here, 1)
                    experts_vector(nc, dve, t, b, units, lambda b, c, j, e: None if e == 0 else
                                   t.gate[:, ds(b * NT + (4 * c + j), 1), e:e + 1].rearrange("p a e -> p (a e)"), 1, NE)

            @block.scalar
            def _(act):
                await_loads(act, t, "b1_cols")
                with act.Fori(0, B) as b:
                    experts_scalar(nc, act, t, b, NF, units, ACT.Gelu_apprx_tanh,
                                   lambda e, f: t.b1_cols[:, e * NF + f:e * NF + f + 1])


def spiking_mlp(nc, t):
    NF = 4
    with ExitStack() as ctx:
        open_ffn(nc, ctx, t, 2, NF)
        open_sb(nc, ctx, t, f2_hT=([P, T], F32), f2_r=([P, 2, NF, CHUNK], F32), f2_y=([P, 4, C], F32),
                f2_n=([P, 4, C], F32), f2_t=([P, 4, C], F32))
        open_sems(nc, ctx, t, "mlp2_", FFN_SEMS + " sq_done v fires")
        V = 2 + 2 * (SEQ_STEPS - 1)
        with nc.Block() as block:
            @block.tensor
            def _(pe):
                await_loads(pe, t, "f2_w1 f2_w2")
                with pe.Fori(0, B) as b:
                    ln_tensor_transpose(nc, pe, t, b)
                    pe.wait_ge(t.hT_ready, b * NCH + NCH)
                    for c in range(NCH):
                        for f in range(NF):
                            if c:
                                pe.wait_ge(t.sq_done, b * (NCH * NF) + (f + 1))
                            nc.tensor.matmul(t.ps_h[f], t.f2_w1[:, f * P:(f + 1) * P], t.f2_hT[:, c * CHUNK:(c + 1) * CHUNK],
                                             start=True, stop=True).then_inc(t.h_done, 1)
                    for c in range(NCH):
                        pe.wait_ge(t.sq_done, b * (NCH * NF) + (c + 1) * NF)
                        for j in range(4):
                            for f in range(NF):
                                mm = nc.tensor.matmul(t.ps_y[c][:, j * C:(j + 1) * C], t.hid[:, c, f, j * P:(j + 1) * P],
                                                      t.f2_w2[:, f, :], start=(f == 0), stop=(f == NF - 1))
                        mm.then_inc(t.y_done, 1)

            @block.scalar
            def _(act):
                with act.Fori(0, B) as b:
                    for i in range(NCH * NF):
                        act.wait_ge(t.h_done, b * (NCH * NF) + (i + 1))
                        nc.scalar.activation(t.f2_r[:, i // NF, i % NF, :], t.ps_h[i % 4], ACT.Relu).then_inc(t.act_done, 1)

            @block.vector
            def _(dve):
                with dve.Fori(0, B) as b:
                    ln_vector_normalise(nc, dve, t, b)
                    ln_vector_modulate(nc, dve, t, b, 2, CB, SB,
                                       [t.f2_hT[:, c * CHUNK:(c + 1) * CHUNK] for c in range(NCH)])
                    for i in range(NCH * NF):
                        dve.wait_ge(t.act_done, b * (NCH * NF) + (i + 1))
                        nc.vector.tensor_tensor(t.hid[:, i // NF, i % NF, :], t.ps_h[i % 4], t.f2_r[:, i // NF, i % NF, :],
                                                ALU.mult).then_inc(t.sq_done, 1)
                    for c in range(NCH):
                        v0 = (b * NCH + c) * V
                        dve.wait_ge(t.y_done, b * NCH + (c + 1))
                        nc.vector.tensor_copy(t.f2_y[:, :, :], t.ps_y[c][:, :].rearrange("p (j c) -> p j c", c=C)).then_inc(t.v, 1)
                        dve.wait_ge(t.v, v0 + 1)
                        nc.vector.tensor_scalar(t.f2_n[:, :, :], t.f2_y[:, :, :], -1.0, None, ALU.mult).then_inc(t.v, 1)
                        nc.vector.tensor_scalar(t.acc[:, :, :], t.f2_y[:, :, :], 1.0, None, ALU.is_gt).then_inc(t.fires, 1)
                        for s in range(1, SEQ_STEPS):
                            dve.wait_ge(t.v, v0 + 2 * s)
                            nc.vector.scalar_tensor_tensor(out=t.f2_t[:, :, :], in0=t.f2_n[:, :, :], scalar=-0.9,
                                                           in1=t.f2_y[:, :, :], op0=ALU.mult, op1=ALU.add).then_inc(t.v, 1)
                            dve.wait_ge(t.v, v0 + (2 * s + 1))
                            nc.vector.scalar_tensor_tensor(out=t.f2_n[:, :, :], in0=t.f2_n[:, :, :], scalar=-1.0,
                                                           in1=t.f2_t[:, :, :], op0=ALU.is_lt, op1=ALU.subtract).then_inc(t.v, 1)
                            dve.wait_ge(t.v, v0 + (2 * s + 2))
                            dve.wait_ge(t.fires, (b * NCH + c) * SEQ_STEPS + s)
                            nc.vector.scalar_tensor_tensor(out=t.acc[:, :, :], in0=t.f2_n[:, :, :], scalar=-1.0,
                                                           in1=t.acc[:, :, :], op0=ALU.is_lt, op1=ALU.add).then_inc(t.fires, 1)
                        dve.wait_ge(t.fires, (b * NCH + c) * SEQ_STEPS + SEQ_STEPS)
                        nc.vector.tensor_scalar(t.acc[:, :, :], t.acc[:, :, :], 1.0 / SEQ_STEPS, None, ALU.mult).then_inc(t.acc_done, 1)
                        dve.wait_ge(t.acc_done, b * NCH + (c + 1))
                        ffn_residual(nc, dve, t, b, c, 2)

            @block.gpsimd
            def _(pool):
                with pool.Fori(0, B) as b:
                    ln_pool_rstd(nc, pool, t, b)


def linear_chain(nc, t, out):
    with ExitStack() as ctx:
        open_ffn(nc, ctx, t, 3, 1)
        open_sb(nc, ctx, t, f3_hT=([P, T], F32), f3_a=([P, T], F32), f3_b=([P, T], F32))
        open_sems(nc, ctx, t, "chain3_", FFN_SEMS + " m1 m2 c1 c2 stored")
        with nc.Block() as block:
            @block.sync
            def _(sp):
                with sp.Fori(0, B) as b:
                    sp.wait_ge(t.x_done, b * NCH + NCH)
                    sp.dma_start(out.rearrange("(b n p) c -> p b n c", p=P, n=NT)[:, ds(b, 1), :, :],
                                 t.x[:, ds(b * NT, NT), :].unsqueeze(1)).then_inc(t.stored, 16)
                sp.wait_ge(t.stored, 16 * B)

            @block.tensor
            def _(pe):
                await_loads(pe, t, "f3_w f3_a1 f3_a2 f3_bias")
                with pe.Fori(0, B) as b:
                    ln_tensor_transpose(nc, pe, t, b)
                    pe.wait_ge(t.hT_ready, b * NCH + NCH)
                    for w, src, ps, done, before in ((t.f3_w, t.f3_hT, t.ps_s[0], t.m1, None),
                                                     (t.f3_a1, t.f3_a, t.ps_s[1], t.m2, t.c1)):
                        if before:
                            pe.wait_ge(before, b + 1)
                        for c in range(NCH):
                            mm = nc.tensor.matmul(ps[:, c * CHUNK:(c + 1) * CHUNK], w[:, :], src[:, c * CHUNK:(c + 1) * CHUNK],
                                                  start=True, stop=True)
                        mm.then_inc(done, 1)
                    pe.wait_ge(t.c2, b + 1)
                    for c in range(NCH):
                        for j in range(4):
                            at = c * CHUNK + j * P
                            mm = nc.tensor.matmul(t.ps_y[c][:, j * C:(j + 1) * C], t.f3_b[:, at:at + P], t.f3_a2[:, :],
                                                  start=True, stop=True)
                        mm.then_inc(t.y_done, 1)

            @block.scalar
            def _(act):
                with act.Fori(0, B) as b:
                    act.wait_ge(t.m1, b + 1)
                    nc.scalar.copy(t.f3_a[:, :], t.ps_s[0][:, :]).then_inc(t.c1, 1)
                    act.wait_ge(t.m2, b + 1)
                    nc.scalar.copy(t.f3_b[:, :], t.ps_s[1][:, :]).then_inc(t.c2, 1)
                    for c in range(NCH):
                        act.wait_ge(t.h_done, b * NCH + (c + 1))
                        nc.scalar.activation(t.hid[:, c, 0, :], t.hid[:, c, 0, :], ACT.Tanh).then_inc(t.act_done, 1)

            @block.vector
            def _(dve):
                with dve.Fori(0, B) as b:
                    ln_vector_normalise(nc, dve, t, b)
                    ln_vector_modulate(nc, dve, t, b, 3, CB, SB,
                                       [t.f3_hT[:, c * CHUNK:(c + 1) * CHUNK] for c in range(NCH)])
                    for c in range(NCH):
                        dve.wait_ge(t.y_done, b * NCH + (c + 1))
                        nc.vector.tensor_tensor(t.hid[:, c, 0, :].rearrange("p (j c) -> p j c", c=C),
                                                t.ps_y[c][:, :].rearrange("p (j c) -> p j c", c=C),
                                                bc_tiles(t.f3_bias[:, :], 4), ALU.add).then_inc(t.h_done, 1)
                    for c in range(NCH):
                        dve.wait_ge(t.act_done, b * NCH + (c + 1))
                        nc.vector.tensor_copy(t.acc[:, :, :], t.hid[:, c, 0, :].rearrange("p (j c) -> p j c", c=C)).then_inc(t.acc_done, 1)
                        dve.wait_ge(t.acc_done, b * NCH + (c + 1))
                        ffn_residual(nc, dve, t, b, c, 3)

            @block.gpsimd
            def _(pool):
                with pool.Fori(0, B) as b:
                    ln_pool_rstd(nc, pool, t, b)


ALWAYS = [
    ("router", [P, EXPERTS]), ("iota8", [P, EXPERTS]),
    ("W1T", [P, C]), ("W2T", [P, C]), ("WlT", [P, C]), ("BwT", [P, 64]), ("CwT", [64, C]), ("DwT", [P, C]),
    ("dwT", [P, 64]), ("conv_w", [P, 3]), ("conv_b", [P, 1]), ("norm_w", [P, 1]), ("Avec", [64, 1]), ("Bb", [64, 1]),
    ("Cb", [P, 1]), ("Db", [P, 1]), ("db", [64, 1]),
    ("gwT", [P, EXPERTS]), ("b1_cols", [P, 9 * 4]), ("b2_rows", [9, C]),
]
LATENT = [
    ("ca_w", [P, 3, C]), ("ca_b", [P, 3]), ("bd_q", [P, 512]), ("bd_kv", [P, 512]), ("bd_o", [P, 512]),
    ("rot", [P, P]), ("wqk_rep", [P, 4, P]), ("sel_rep", [P, 4, P]), ("qlb", [P, 1]), ("kvlb_col", [P, 1]), ("kvlb_rows", [P, 512]),
    ("wqk_b", [P, 1]), ("l2ob", [P, 1]), ("cprojT", [P, C]), ("cpb_rows", [P, C]), ("cos", [P, T]), ("sin", [P, T]),
]
EXPERTS0 = [("f0_w1", [P, EXPERTS, 256]), ("f0_w2", [P, EXPERTS, 2, C])]
EXPERTS1 = [("f1_w1", [P, 9, 512]), ("f1_w2", [P, 9, 4, C])]
LATE = [
    ("w_out2", [P, 8, C]), ("f2_w1", [P, 512]), ("f2_w2", [P, 4, C]),
    ("w_out3", [P, 8, C]), ("f3_w", [P, C]), ("f3_a1", [P, C]), ("f3_a2", [P, C]), ("f3_bias", [P, C]),
]
ROW_VECTORS = {"kvlb_rows", "cpb_rows", "f3_bias"}


def open_weights(nc, ctx, t, dram, label, group):
    loads = []
    landed = ctx.enter_context(nc.semaphore(label + "_loaded"))
    t.finished.append(landed)
    for name, shape in group:
        open_sb(nc, ctx, t, **{name: (shape, F32)})
        t.loads[name] = (landed, 16 * len(group))
        dst = t[name]
        src = dram[name]
        if name in ROW_VECTORS:
            src = src.to_broadcast([P, shape[1]])
        loads.append((name, dst[tuple(slice(None) for _ in shape)], src))
    return loads


def load_weights(nc, t, label, loads):
    with nc.Block(label + "_weights") as block:
        @block.sync
        def _(sp):
            for name, dst, src in loads:
                sp.dma_start(dst, src).then_inc(t.loads[name][0], 16)
            if DEBUG:
                await_loads(sp, t, loads[0][0])


def build(nc, dram, out, last=99, first=0):
    t = Ctx()
    t["finished"] = []
    with ExitStack() as ctx:
        APART["sem"] = ctx.enter_context(nc.semaphore("waits_apart"))
        open_sb(nc, ctx, t, x=([P, NTILES, C], F32), ident=([P, P], F32), ident16=([P, P], BF16), maskp=([P, P], BF16),
                tri=([P, P], F32), ones=([P, P], F32), minus_half=([P, NT], F32), modT=([P, LAYERS * 6 * B], F32),
                gate_rows=([P, LAYERS * B, 2 * C], F32), sa_rows=([P, B, C], F32), ca_rows=([P, B, C], F32))
        t["ps_s"] = [ctx.enter_context(nc.psum_tensor(f"ps_s{i}", [P, 2 * CHUNK], F32)) for i in range(2)]
        t["ps_t"] = [ctx.enter_context(nc.psum_tensor(f"ps_t{i}", [P, CHUNK], F32)) for i in range(2)]
        t["ps_o"] = [ctx.enter_context(nc.psum_tensor(f"ps_o{i}", [P, CHUNK], F32)) for i in range(2)]
        open_sems(nc, ctx, t, "", "x_loaded x_out")
        t["w_out"], t["loads"] = {}, {}
        loads = open_weights(nc, ctx, t, dram, "always", ALWAYS)
        with ExitStack() as early:
            loads += open_weights(nc, early, t, dram, "experts0", EXPERTS0)
            with ExitStack() as latent:
                loads = open_weights(nc, latent, t, dram, "latent", LATENT) + loads
                open_sb(nc, latent, t, w_lat=([P, 4, 3 * C], F32), w_out_lat=([P, 4, C], F32), lat_b=([P, 8], F32),
                        v_b_rows=([P, 4, C], F32), out_b_rows=([P, C], F32))
                open_sems(nc, latent, t, "", "w_out_lat_ready")
                t.w_out[0], t.loads["w_out0"] = t.w_out_lat, (t.w_out_lat_ready, 1)
                setup(nc, t, dram, loads)
                if first < 1 <= last:
                    attention(nc, t, 0, 4, 4, LatentProjection(LATENT_DIM), stage_on_chip, compose_latent)
            load_weights(nc, t, "experts1", open_weights(nc, early, t, dram, "experts1", EXPERTS1))
            if first < 2 <= last:
                moe_top2(nc, t)
            if first < 3 <= last:
                gated_scan(nc, t)
            if first < 4 <= last:
                moe_global(nc, t)
        with nc.Block("recycle") as block:
            @block.gpsimd
            def _(pool):
                for sem in t.finished:
                    pool.sem_clear(sem)
        loads = open_weights(nc, ctx, t, dram, "late", LATE)
        load_weights(nc, t, "late", loads)
        for layer in (2, 3):
            t.w_out[layer] = t[f"w_out{layer}"]
        if first < 5 <= last:
            attention(nc, t, 2, 8, 2, PlainProjection(64, 2, 2), stage_from_dram(dram["wqkv2"]))
        if first < 6 <= last:
            spiking_mlp(nc, t)
        if first < 7 <= last:
            attention(nc, t, 3, 8, 2, PlainProjection(64, 2, 1), stage_from_dram(dram["wqkv3"]))
        if first < 8 <= last:
            linear_chain(nc, t, out)
        else:
            with nc.Block() as block:
                @block.sync
                def _(sp):
                    await_loads(sp, t, " ".join(name for name, _, _ in loads))
                    sp.dma_start(out.rearrange("(n p) c -> p n c", p=P), t.x[:, :, :]).then_inc(t.x_out, 16)
                    sp.wait_ge(t.x_out, 16)


def block_diagonal(block, times):
    r, c = block.shape
    m = np.zeros((r * times, c * times), block.dtype)
    for i in range(times):
        m[i * r:(i + 1) * r, i * c:(i + 1) * c] = block
    return m


def four_times(block):
    m = np.zeros((P, 4, P), block.dtype)
    for h in range(4):
        m[h * 32:(h + 1) * 32, h, :] = np.concatenate([block] * 4, axis=1)
    return m


def twice(w):
    h = w.reshape(C, -1, 2, 1, 64)
    return np.concatenate([h, h], axis=3).transpose(1, 0, 2, 3, 4).reshape(-1, C, 2 * C)


def rotary_tables(latent):
    inv = (np.float32(1.0) / np.power(np.float32(10000.0), np.arange(0, latent, 2, dtype=np.float32) / np.float32(latent)))
    freqs = np.outer(np.arange(T, dtype=np.float32), inv.astype(np.float32)).astype(np.float32)
    cos = np.tile(np.repeat(np.cos(freqs), 2, axis=1).T, (4, 1)).astype(np.float32)
    sin = np.tile(np.repeat(np.sin(freqs), 2, axis=1).T, (4, 1)).astype(np.float32)
    rot = np.zeros((P, P), np.float32)
    for j in range(0, P, 2):
        rot[j + 1, j] = -1.0
        rot[j, j + 1] = 1.0
    return np.ascontiguousarray(cos), np.ascontiguousarray(sin), rot


def layout(i):
    i = {k: np.asarray(v) for k, v in i.items()}
    a = {}
    a["x"] = i["L0_attn_x"].reshape(B * T, C)
    a["cT"] = np.concatenate([i[f"L{l}_c"].T for l in range(LAYERS)], axis=1)
    a["wmod"] = np.stack([i[f"L{l}_wmod"] for l in range(LAYERS)])
    p = "L0_attn_"
    a["ca_w"] = i[p + "c_attn_w"].reshape(3, P, C).transpose(1, 0, 2)
    a["ca_b"] = i[p + "c_attn_b"].reshape(3, P).T
    a["bd_q"] = block_diagonal(i[p + "q2l_w"].T, 16)
    a["bd_kv"] = block_diagonal(i[p + "kv2l_w"].T, 16)
    a["bd_o"] = block_diagonal(i[p + "l2o_w"], 16)
    a["cos"], a["sin"], a["rot"] = rotary_tables(32)
    a["wqk_rep"], a["sel_rep"] = (four_times(m) for m in (i[p + "wqk_w"].T, np.eye(32, dtype=np.float32)))
    a["qlb"] = np.tile(i[p + "q2l_b"], 4)[:, None]
    a["kvlb_col"] = np.tile(i[p + "kv2l_b"], 4)[:, None]
    a["kvlb_rows"] = np.tile(i[p + "kv2l_b"], 16)[None, :]
    a["wqk_b"] = np.tile(i[p + "wqk_b"], 4)[:, None]
    a["l2ob"] = np.tile(i[p + "l2o_b"], 16)[:, None]
    a["cprojT"] = i[p + "cproj_w"].T
    a["cpb_rows"] = i[p + "cproj_b"][None, :]
    a["router"] = i["L0_ffn_router_w"].T
    a["iota8"] = np.tile(np.arange(EXPERTS, dtype=np.float32), (P, 1))
    a["f0_w1"] = i["L0_ffn_w1"].transpose(1, 0, 2)
    a["f0_w2"] = i["L0_ffn_w2"].reshape(EXPERTS, 2, P, C).transpose(2, 0, 1, 3)
    p = "L1_attn_"
    for name, key in (("W1T", "W1"), ("W2T", "W2"), ("WlT", "Wlast"), ("BwT", "Bw"), ("CwT", "Cw"), ("DwT", "Dw"), ("dwT", "dw")):
        a[name] = i[p + key].T
    a["conv_w"] = i[p + "conv_w"]
    for name, key in (("conv_b", "conv_b"), ("norm_w", "norm_w"), ("Avec", "A"), ("Bb", "Bb"), ("Cb", "Cb"), ("Db", "Db"), ("db", "db")):
        a[name] = i[p + key][:, None]
    p = "L1_ffn_"
    a["gwT"] = i[p + "gate_weight"].T
    b1 = np.concatenate([i[p + "bs1"][None], i[p + "b1"]])
    a["b1_cols"] = b1.reshape(9 * 4, P).T
    a["b2_rows"] = np.concatenate([i[p + "bs2"][None], i[p + "b2"]])
    a["f1_w1"] = np.concatenate([i[p + "Ws1"][None], i[p + "W1"]]).transpose(1, 0, 2)
    a["f1_w2"] = np.concatenate([i[p + "Ws2"][None], i[p + "W2"]]).reshape(9, 4, P, C).transpose(2, 0, 1, 3)
    q, k, v = np.split(i["L2_attn_W_qkv"], 3, axis=1)
    a["wqkv2"] = np.concatenate([twice(q), twice(k), v.reshape(C, 8, C).transpose(1, 0, 2)], axis=2)
    a["w_out2"] = i["L2_attn_W_out"].reshape(8, P, C).transpose(1, 0, 2)
    a["f2_w1"] = i["L2_ffn_W_fc"].T
    a["f2_w2"] = i["L2_ffn_W_proj"].T.reshape(4, P, C).transpose(1, 0, 2)
    kv = [np.repeat(np.concatenate([m.reshape(4, 64, C)] * 2, axis=1), 2, axis=0).transpose(0, 2, 1)
          for m in (i["L3_attn_Wk"], i["L3_attn_Wv"])]
    a["wqkv3"] = np.concatenate([twice(i["L3_attn_Wq"].T)] + kv, axis=2)
    a["w_out3"] = i["L3_attn_Wo"].T.reshape(8, P, C).transpose(1, 0, 2)
    a["f3_w"], a["f3_a1"], a["f3_a2"] = i["L3_ffn_weight"], i["L3_ffn_aux_weight1"], i["L3_ffn_aux_weight2"]
    a["f3_bias"] = i["L3_ffn_bias"][None, :]
    return {k: np.ascontiguousarray(v) for k, v in a.items()}


def program(nc, arrays, last=99, first=0):
    dram = {k: nc.dram_tensor("in_" + k, list(v.shape), F32, kind="ExternalInput").ap() for k, v in arrays.items()}
    out = nc.dram_tensor("out_x", [B * T, C], F32, kind="ExternalOutput").ap()
    build(nc, dram, out, last, first)


def kernel(**inputs):
    import concourse.bacc as bacc
    from concourse.bass_utils import run_bass_kernel_spmd
    arrays = layout(inputs)
    nc = bacc.Bacc("TRN2", target_bir_lowering=False, num_devices=1)
    program(nc, arrays)
    r = run_bass_kernel_spmd(nc, [{"in_" + k: v for k, v in arrays.items()}], core_ids=[0])
    return r.results[0]["out_x"].reshape(B, T, C)
```

```python
from contextlib import ExitStack

import numpy as np

import concourse.bass as bass
from concourse import mybir

F32, BF16, I32, U32, F32R = (mybir.dt.float32, mybir.dt.bfloat16, mybir.dt.int32, mybir.dt.uint32,
                             mybir.dt.float32r)
ALU, ACT, AX = mybir.AluOpType, mybir.ActivationFunctionType, mybir.AxisListType.X
ds = bass.ds

P = 128
B, T, C = 4, 1024, 128
NT = T // P
NTILES = B * NT
CHUNK = 512
NCH = T // CHUNK
LAYERS = 4
DEBUG = False
SA, CA, GA, SB, CB, GB = range(6)
LN_EPS = 1e-5
RMS_EPS = float(np.finfo(np.float32).eps)
EXPERTS = 8
TOPK_ALL = B * T * 2
MASKED = 1e30
LATENT_DIM = 32
SEQ_STEPS = 5


class Ctx(dict):
    def __getattr__(self, name):
        return self[name]


def open_sb(nc, ctx, t, **shapes):
    for name, (shape, dt) in shapes.items():
        t[name] = ctx.enter_context(nc.sbuf_tensor(name, shape, dt))


def open_sems(nc, ctx, t, prefix, names):
    for n in names.split():
        t[n] = ctx.enter_context(nc.semaphore(prefix + n))
        t.finished.append(t[n])


def bc_tiles(row, n):
    return row.unsqueeze(1).to_broadcast([P, n, row.shape[-1]])


def bc_last(col, n):
    return col.unsqueeze(2).to_broadcast([P, col.shape[-1], n])


def await_loads(eng, t, names):
    for sem, count in {str(t.loads[n][0]): t.loads[n] for n in names.split()}.values():
        eng.wait_ge(sem, count)


APART = {}


def wait_apart(eng, sem, value):
    eng.wait_ge(sem, value)
    eng.sem_inc(APART["sem"], 1)


LN_SEMS = "ln_stats ln_aggr ln_eps ln_rstd ln_xn ln_tr hT_ready"


def open_ln(nc, ctx, t, tag):
    open_sb(nc, ctx, t, **{
        "ln_st" + tag: ([P, NT, 6], F32), "ln_mv" + tag: ([P, NT, 2], F32), "ln_ve" + tag: ([P, NT], F32),
        "ln_rs" + tag: ([P, NT], F32), "xn" + tag: ([P, NT, C], F32)})
    for n in ("ln_st", "ln_mv", "ln_ve", "ln_rs", "xn"):
        t[n] = t[n + tag]


def ln_vector_normalise(nc, dve, t, b):
    ln_vector_stats(nc, t, b)
    ln_vector_aggregate(nc, dve, t, b)
    ln_vector_scale(nc, dve, t, b)


def ln_vector_stats(nc, t, b):
    for j in range(NT):
        nc.vector.bn_stats(t.ln_st[:, j, :], t.x[:, ds(b * NT + j, 1), :]).then_inc(t.ln_stats, 1)


def ln_vector_aggregate(nc, dve, t, b):
    wait_apart(dve, t.ln_stats, b * NT + NT)
    for j in range(NT):
        nc.vector.bn_aggr(t.ln_mv[:, j, :], t.ln_st[:, j, :]).then_inc(t.ln_aggr, 1)


def ln_vector_scale(nc, dve, t, b):
    dve.wait_ge(t.ln_rstd, b + 1)
    for j in range(NT):
        nc.vector.tensor_scalar(t.xn[:, j, :], t.x[:, ds(b * NT + j, 1), :], t.ln_mv[:, j, 0:1],
                                t.ln_rs[:, j:j + 1], ALU.subtract, ALU.mult).then_inc(t.ln_xn, 1)


def ln_pool_rstd(nc, pool, t, b):
    wait_apart(pool, t.ln_aggr, b * NT + NT)
    nc.gpsimd.tensor_scalar(t.ln_ve[:, :], t.ln_mv[:, :, 1], LN_EPS, None, ALU.add).then_inc(t.ln_eps, 1)
    pool.wait_ge(t.ln_eps, b + 1)
    nc.gpsimd.tensor_tensor(t.ln_rs[:, :], t.ln_ve[:, :], t.minus_half[:, 0:NT], ALU.pow).then_inc(t.ln_rstd, 1)


def ln_tensor_transpose(nc, pe, t, b):
    for j in range(NT):
        if j % 4 == 0:
            pe.wait_ge(t.ln_xn, b * NT + (j + 4))
        mm = nc.tensor.transpose(t.ps_t[j // 4][:, (j % 4) * P:(j % 4 + 1) * P], t.xn[:, j, :], t.ident[:, :])
        if j % 4 == 3:
            mm.then_inc(t.ln_tr, 1)


def ln_vector_modulate(nc, dve, t, b, layer, scale, shift, hT):
    for c in range(NCH):
        dve.wait_ge(t.ln_tr, b * NCH + (c + 1))
        nc.vector.tensor_scalar(hT[c], t.ps_t[c][:, :], t.modT[:, ds(b + (layer * 6 + scale) * B, 1)],
                                t.modT[:, ds(b + (layer * 6 + shift) * B, 1)], ALU.mult, ALU.add)\
            .then_inc(t.hT_ready, 1)


def setup(nc, t, dram, weights):
    with ExitStack() as ctx:
        open_sb(nc, ctx, t, cT=([P, LAYERS * B], F32), sil=([P, LAYERS * B], F32),
                wmod=([P, LAYERS, 6 * C], F32), sil_rep=([P, LAYERS * B, P], F32),
                g_sign=([P, 2 * C], F32), g_abs=([P, 2 * C], F32))
        open_sems(nc, ctx, t, "setup_", "c_loaded wmod_loaded sil_done rep_done const_done id_zero id_done "
                  "mod_ps rows_ps mod_done sign_done abs_done rows_done")
        with nc.Block() as block:
            @block.sync
            def _(sp):
                sp.dma_start(t.cT[:, :], dram["cT"]).then_inc(t.c_loaded, 16)
                sp.dma_start(t.wmod[:, :, :], dram["wmod"].rearrange("l p n -> p l n")).then_inc(t.wmod_loaded, 16)
                sp.dma_start(t.x[:, :, :], dram["x"].rearrange("(n p) c -> p n c", p=P)).then_inc(t.x_loaded, 16)
                for name, dst, src in weights:
                    sp.dma_start(dst, src).then_inc(t.loads[name][0], 16)
                if DEBUG:
                    await_loads(sp, t, " ".join(name for name, _, _ in weights))
                    sp.wait_ge(t.x_loaded, 16)

            @block.gpsimd
            def _(pool):
                nc.gpsimd.memset(t.minus_half[:, :], -0.5).then_inc(t.id_zero, 1)
                nc.gpsimd.memset(t.ones[:, :], 1.0).then_inc(t.id_zero, 1)
                for m in (t.ident, t.ident16, t.maskp, t.tri):
                    nc.gpsimd.memset(m[:, :], 0.0).then_inc(t.id_zero, 1)
                pool.wait_ge(t.id_zero, 6)
                for m in (t.ident, t.ident16):
                    nc.gpsimd.affine_select(out=m[:, :], in_=m[:, :], compare_op=ALU.not_equal, fill=1.0, base=0,
                                            pattern=[[-1, P]], channel_multiplier=1).then_inc(t.id_done, 1)
                nc.gpsimd.affine_select(out=t.maskp[:, :], in_=t.maskp[:, :], compare_op=ALU.is_ge, fill=MASKED,
                                        base=0, pattern=[[-1, P]], channel_multiplier=1).then_inc(t.id_done, 1)
                nc.gpsimd.affine_select(out=t.tri[:, :], in_=t.tri[:, :], compare_op=ALU.is_ge, fill=1.0,
                                        base=0, pattern=[[-1, P]], channel_multiplier=1).then_inc(t.id_done, 1)

            @block.scalar
            def _(act):
                act.wait_ge(t.c_loaded, 16)
                nc.scalar.activation(t.sil[:, :], t.cT[:, :], ACT.Silu).then_inc(t.sil_done, 1)

            @block.tensor
            def _(pe):
                pe.wait_ge(t.sil_done, 1)
                pe.wait_ge(t.wmod_loaded, 16)
                for l in range(LAYERS):
                    for j in range(6):
                        at = (l * 6 + j) * B
                        mm = nc.tensor.matmul(t.ps_o[0][:, at:at + B], t.wmod[:, l, j * C:(j + 1) * C],
                                              t.sil[:, l * B:(l + 1) * B], start=True, stop=True)
                mm.then_inc(t.mod_ps, 1)
                pe.wait_ge(t.rep_done, LAYERS * B)
                for n in range(LAYERS * B):
                    l = n // B
                    if n >= 2:
                        pe.wait_ge(t.rows_done, n - 1)
                    ps = t.ps_t[n % 2]
                    for i, j in enumerate((GA, GB) + ((SA, CA) if l == 1 else ())):
                        mm = nc.tensor.matmul(ps[:, i * C:(i + 1) * C], t.sil_rep[:, n, :],
                                              t.wmod[:, l, j * C:(j + 1) * C], start=True, stop=True)
                    mm.then_inc(t.rows_ps, 1)

            @block.vector
            def _(dve):
                dve.wait_ge(t.sil_done, 1)
                for n in range(LAYERS * B):
                    nc.vector.tensor_copy(t.sil_rep[:, n, :], t.sil[:, n:n + 1].to_broadcast([P, P]))\
                        .then_inc(t.rep_done, 1)
                dve.wait_ge(t.mod_ps, 1)
                for l in range(LAYERS):
                    for j in range(6):
                        at = (l * 6 + j) * B
                        nc.vector.tensor_scalar(t.modT[:, at:at + B], t.ps_o[0][:, at:at + B],
                                                1.0 if j in (CA, CB) else 0.0, None, ALU.add).then_inc(t.mod_done, 1)
                for n in range(LAYERS * B):
                    l, b = n // B, n % B
                    ps = t.ps_t[n % 2]
                    dve.wait_ge(t.rows_ps, n + 1)
                    if n >= 1:
                        dve.wait_ge(t.rows_done, n)
                    nc.vector.tensor_scalar(t.g_sign[:, :], ps[:, 0:2 * C], 0.0, 2.0, ALU.is_ge, ALU.mult)\
                        .then_inc(t.sign_done, 1)
                    dve.wait_ge(t.sign_done, 2 * n + 1)
                    nc.vector.tensor_scalar(t.g_sign[:, :], t.g_sign[:, :], -1.0, None, ALU.add).then_inc(t.sign_done, 1)
                    dve.wait_ge(t.sign_done, 2 * n + 2)
                    nc.vector.tensor_tensor(t.g_abs[:, :], ps[:, 0:2 * C], t.g_sign[:, :], ALU.mult).then_inc(t.abs_done, 1)
                    if l == 1:
                        nc.vector.tensor_copy(t.sa_rows[:, b, :], ps[:, 2 * C:3 * C]).then_inc(t.mod_done, 1)
                        nc.vector.tensor_scalar(t.ca_rows[:, b, :], ps[:, 3 * C:4 * C], 1.0, None, ALU.add)\
                            .then_inc(t.mod_done, 1)
                    dve.wait_ge(t.abs_done, n + 1)
                    nc.vector.scalar_tensor_tensor(out=t.gate_rows[:, n, :], in0=t.g_abs[:, :], scalar=0.25,
                                                   in1=t.g_sign[:, :], op0=ALU.max, op1=ALU.mult)\
                        .then_inc(t.rows_done, 1)


def attention(nc, t, layer, groups, heads, project, w_stage, before=None):
    D = C // heads
    STEPS = heads * NT
    tag = f"_L{layer}"
    chunks = []
    of_step = []
    for s in range(STEPS):
        n = s % NT + 1
        of_step.append([])
        for k in range(0, n, 4):
            of_step[s].append(len(chunks))
            chunks.append((s, k, min(4, n - k)))
    NCK = len(chunks)
    on = [c % 2 for c in range(NCK)]
    until = [on.count(e) for e in (0, 1)]
    OCH = (groups + 3) // 4
    SETS = NT * OCH // 2

    V_COLS = max(D, 64)
    O_BANKS = 1 if project.ahead else 2
    SIDES = 2 if project.ahead else 1

    def seen(c):
        return on[:c + 1].count(on[c])

    def v_at(a):
        return a * D % V_COLS

    def over_batches(eng, start, first, group, finish):
        if not project.ahead:
            with eng.Fori(0, B) as b:
                start(b)
                with eng.Fori(0, groups) as g:
                    first(b * groups + g, g)
                    group(b * groups + g, g, 0, {}, None)
                finish(b, None)
            return

        def batch(b, next_b):
            with eng.Fori(0, groups // 2 - 1) as pair:
                for side in (0, 1):
                    group(b * groups + (pair * 2 + side), pair * 2 + side, side, project.units_at, None)
            group(b * groups + (groups - 2), groups - 2, 0, project.units_at, None)
            group(b * groups + (groups - 1), groups - 1, 1, {} if next_b is None else project.late_units_at, next_b)
            finish(b, next_b)

        start(0)
        first(0, 0)
        with eng.Fori(0, B - 1) as b:
            batch(b, b + 1)
        batch(B - 1, None)

    with ExitStack() as ctx:
        open_ln(nc, ctx, t, tag)
        open_sb(nc, ctx, t, **{
            "hT" + tag: ([P, T], F32), "wbuf" + tag: ([P, project.w_cols], F32),
            "qs" + tag: ([P, SIDES * heads, T], F32R), "ks" + tag: ([P, SIDES * project.k_heads, project.k_parts, T], F32R),
            "vv" + tag: ([P, SIDES * NT, C], F32), "pp" + tag: ([P, 2, T], F32),
            "pT" + tag: ([P, 2, T], F32), "nmax" + tag: ([P, 4], F32), "rsum" + tag: ([P, 4], F32),
            "rinv" + tag: ([P, 4], F32), "o_all" + tag: ([P, NT, groups * C], F32),
            "oT" + tag: ([P, 2, groups * C], F32), "att_out" + tag: ([P, C], F32), "table_in" + tag: ([P, 1], F32)})
        for n in ("hT", "wbuf", "qs", "ks", "vv", "pp", "pT", "nmax", "rsum", "rinv", "o_all", "oT", "att_out", "table_in"):
            t[n] = t[n + tag]
        open_sems(nc, ctx, t, f"att{layer}_", LN_SEMS + " w_here table_here "
                  "s_done max_done exp_done tr_done evac0 evac1 av_done rinv_done o_done "
                  "otr_done oevac0 oevac1 out_done scaled_done x_done" + project.sems)
        evac = (t.evac0, t.evac1)
        oevac = (t.oevac0, t.oevac1)
        if before:
            before(nc, t)
        with nc.Block() as block:
            w_stage(nc, block, t, groups)

            def copy_chunk(eng, copy, n, c):
                s, k, m = chunks[c]
                eng.wait_ge(t.tr_done, n * NCK + (c + 1))
                if s >= 2:
                    eng.wait_ge(t.av_done, n * STEPS + (s - 1))
                copy(t.pT[:, s % 2, k * P:(k + m) * P], t.ps_t[c % 2][:, 0:m * P]).then_inc(evac[on[c]], 1)

            def copy_out_chunk(eng, copy, b, i, u):
                c = i * OCH + u
                m = min(4, groups - 4 * u)
                eng.wait_ge(t.otr_done, b * NT * OCH + (c + 1))
                if i >= 2:
                    eng.wait_ge(t.out_done, b * NT + (i - 1))
                copy(t.oT[:, i % 2, u * 4 * P:(u * 4 + m) * P], t.ps_t[c % 2][:, 0:m * P]).then_inc(oevac[c % 2], 1)

            @block.tensor
            def _(pe):
                def scores(n, s, side):
                    a, i = s // NT, s % NT
                    w = (i + 1) * P
                    if s >= 2:
                        pe.wait_ge(t.exp_done, n * STEPS + (s - 1))
                    ps = t.ps_s[s % 2]
                    for k0 in range(0, w, CHUNK):
                        k1 = min(w, k0 + CHUNK)
                        for part in range(project.k_parts):
                            nc.tensor.matmul(ps[:, k0:k1], t.qs[:, side * heads + a, i * P:(i + 1) * P],
                                             t.ks[:, side * project.k_heads + a % project.k_heads, part, k0:k1], start=(part == 0),
                                             stop=(k1 < w and part == project.k_parts - 1))
                    nc.tensor.matmul(ps[:, i * P:w], t.ident16[:, :], t.maskp[:, :],
                                     start=False, stop=True).then_inc(t.s_done, 1)

                def transposes(n, s):
                    pe.wait_ge(t.exp_done, n * STEPS + (s + 1))
                    for c in of_step[s]:
                        _, k, m = chunks[c]
                        if c >= 2:
                            pe.wait_ge(evac[on[c - 2]], n * until[on[c - 2]] + seen(c - 2))
                        for q in range(m):
                            mm = nc.tensor.transpose(t.ps_t[c % 2][:, q * P:(q + 1) * P],
                                                     t.pp[:, s % 2, (k + q) * P:(k + q + 1) * P], t.ident[:, :])
                        mm.then_inc(t.tr_done, 1)

                def values(n, s, side):
                    a, i = s // NT, s % NT
                    for c in of_step[s]:
                        pe.wait_ge(evac[on[c]], n * until[on[c]] + seen(c))
                    if s >= O_BANKS:
                        pe.wait_ge(t.o_done, n * STEPS + (s - O_BANKS + 1))
                    for k in range(i + 1):
                        mm = nc.tensor.matmul(t.ps_o[s % O_BANKS][:, 0:V_COLS], t.pT[:, s % 2, k * P:(k + 1) * P],
                                              t.vv[:, side * NT + k, a * D - v_at(a):a * D - v_at(a) + V_COLS], start=(k == 0), stop=(k == i))
                    mm.then_inc(t.av_done, 1)

                def start(b):
                    ln_tensor_transpose(nc, pe, t, b)
                    wait_apart(pe, t.hT_ready, b * NCH + NCH)

                def norm_ahead(b, c):
                    if c:
                        pe.wait_ge(t.hT_ready, b * NCH + c)
                    pe.wait_ge(t.ln_xn, b * NT + 4 * (c + 1))
                    for j in range(4):
                        mm = nc.tensor.transpose(t.ps_o[1][:, j * P:(j + 1) * P], t.xn[:, 4 * c + j, :], t.ident[:, :])
                    mm.then_inc(t.ln_tr, 1)

                def group(n, g, side, units, next_b):
                    project.tensor_wait(pe, t, n)
                    scores(n, 0, side)
                    for s in range(STEPS + 1):
                        if s + 1 < STEPS:
                            scores(n, s + 1, side)
                        if s < STEPS:
                            transposes(n, s)
                        if s >= 1:
                            values(n, s - 1, side)
                        if next_b is not None and s in (3, 4):
                            norm_ahead(next_b, s - 3)
                        if s in units:
                            if next_b is not None and units[s] == 0:
                                pe.wait_ge(t.hT_ready, next_b * NCH + NCH)
                            project.tensor_ahead(nc, pe, t, n + 1, units[s])

                def finish(b, next_b):
                    if next_b is not None:
                        project.tensor_wait(pe, t, b * groups + groups)
                    pe.wait_ge(t.o_done, b * (groups * STEPS) + groups * STEPS)
                    await_loads(pe, t, f"w_out{layer}")

                    def out_transposes(i):
                        for u in range(OCH):
                            c = i * OCH + u
                            if c >= 2:
                                pe.wait_ge(oevac[c % 2], b * SETS + c // 2)
                            for q in range(min(4, groups - 4 * u)):
                                mm = nc.tensor.transpose(t.ps_t[c % 2][:, q * P:(q + 1) * P],
                                                         t.o_all[:, i, (4 * u + q) * P:(4 * u + q + 1) * P],
                                                         t.ident[:, :])
                            mm.then_inc(t.otr_done, 1)

                    def out_product(i):
                        for u in range(OCH):
                            c = i * OCH + u
                            pe.wait_ge(oevac[c % 2], b * SETS + (c // 2 + 1))
                        if i >= 2:
                            pe.wait_ge(t.scaled_done, b * NT + (i - 1))
                        for q in range(groups):
                            mm = nc.tensor.matmul(t.ps_o[i % 2][:, 0:C], t.oT[:, i % 2, q * P:(q + 1) * P],
                                                  t.w_out[layer][:, q, :], start=(q == 0), stop=(q == groups - 1))
                        mm.then_inc(t.out_done, 1)

                    out_transposes(0)
                    for i in range(NT):
                        if i + 1 < NT:
                            out_transposes(i + 1)
                        out_product(i)

                over_batches(pe, start, lambda n, g: project.tensor(nc, pe, t, n), group, finish)

            @block.vector
            def _(dve):
                def row_max(n, s):
                    w = (s % NT + 1) * P
                    dve.wait_ge(t.s_done, n * STEPS + (s + 1))
                    nc.vector.tensor_reduce(t.nmax[:, s % 4:s % 4 + 1], t.ps_s[s % 2][:, 0:w], AX, ALU.min)\
                        .then_inc(t.max_done, 1)

                def row_scale(n, s):
                    dve.wait_ge(t.exp_done, n * STEPS + (s + 1))
                    nc.vector.reciprocal(t.rinv[:, s % 4:s % 4 + 1], t.rsum[:, s % 4:s % 4 + 1]).then_inc(t.rinv_done, 1)

                def head_out(n, g, s):
                    a, i = s // NT, s % NT
                    dve.wait_ge(t.av_done, n * STEPS + (s + 1))
                    dve.wait_ge(t.rinv_done, n * STEPS + (s + 1))
                    nc.vector.tensor_scalar(t.o_all[:, i, ds(g * C + a * D, D)], t.ps_o[s % O_BANKS][:, v_at(a):v_at(a) + D],
                                            t.rinv[:, s % 4:s % 4 + 1], None, ALU.mult).then_inc(t.o_done, 1)

                def evacuate(n, s):
                    for c in of_step[s]:
                        if on[c] == 0:
                            copy_chunk(dve, nc.vector.tensor_copy, n, c)

                def attention_residual(b, i):
                    dve.wait_ge(t.out_done, b * NT + (i + 1))
                    src = t.ps_o[i % 2][:, 0:C]
                    if project.out_bias is not None:
                        nc.vector.tensor_tensor(t.att_out[:, :], src, project.out_bias(t), ALU.add)\
                            .then_inc(t.c3, 1)
                        dve.wait_ge(t.c3, b * NT + (i + 1))
                        src = t.att_out[:, :]
                    nc.vector.tensor_tensor(t.att_out[:, :], src, t.gate_rows[:, ds(b + layer * B, 1), 0:C], ALU.mult)\
                        .then_inc(t.scaled_done, 1)
                    dve.wait_ge(t.scaled_done, b * NT + (i + 1))
                    nc.vector.tensor_tensor(t.x[:, ds(b * NT + i, 1), :], t.x[:, ds(b * NT + i, 1), :],
                                            t.att_out[:, :].unsqueeze(1), ALU.add).then_inc(t.x_done, 1)
                    dve.wait_ge(t.x_done, b * NT + (i + 1))

                if layer == 0:
                    dve.wait_ge(t.x_loaded, 16)
                project.vector_start(nc, dve, t)
                def start(b):
                    ln_vector_normalise(nc, dve, t, b)
                    ln_vector_modulate(nc, dve, t, b, layer, CA, SA,
                                       [t.hT[:, c * CHUNK:(c + 1) * CHUNK] for c in range(NCH)])

                def norm_ahead(b, c):
                    dve.wait_ge(t.ln_tr, b * NCH + (c + 1))
                    nc.vector.tensor_scalar(t.hT[:, c * CHUNK:(c + 1) * CHUNK], t.ps_o[1][:, :],
                                            t.modT[:, ds(b + (layer * 6 + CA) * B, 1)],
                                            t.modT[:, ds(b + (layer * 6 + SA) * B, 1)], ALU.mult, ALU.add)\
                        .then_inc(t.hT_ready, 1)

                def group(n, g, side, units, next_b):
                    for s in range(STEPS + 2):
                        if s < STEPS:
                            row_max(n, s)
                        if 1 <= s <= STEPS:
                            row_scale(n, s - 1)
                            evacuate(n, s - 1)
                        if s >= 2:
                            head_out(n, g, s - 2)
                        if s - 1 in units:
                            project.vector_ahead(nc, dve, t, n + 1, units[s - 1], 1 - side)
                        if next_b is not None:
                            if s == 0:
                                ln_vector_stats(nc, t, next_b)
                            elif s == 1:
                                ln_vector_aggregate(nc, dve, t, next_b)
                            elif s == 3:
                                ln_vector_scale(nc, dve, t, next_b)
                            elif s in (4, 5):
                                norm_ahead(next_b, s - 4)

                def finish(b, next_b):
                    for i in range(NT):
                        for u in range(OCH):
                            if (i * OCH + u) % 2 == 0:
                                copy_out_chunk(dve, nc.vector.tensor_copy, b, i, u)
                        if i >= 1:
                            attention_residual(b, i - 1)
                    attention_residual(b, NT - 1)

                over_batches(dve, start, lambda n, g: project.vector(nc, dve, t, n, g), group, finish)

            @block.scalar
            def _(act):
                def exponential(n, s):
                    w = (s % NT + 1) * P
                    act.wait_ge(t.max_done, n * STEPS + (s + 1))
                    if s >= 2:
                        act.wait_ge(t.tr_done, n * NCK + (of_step[s - 2][-1] + 1))
                    nc.scalar.activation(t.pp[:, s % 2, 0:w], t.ps_s[s % 2][:, 0:w], ACT.Exp,
                                         bias=t.nmax[:, s % 4:s % 4 + 1], scale=-1.0,
                                         accum_out=t.rsum[:, s % 4:s % 4 + 1]).then_inc(t.exp_done, 1)

                def evacuate(n, s):
                    for c in of_step[s]:
                        if on[c] == 1:
                            copy_chunk(act, nc.scalar.copy, n, c)

                def start(b):
                    pass

                def group(n, g, side, units, next_b):
                    for s in range(STEPS + 1):
                        if s < STEPS:
                            exponential(n, s)
                        if s - 1 in units:
                            project.scalar_ahead(nc, act, t, n + 1, units[s - 1], 1 - side)
                        if s >= 1:
                            evacuate(n, s - 1)

                def finish(b, next_b):
                    for i in range(NT):
                        for u in range(OCH):
                            if (i * OCH + u) % 2 == 1:
                                copy_out_chunk(act, nc.scalar.copy, b, i, u)

                nc.scalar.activation(t.table_in[:, :], t.minus_half[:, 0:1], ACT.Exp).then_inc(t.table_here, 1)
                over_batches(act, start, lambda n, g: project.scalar(nc, act, t, n, g), group, finish)

            @block.gpsimd
            def _(pool):
                with pool.Fori(0, B) as b:
                    ln_pool_rstd(nc, pool, t, b)
                    project.pool(nc, pool, t, b, groups)


class PlainProjection:
    out_bias = None
    ahead = True
    sems = " unit_done hi_done unit_read"
    k_parts = 2

    def __init__(self, head_dim, q_heads, k_heads):
        self.scale, self.D = head_dim ** -0.5, head_dim
        self.heads, self.k_heads = q_heads, k_heads
        self.w_cols = (q_heads + k_heads + 1) * C
        kinds = [("k", a) for a in range(k_heads)] + [("q", a) for a in range(q_heads)] + [("v", 0)]
        self.units = [(kind, a, c) for kind, a in kinds for c in range(NCH)]
        self.split = [u for u, (kind, _, _) in enumerate(self.units) if kind != "v"]
        self.late_units_at = {q_heads * NT - len(self.units) + s: s for s in range(len(self.units))}
        self.units_at = {s + 1: s for s in range(len(self.units))}

    def vector_start(self, nc, dve, t):
        pass

    def pool(self, nc, pool, t, b, groups):
        pass

    def product(self, nc, t, u, ps):
        kind, a, c = self.units[u]
        if kind == "v":
            block = self.heads + self.k_heads
            for j in range(4):
                mm = nc.tensor.matmul(ps[:, j * C:(j + 1) * C], t.hT[:, c * CHUNK + j * P:c * CHUNK + (j + 1) * P],
                                      t.wbuf[:, block * C:(block + 1) * C], start=True, stop=True)
        else:
            block = a + (self.heads if kind == "k" else 0)
            mm = nc.tensor.matmul(ps, t.wbuf[:, block * C:(block + 1) * C], t.hT[:, c * CHUNK:(c + 1) * CHUNK],
                                  start=True, stop=True)
        mm.then_inc(t.unit_done, 1)

    def high(self, nc, act, t, n, u, side, ps):
        kind, a, c = self.units[u]
        if kind == "v":
            return
        cols = slice(c * CHUNK, (c + 1) * CHUNK)
        act.wait_ge(t.unit_done, n * len(self.units) + (u + 2))
        if kind == "q":
            nc.scalar.mul(t.qs[:, side * self.heads + a, cols], ps, -self.scale).then_inc(t.hi_done, 1)
        else:
            nc.scalar.copy(t.ks[:, side * self.k_heads + a, 0, cols], ps).then_inc(t.hi_done, 1)

    def low(self, nc, dve, t, n, u, side, ps):
        kind, a, c = self.units[u]
        cols = slice(c * CHUNK, (c + 1) * CHUNK)
        if kind == "v":
            dve.wait_ge(t.unit_done, n * len(self.units) + (u + 2))
            nc.vector.tensor_copy(t.vv[:, side * NT + 4 * c:side * NT + 4 * c + 4, :],
                                  ps.rearrange("p (j c) -> p j c", c=C)).then_inc(t.unit_read, 1)
            return
        dve.wait_ge(t.hi_done, n * len(self.split) + (u + 1))
        if kind == "q":
            lo = t.qs[self.D:P, side * self.heads + a, cols]
            nc.vector.scalar_tensor_tensor(out=lo, in0=ps[self.D:P, :], scalar=-self.scale, in1=lo.bitcast(F32),
                                           op0=ALU.mult, op1=ALU.subtract).then_inc(t.unit_read, 1)
        else:
            nc.vector.tensor_tensor(t.ks[:, side * self.k_heads + a, 1, cols], ps,
                                    t.ks[:, side * self.k_heads + a, 0, cols].bitcast(F32), ALU.subtract)\
                .then_inc(t.unit_read, 1)

    def bank(self, t, u):
        return t.ps_s[u // 2 % 2][:, (u % 2) * CHUNK:(u % 2 + 1) * CHUNK]

    def tensor(self, nc, pe, t, n):
        pe.wait_ge(t.w_here, n * 16 + 16)
        for u in range(len(self.units)):
            if u >= 4:
                pe.wait_ge(t.unit_read, n * len(self.units) + (u - 3))
            self.product(nc, t, u, self.bank(t, u))

    def scalar(self, nc, act, t, n, g):
        for u in range(len(self.units)):
            self.high(nc, act, t, n, u, 0, self.bank(t, u))

    def vector(self, nc, dve, t, n, g):
        for u in range(len(self.units)):
            self.low(nc, dve, t, n, u, 0, self.bank(t, u))

    def tensor_wait(self, pe, t, n):
        pe.wait_ge(t.unit_read, n * len(self.units) + len(self.units))

    def tensor_ahead(self, nc, pe, t, n, u):
        if u == 0:
            pe.wait_ge(t.w_here, n * 16 + 16)
        else:
            pe.wait_ge(t.unit_read, n * len(self.units) + u)
        self.product(nc, t, u, t.ps_o[1][:, :])

    def scalar_ahead(self, nc, act, t, n, u, side):
        self.high(nc, act, t, n, u, side, t.ps_o[1][:, :])

    def vector_ahead(self, nc, dve, t, n, u, side):
        self.low(nc, dve, t, n, u, side, t.ps_o[1][:, :])


def channel_projection(nc, t, ps, block):
    for c in range(NCH):
        mm = nc.tensor.matmul(ps[:, c * CHUNK:(c + 1) * CHUNK], t.wbuf[:, block * C:(block + 1) * C],
                              t.hT[:, c * CHUNK:(c + 1) * CHUNK], start=True, stop=True)
    return mm


def token_projection(nc, t, block):
    for j in range(NT):
        mm = nc.tensor.matmul(t.ps_t[j // 4][:, (j % 4) * C:(j % 4 + 1) * C], t.hT[:, j * P:(j + 1) * P],
                              t.wbuf[:, block * C:(block + 1) * C], start=True, stop=True)
        if j % 4 == 3:
            mm.then_inc(t.v_done, 1)


def stage_from_dram(w_dram, units):
    def stage(nc, block, t, groups):
        @block.sync
        def _(sp):
            sp.sem_inc(t.unit_done, 1)
            with sp.Fori(0, B) as b:
                with sp.Fori(0, groups) as g:
                    n = b * groups + g
                    sp.wait_ge(t.unit_done, n * units + 1)
                    sp.dma_start(t.wbuf[:, :], w_dram[ds(g, 1), :, :].rearrange("a p n -> (a p) n"))\
                        .then_inc(t.w_here, 16)
    return stage


class LatentProjection:
    ahead = False
    sems = (" v_done q_done k_done q_hi k_hi q_ready k_ready v_ready lat_q lat_k rot_done sin_q sin_k cos_q cos_k"
            " rope_q rope_k const_ready c1 c2 c3")
    k_parts, w_cols = 1, 3 * C

    def __init__(self, latent):
        self.scale, self.L = latent ** -0.5, latent
        self.heads = self.k_heads = P // latent

    def tensor_wait(self, pe, t, n):
        pe.wait_ge(t.q_ready, n * self.heads + self.heads)
        pe.wait_ge(t.k_ready, n * self.k_heads + self.k_heads)
        pe.wait_ge(t.v_ready, n * NCH + (NCH + 1))

    def out_bias(self, t):
        return t.out_b_rows[:, :]

    def vector_start(self, nc, dve, t):
        pass

    def tensor(self, nc, pe, t, n):
        H = self.heads
        pe.wait_ge(t.w_here, n + 1)
        channel_projection(nc, t, t.ps_s[0], 0).then_inc(t.q_done, 1)
        channel_projection(nc, t, t.ps_s[1], 1).then_inc(t.k_done, 1)
        token_projection(nc, t, 2)
        for part, ready in ((0, t.lat_q), (1, t.lat_k)):
            pe.wait_ge(ready, n + 1)
            for c in range(NCH):
                mm = nc.tensor.matmul(t.ps_s[part][:, c * CHUNK:(c + 1) * CHUNK], t.rot[:, :],
                                      t.pp[:, part, c * CHUNK:(c + 1) * CHUNK], start=True, stop=True)
            mm.then_inc(t.rot_done, 1)
        for a in range(H):
            for part, rope, ready, done, w in ((0, t.rope_q, t.q_ready, t.q_done, t.wqk_rep),
                                               (1, t.rope_k, t.k_ready, t.k_done, t.sel_rep)):
                if a == 0:
                    pe.wait_ge(rope, n + 1)
                elif a == 1:
                    pe.wait_ge(t.v_ready, n * NCH + (NCH + 1))
                else:
                    pe.wait_ge(ready, n * H + (a - 1))
                for c in range(NCH):
                    mm = nc.tensor.matmul(self.bank_pair(t, part, a)[:, c * CHUNK:(c + 1) * CHUNK], w[:, a, :],
                                          t.pT[:, part, c * CHUNK:(c + 1) * CHUNK], start=True, stop=True)
                mm.then_inc(done, 1)

    def bank_pair(self, t, part, a):
        return ((t.ps_s[0], t.ps_s[1]), (t.ps_tt, t.ps_oo))[a % 2][part]

    def vector(self, nc, dve, t, n, g):
        H, L = self.heads, self.L
        dve.wait_ge(t.k_done, n * (H + 1) + 1)
        nc.vector.tensor_scalar(t.pp[:, 1, :], t.ps_s[1][:, :], t.lat_b[:, ds(g + 4, 1)], None, ALU.add)\
            .then_inc(t.lat_k, 1)
        dve.wait_ge(t.lat_q, n + 1)
        nc.vector.tensor_tensor(t.pT[:, 0, :], t.pp[:, 0, :], t.cos[:, :], ALU.mult).then_inc(t.cos_q, 1)
        for c in range(NCH):
            dve.wait_ge(t.v_done, n * NCH + (c + 1))
            row = t.v_b_rows[:, ds(g, 1), :].to_broadcast([P, 4, C])
            nc.vector.tensor_tensor(t.vv[:, 4 * c:4 * c + 4, :], t.ps_t[c][:, :].rearrange("p (j c) -> p j c", c=C),
                                    row, ALU.add).then_inc(t.v_ready, 1)
        for part, cos, sin, rope in ((0, t.cos_q, t.sin_q, t.rope_q), (1, t.cos_k, t.sin_k, t.rope_k)):
            dve.wait_ge(t.rot_done, n * 2 + (part + 1))
            dve.wait_ge(cos, n + 1)
            nc.vector.tensor_tensor(t.pp[:, part, :], t.ps_s[part][:, :], t.sin[:, :], ALU.mult).then_inc(sin, 1)
            dve.wait_ge(sin, n + 1)
            nc.vector.tensor_tensor(t.pT[:, part, :], t.pT[:, part, :], t.pp[:, part, :], ALU.add).then_inc(rope, 1)
        for a in range(H):
            dve.wait_ge(t.q_hi, n * H + (a + 1))
            lo = t.qs[2 * L:P, a, :]
            nc.vector.scalar_tensor_tensor(out=lo, in0=self.bank_pair(t, 0, a)[2 * L:P, :], scalar=t.wqk_b[2 * L:P, 0:1],
                                           in1=lo.bitcast(F32), op0=ALU.add, op1=ALU.subtract).then_inc(t.q_ready, 1)
            dve.wait_ge(t.k_hi, n * H + (a + 1))
            k = t.ks[:, a, 0, :]
            nc.vector.scalar_tensor_tensor(out=k, in0=k.bitcast(F32), scalar=t.low_copies[:, 0:1],
                                           in1=self.bank_pair(t, 1, a)[:, :], op0=ALU.mult, op1=ALU.add)\
                .then_inc(t.k_ready, 1)

    def scalar(self, nc, act, t, n, g):
        H = self.heads
        act.wait_ge(t.q_done, n * (H + 1) + 1)
        nc.scalar.activation(t.pp[:, 0, :], t.ps_s[0][:, :], ACT.Identity, bias=t.lat_b[:, ds(g, 1)])\
            .then_inc(t.lat_q, 1)
        for a in range(H):
            act.wait_ge(t.q_done, n * (H + 1) + (a + 2))
            nc.scalar.activation(t.qs[:, a, :], self.bank_pair(t, 0, a)[:, :], ACT.Identity, bias=t.wqk_b[:, 0:1]).then_inc(t.q_hi, 1)
            act.wait_ge(t.k_done, n * (H + 1) + (a + 2))
            nc.scalar.copy(t.ks[:, a, 0, :], self.bank_pair(t, 1, a)[:, :]).then_inc(t.k_hi, 1)

    def pool(self, nc, pool, t, b, groups):
        with pool.Fori(0, groups) as g:
            n = b * groups + g
            pool.wait_ge(t.v_ready, n * NCH + 1)
            nc.gpsimd.tensor_copy(t.wbuf[:, :], t.w_lat[:, ds(g, 1), :].rearrange("p a n -> p (a n)"))\
                .then_inc(t.w_here, 1)
            pool.wait_ge(t.lat_k, n + 1)
            nc.gpsimd.tensor_tensor(t.pT[:, 1, :], t.pp[:, 1, :], t.cos[:, :], ALU.mult).then_inc(t.cos_k, 1)


def stage_on_chip(nc, block, t, groups):
    @block.sync
    def _(sp):
        sp.sem_inc(t.v_ready, 1)


LATENT_WEIGHTS = "ca_w ca_b bd_q bd_kv bd_o rot wqk_rep sel_rep qlb kvlb_col kvlb_rows wqk_b l2ob cprojT cpb_rows cos sin"


def compose_latent(nc, t):
    H = 4
    with nc.Block() as block:
        @block.vector
        def _(dve):
            await_loads(dve, t, LATENT_WEIGHTS)
            nc.vector.tensor_copy(t.pp[:, 0, 0:P], t.ca_b[:, 2:3].to_broadcast([P, P])).then_inc(t.c1, 1)
            nc.vector.tensor_copy(t.pp[:, 0, P:2 * P], t.l2ob[:, 0:1].to_broadcast([P, P])).then_inc(t.c1, 1)
            for copy in range(4):
                nc.vector.memset(t.low_copies[copy * LATENT_DIM:(copy + 1) * LATENT_DIM, :], -float(copy % 2))\
                    .then_inc(t.const_ready, 1)
            for w in (t.wqk_rep[:, :, :], t.wqk_b[:, :]):
                nc.vector.tensor_scalar(w, w, -LATENT_DIM ** -0.5, None, ALU.mult).then_inc(t.const_ready, 1)
            dve.wait_ge(t.c2, 1)
            for part in range(3):
                src = t.ps_s[part // 2][:, (part % 2) * CHUNK:(part % 2 + 1) * CHUNK]
                nc.vector.tensor_copy(t.w_lat[:, :, part * C:(part + 1) * C],
                                      src.rearrange("p (g c) -> p g c", c=C)).then_inc(t.const_ready, 1)
            nc.vector.tensor_scalar(t.lat_b[:, 0:4], t.ps_o[0][:, 0:4], t.qlb[:, 0:1], None, ALU.add)\
                .then_inc(t.const_ready, 1)
            nc.vector.tensor_scalar(t.lat_b[:, 4:8], t.ps_o[0][:, 4:8], t.kvlb_col[:, 0:1], None, ALU.add)\
                .then_inc(t.const_ready, 1)
            nc.vector.tensor_tensor(t.v_b_rows[:, :, :], t.ps_o[1][:, :].rearrange("p (g c) -> p g c", c=C),
                                    t.kvlb_rows[:, :].rearrange("p (g c) -> p g c", c=C), ALU.add).then_inc(t.const_ready, 1)
            nc.vector.tensor_copy(t.w_out[0][:, :, :], t.ps_t[0][:, :].rearrange("p (g c) -> p g c", c=C))\
                .then_inc(t.loads["w_out0"][0], 1)
            nc.vector.tensor_tensor(t.out_b_rows[:, :], t.ps_t[1][:, 0:C], t.cpb_rows[:, :], ALU.add)\
                .then_inc(t.const_ready, 1)

        @block.tensor
        def _(pe):
            pe.wait_ge(t.c1, 2)
            for part in range(3):
                nc.tensor.matmul(t.ps_s[part // 2][:, (part % 2) * CHUNK:(part % 2 + 1) * CHUNK], t.ca_w[:, part, :],
                                 (t.bd_q if part == 0 else t.bd_kv)[:, :], start=True, stop=True)
            for part, bd in ((0, t.bd_q), (1, t.bd_kv)):
                for g in range(H):
                    nc.tensor.matmul(t.ps_o[0][:, part * H + g:part * H + g + 1], bd[:, g * P:(g + 1) * P],
                                     t.ca_b[:, part:part + 1], start=True, stop=True)
            nc.tensor.matmul(t.ps_o[1][:, :], t.pp[:, 0, 0:P], t.bd_kv[:, :], start=True, stop=True)
            for g in range(H):
                nc.tensor.matmul(t.ps_t[0][:, g * C:(g + 1) * C], t.bd_o[:, g * P:(g + 1) * P], t.cprojT[:, :],
                                 start=True, stop=True)
            nc.tensor.matmul(t.ps_t[1][:, 0:C], t.pp[:, 0, P:2 * P], t.cprojT[:, :],
                             start=True, stop=True).then_inc(t.c2, 1)


def experts_tensor(nc, pe, t, b, w1, w2, hT, nf, units, extra=None):
    per_b = len(units)

    def hidden(u):
        c, e = units[u]
        for f in range(nf):
            i = u * nf + f
            if i >= 4:
                pe.wait_ge(t.act_done, b * (per_b * nf) + (i - 3))
            nc.tensor.matmul(t.ps_h[i % 4], w1(e, f), hT(c), start=True, stop=True).then_inc(t.h_done, 1)

    def product(u):
        c, e = units[u]
        pe.wait_ge(t.act_done, b * (per_b * nf) + (u + 1) * nf)
        if u >= 2:
            pe.wait_ge(t.acc_done, (b * per_b + (u - 1)) * 4)
        for j in range(4):
            more = extra is not None and e == 0
            for f in range(nf):
                mm = nc.tensor.matmul(t.ps_y[u % 2][:, j * C:(j + 1) * C], t.hid[:, u % 2, f, j * P:(j + 1) * P],
                                      w2(e, f), start=(f == 0), stop=(f == nf - 1 and not more))
            if more:
                mm = extra(c, j, t.ps_y[u % 2][:, j * C:(j + 1) * C])
        mm.then_inc(t.y_done, 1)

    hidden(0)
    for u in range(per_b):
        if u + 1 < per_b:
            hidden(u + 1)
        product(u)


def experts_scalar(nc, act, t, b, nf, units, func, bias):
    per_b = len(units)
    for u, (c, e) in enumerate(units):
        if u >= 2:
            act.wait_ge(t.y_done, b * per_b + (u - 1))
        for f in range(nf):
            i = u * nf + f
            act.wait_ge(t.h_done, b * (per_b * nf) + (i + 1))
            nc.scalar.activation(t.hid[:, u % 2, f, :], t.ps_h[i % 4], func, bias=bias(e, f)).then_inc(t.act_done, 1)


def experts_vector(nc, dve, t, b, units, weight, layer, ne):
    per_b = len(units)
    for u, (c, e) in enumerate(units):
        first, last = e == units[0][1], (u + 1 == per_b or units[u + 1][0] != c)
        dve.wait_ge(t.y_done, b * per_b + (u + 1))
        for j in range(4):
            src = t.ps_y[u % 2][:, j * C:(j + 1) * C]
            w = weight(b, c, j, e)
            if first:
                if w is None:
                    op = nc.vector.tensor_copy(t.acc[:, j, :], src)
                else:
                    op = nc.vector.tensor_scalar(t.acc[:, j, :], src, w, None, ALU.mult)
            else:
                dve.wait_ge(t.acc_done, (b * per_b + (u - 1)) * 4 + (j + 1))
                op = nc.vector.scalar_tensor_tensor(out=t.acc[:, j, :], in0=src, scalar=w, in1=t.acc[:, j, :],
                                                    op0=ALU.mult, op1=ALU.add)
            op.then_inc(t.acc_done, 1)
        if last:
            dve.wait_ge(t.acc_done, (b * per_b + (u + 1)) * 4)
            ffn_residual(nc, dve, t, b, c, layer)


def ffn_residual(nc, dve, t, b, c, layer):
    k = b * NCH + (c + 1)
    nc.vector.tensor_tensor(t.acc[:, :, :], t.acc[:, :, :],
                            t.gate_rows[:, ds(b + layer * B, 1), C:2 * C].to_broadcast([P, 4, C]), ALU.mult)\
        .then_inc(t.gated_done, 1)
    dve.wait_ge(t.gated_done, k)
    xs = t.x[:, ds(b * NT + 4 * c, 4), :]
    nc.vector.tensor_tensor(xs, xs, t.acc[:, :, :], ALU.add).then_inc(t.x_done, 1)
    dve.wait_ge(t.x_done, k)


FFN_SEMS = LN_SEMS + " h_done act_done y_done acc_done gated_done x_done"


def open_ffn(nc, ctx, t, layer, nf):
    tag = f"_F{layer}"
    open_ln(nc, ctx, t, tag)
    open_sb(nc, ctx, t, **{"hid" + tag: ([P, 2, nf, CHUNK], F32), "acc" + tag: ([P, 4, C], F32)})
    t["hid"], t["acc"] = t["hid" + tag], t["acc" + tag]
    t["ps_h"] = [t.ps_s[i // 2][:, (i % 2) * CHUNK:(i % 2 + 1) * CHUNK] for i in range(4)]
    t["ps_y"] = t.ps_o


def moe_top2(nc, t):
    F, NF = 256, 2
    units = [(c, e) for c in range(NCH) for e in range(EXPERTS)]
    E8 = EXPERTS
    with ExitStack() as ctx:
        open_ffn(nc, ctx, t, 0, NF)
        open_sb(nc, ctx, t, f0_hT=([P, T], F32), lg=([P, NT, E8], F32), top=([P, NT, E8], F32),
                topi=([P, NT, E8], U32), topf=([P, NT, 2], F32), gap=([P, NT], F32), eg=([P, NT], F32),
                den=([P, NT], F32), pw=([P, NT, 2], F32), hot=([P, 2, NT, E8], F32), gw=([P, NT, E8], F32))
        open_sems(nc, ctx, t, "moe0_", FFN_SEMS + " lg_ps lg_done top_done idx_done step exp_done gw_done")
        with nc.Block() as block:
            @block.tensor
            def _(pe):
                await_loads(pe, t, "f0_w1 f0_w2 router")
                with pe.Fori(0, B) as b:
                    ln_tensor_transpose(nc, pe, t, b)
                    pe.wait_ge(t.hT_ready, b * NCH + NCH)
                    for j in range(NT):
                        mm = nc.tensor.matmul(t.ps_o[0][:, j * E8:(j + 1) * E8], t.f0_hT[:, j * P:(j + 1) * P],
                                              t.router[:, :], start=True, stop=True)
                    mm.then_inc(t.lg_ps, 1)
                    pe.wait_ge(t.lg_done, b + 1)
                    experts_tensor(nc, pe, t, b, lambda e, f: t.f0_w1[:, e, f * P:(f + 1) * P],
                                   lambda e, f: t.f0_w2[:, e, f, :],
                                   lambda c: t.f0_hT[:, c * CHUNK:(c + 1) * CHUNK], NF, units)

            @block.vector
            def _(dve):
                STEP = 8
                await_loads(dve, t, "iota8")
                with dve.Fori(0, B) as b:
                    ln_vector_normalise(nc, dve, t, b)
                    ln_vector_modulate(nc, dve, t, b, 0, CB, SB,
                                       [t.f0_hT[:, c * CHUNK:(c + 1) * CHUNK] for c in range(NCH)])
                    dve.wait_ge(t.lg_ps, b + 1)
                    nc.vector.tensor_copy(t.lg[:, :, :], t.ps_o[0][:, 0:NT * E8].rearrange("p (j e) -> p j e", e=E8))\
                        .then_inc(t.lg_done, 1)
                    wait_apart(dve, t.lg_done, b + 1)
                    for j in range(NT):
                        nc.vector.max(t.top[:, j, :], t.lg[:, j, :]).then_inc(t.top_done, 1)
                    wait_apart(dve, t.top_done, b * NT + NT)
                    for j in range(NT):
                        nc.vector.max_index(t.topi[:, j, :], t.top[:, j, :], t.lg[:, j, :]).then_inc(t.idx_done, 1)
                    nc.vector.tensor_tensor(t.gap[:, :], t.top[:, :, 1], t.top[:, :, 0], ALU.subtract).then_inc(t.step, 1)
                    dve.wait_ge(t.idx_done, b * NT + NT)
                    nc.vector.tensor_copy(t.topf[:, :, :], t.topi[:, :, 0:2]).then_inc(t.step, 1)
                    dve.wait_ge(t.exp_done, b + 1)
                    nc.vector.tensor_scalar(t.den[:, :], t.eg[:, :], 1.0, None, ALU.add).then_inc(t.step, 1)
                    dve.wait_ge(t.step, b * STEP + 3)
                    nc.vector.reciprocal(t.pw[:, :, 0], t.den[:, :]).then_inc(t.step, 1)
                    dve.wait_ge(t.step, b * STEP + 4)
                    nc.vector.tensor_tensor(t.pw[:, :, 1], t.pw[:, :, 0], t.eg[:, :], ALU.mult).then_inc(t.step, 1)
                    for k in range(2):
                        nc.vector.tensor_tensor(t.hot[:, k, :, :], bc_tiles(t.iota8[:, :], NT),
                                                bc_last(t.topf[:, :, k], E8), ALU.is_equal).then_inc(t.step, 1)
                    dve.wait_ge(t.step, b * STEP + 7)
                    for k in range(2):
                        nc.vector.tensor_tensor(t.hot[:, k, :, :], t.hot[:, k, :, :], bc_last(t.pw[:, :, k], E8),
                                                ALU.mult).then_inc(t.gw_done, 1)
                    dve.wait_ge(t.gw_done, b * 2 + 2)
                    nc.vector.tensor_tensor(t.gw[:, :, :], t.hot[:, 0, :, :], t.hot[:, 1, :, :], ALU.add)\
                        .then_inc(t.step, 1)
                    dve.wait_ge(t.step, b * STEP + STEP)
                    experts_vector(nc, dve, t, b, units, lambda b, c, j, e: t.gw[:, 4 * c + j, e:e + 1], 0, E8)

            @block.scalar
            def _(act):
                with act.Fori(0, B) as b:
                    act.wait_ge(t.step, b * STEP0 + 1)
                    nc.scalar.activation(t.eg[:, :], t.gap[:, :], ACT.Exp).then_inc(t.exp_done, 1)
                    experts_scalar(nc, act, t, b, NF, units, ACT.Gelu, lambda e, f: 0.0)

            @block.gpsimd
            def _(pool):
                with pool.Fori(0, B) as b:
                    ln_pool_rstd(nc, pool, t, b)


STEP0 = 8


def gated_scan(nc, t):
    H = 64
    with ExitStack() as ctx:
        open_ln(nc, ctx, t, "_S")
        open_sb(nc, ctx, t, s_sq=([P, NT, C], F32), s_ms=([P, NT], F32), s_me=([P, NT], F32), s_rr=([P, NT], F32),
                s_xn=([P, NT, C], F32), s_xnT=([P, T], F32), s_xb=([P, 2 + T], F32), s_cv=([P, T], F32),
                s_xc=([P, T], F32), s_sz=([P, T], F32), s_v=([H, T], F32), s_a=([H, T], F32), s_e=([H, T], F32),
                s_l=([H, T], F32), s_dl=([H, T], F32), s_bb=([H, T], F32), s_cum=([H, 1 + T], F32),
                s_e1=([H, T], F32), s_e2=([H, T], F32), s_ones=([H, T], F32), s_g=([P, T], F32),
                s_out=([P, NT, C], F32), s_negA=([H, 4], F32), s_yb=([P, 1], F32))
        open_sems(nc, ctx, t, "scan_", LN_SEMS + " v p mm sc a0 a1 const_done")
        VN, SN, MN = 24, 6, 6
        with nc.Block() as block:
            @block.scalar
            def _(act):
                act.wait_ge(t.a0, 1)
                nc.scalar.activation(t.s_negA[:, 1:2], t.s_negA[:, 0:1], ACT.Exp).then_inc(t.a1, 1)
                act.wait_ge(t.a1, 1)
                nc.scalar.activation(t.s_negA[:, 2:3], t.s_negA[:, 1:2], ACT.Ln, bias=1.0).then_inc(t.a1, 1)
                with act.Fori(0, B) as b:
                    s0 = b * SN
                    act.wait_ge(t.mm, b * MN + 2)
                    nc.scalar.activation(t.s_sz[:, :], t.ps_s[1][:, :], ACT.Silu).then_inc(t.sc, 1)
                    act.wait_ge(t.v, b * VN + 9)
                    nc.scalar.activation(t.s_xc[:, :], t.s_cv[:, :], ACT.Silu, bias=t.conv_b[:, 0:1]).then_inc(t.sc, 1)
                    act.wait_ge(t.v, b * VN + 11)
                    nc.scalar.activation(t.s_e[:, :], t.s_a[:, :], ACT.Exp).then_inc(t.sc, 1)
                    act.wait_ge(t.sc, s0 + 3)
                    nc.scalar.activation(t.s_l[:, :], t.s_e[:, :], ACT.Ln, bias=1.0).then_inc(t.sc, 1)
                    act.wait_ge(t.v, b * VN + 17)
                    nc.scalar.activation(t.s_e1[:, :], t.s_cum[:, 1:1 + T], ACT.Exp).then_inc(t.sc, 1)
                    nc.scalar.activation(t.s_e2[:, :], t.s_cum[:, 0:T], ACT.Exp, scale=-1.0).then_inc(t.sc, 1)

            @block.gpsimd
            def _(pool):
                with pool.Fori(0, B) as b:
                    ln_pool_rstd(nc, pool, t, b)
                    wait_apart(pool, t.v, b * VN + 4)
                    nc.gpsimd.tensor_scalar(t.s_me[:, :], t.s_ms[:, :], 1.0 / C, RMS_EPS, ALU.mult, ALU.add).then_inc(t.p, 1)
                    pool.wait_ge(t.p, b * 2 + 1)
                    nc.gpsimd.tensor_tensor(t.s_rr[:, :], t.s_me[:, :], t.minus_half[:, 0:NT], ALU.pow).then_inc(t.p, 1)

            @block.tensor
            def _(pe):
                await_loads(pe, t, "W1T W2T WlT BwT CwT DwT dwT")

                def pair(out, w, src, start, stop):
                    for c in range(NCH):
                        mm = nc.tensor.matmul(out(c), w, src(c), start=start, stop=stop)
                    return mm

                def cols(a):
                    return lambda c: a[:, c * CHUNK:(c + 1) * CHUNK]
                with pe.Fori(0, B) as b:
                    pe.wait_ge(t.v, b * VN + 5)
                    for j in range(NT):
                        mm = nc.tensor.transpose(t.ps_t[j // 4][:, (j % 4) * P:(j % 4 + 1) * P], t.s_xn[:, j, :], t.ident[:, :])
                    mm.then_inc(t.ln_tr, 1)
                    pe.wait_ge(t.v, b * VN + 6)
                    pair(cols(t.ps_s[0]), t.W1T[:, :], cols(t.s_xnT), True, True).then_inc(t.mm, 1)
                    pair(cols(t.ps_s[1]), t.W2T[:, :], cols(t.s_xnT), True, True).then_inc(t.mm, 1)
                    pe.wait_ge(t.sc, b * SN + 2)
                    pair(lambda c: t.ps_s[0][0:H, c * CHUNK:(c + 1) * CHUNK], t.dwT[:, :], cols(t.s_xc), True, True)\
                        .then_inc(t.mm, 1)
                    pair(lambda c: t.ps_s[1][0:H, c * CHUNK:(c + 1) * CHUNK], t.BwT[:, :], cols(t.s_xc), True, True)\
                        .then_inc(t.mm, 1)
                    pe.wait_ge(t.v, b * VN + 20)
                    for c in range(NCH):
                        nc.tensor.matmul(t.ps_s[0][:, c * CHUNK:(c + 1) * CHUNK], t.DwT[:, :],
                                         t.s_xc[:, c * CHUNK:(c + 1) * CHUNK], start=True, stop=False)
                        mm = nc.tensor.matmul(t.ps_s[0][:, c * CHUNK:(c + 1) * CHUNK], t.CwT[:, :],
                                              t.s_bb[:, c * CHUNK:(c + 1) * CHUNK], start=False, stop=True)
                    mm.then_inc(t.mm, 1)
                    pe.wait_ge(t.v, b * VN + 21)
                    for j in range(NT):
                        mm = nc.tensor.matmul(t.ps_s[1][:, j * C:(j + 1) * C], t.s_g[:, j * P:(j + 1) * P], t.WlT[:, :],
                                              start=True, stop=True)
                    mm.then_inc(t.mm, 1)

            @block.vector
            def _(dve):
                await_loads(dve, t, "conv_w conv_b norm_w Avec Bb Cb Db db")
                nc.vector.memset(t.s_ones[:, :], 1.0).then_inc(t.const_done, 1)
                nc.vector.memset(t.s_xb[:, 0:2], 0.0).then_inc(t.const_done, 1)
                nc.vector.memset(t.s_cum[:, 0:1], 0.0).then_inc(t.const_done, 1)
                nc.vector.tensor_tensor(t.s_yb[:, :], t.Cb[:, :], t.Db[:, :], ALU.add).then_inc(t.const_done, 1)
                nc.vector.scalar_tensor_tensor(out=t.s_negA[:, 0:1], in0=t.Avec[:, :], scalar=-1.0, in1=t.Avec[:, :],
                                               op0=ALU.mult, op1=ALU.min).then_inc(t.a0, 1)
                dve.wait_ge(t.a1, 2)
                nc.vector.scalar_tensor_tensor(out=t.s_negA[:, 3:4], in0=t.Avec[:, :], scalar=0.0, in1=t.s_negA[:, 2:3],
                                               op0=ALU.max, op1=ALU.add).then_inc(t.const_done, 1)
                dve.wait_ge(t.const_done, 5)
                nc.vector.tensor_scalar(t.s_negA[:, 0:1], t.s_negA[:, 3:4], -1.0, None, ALU.mult).then_inc(t.const_done, 1)
                dve.wait_ge(t.const_done, 6)
                with dve.Fori(0, B) as b:
                    v0 = b * VN
                    step = [0]

                    def does(ins, wait=True):
                        step[0] += 1
                        ins.then_inc(t.v, 1)
                        if wait:
                            dve.wait_ge(t.v, v0 + step[0])
                    ln_vector_normalise(nc, dve, t, b)
                    dve.wait_ge(t.ln_xn, b * NT + NT)
                    does(nc.vector.tensor_tensor(t.xn[:, :, :], t.xn[:, :, :],
                                                 t.ca_rows[:, ds(b, 1), :].to_broadcast([P, NT, C]), ALU.mult))
                    does(nc.vector.tensor_tensor(t.xn[:, :, :], t.xn[:, :, :],
                                                 t.sa_rows[:, ds(b, 1), :].to_broadcast([P, NT, C]), ALU.add))
                    does(nc.vector.tensor_tensor(t.s_sq[:, :, :], t.xn[:, :, :], t.xn[:, :, :], ALU.mult))
                    does(nc.vector.tensor_reduce(t.s_ms[:, :], t.s_sq[:, :, :], AX, ALU.add))
                    dve.wait_ge(t.p, b * 2 + 2)
                    does(nc.vector.tensor_tensor(t.s_xn[:, :, :], t.xn[:, :, :], bc_last(t.s_rr[:, :], C), ALU.mult))
                    assert step[0] == 5
                    dve.wait_ge(t.ln_tr, b + 1)
                    nc.vector.tensor_scalar(t.s_xnT[:, 0:CHUNK], t.ps_t[0][:, :], t.norm_w[:, 0:1], None, ALU.mult)\
                        .then_inc(t.hT_ready, 1)
                    dve.wait_ge(t.hT_ready, b + 1)
                    does(nc.vector.tensor_scalar(t.s_xnT[:, CHUNK:T], t.ps_t[1][:, :], t.norm_w[:, 0:1], None, ALU.mult))
                    assert step[0] == 6
                    dve.wait_ge(t.mm, b * MN + 1)
                    does(nc.vector.tensor_copy(t.s_xb[:, 2:2 + T], t.ps_s[0][:, :]))
                    does(nc.vector.tensor_scalar(t.s_cv[:, :], t.s_xb[:, 2:2 + T], t.conv_w[:, 2:3], None, ALU.mult))
                    tap = nc.vector.scalar_tensor_tensor(out=t.s_g[:, :], in0=t.s_xb[:, 1:1 + T], scalar=t.conv_w[:, 1:2],
                                                         in1=t.s_cv[:, :], op0=ALU.mult, op1=ALU.add)
                    tap.then_inc(t.a0, 1)
                    dve.wait_ge(t.a0, b + 2)
                    does(nc.vector.scalar_tensor_tensor(out=t.s_cv[:, :], in0=t.s_xb[:, 0:T], scalar=t.conv_w[:, 0:1],
                                                        in1=t.s_g[:, :], op0=ALU.mult, op1=ALU.add))
                    assert step[0] == 9
                    dve.wait_ge(t.mm, b * MN + 3)
                    does(nc.vector.tensor_scalar(t.s_v[:, :], t.ps_s[0][0:H, :], t.db[:, 0:1], None, ALU.add))
                    does(nc.vector.scalar_tensor_tensor(out=t.s_a[:, :], in0=t.s_v[:, :], scalar=-1.0, in1=t.s_v[:, :],
                                                        op0=ALU.mult, op1=ALU.min))
                    assert step[0] == 11
                    dve.wait_ge(t.sc, b * SN + 4)
                    does(nc.vector.scalar_tensor_tensor(out=t.s_dl[:, :], in0=t.s_v[:, :], scalar=0.0, in1=t.s_l[:, :],
                                                        op0=ALU.max, op1=ALU.add))
                    does(nc.vector.tensor_scalar(t.s_a[:, :], t.s_dl[:, :], t.s_negA[:, 0:1], None, ALU.mult))
                    dve.wait_ge(t.mm, b * MN + 4)
                    does(nc.vector.scalar_tensor_tensor(out=t.s_v[:, :], in0=t.ps_s[1][0:H, :], scalar=t.Bb[:, 0:1],
                                                        in1=t.s_dl[:, :], op0=ALU.add, op1=ALU.mult))
                    does(nc.vector.tensor_tensor_scan(t.s_cum[:, 1:1 + T], t.s_ones[:, :], t.s_a[:, :], 0.0, ALU.mult, ALU.add))
                    does(nc.vector.tensor_scalar(t.s_cum[:, 1:1 + T], t.s_cum[:, 1:1 + T], -20.0, 20.0, ALU.max, ALU.min))
                    does(nc.vector.memset(t.s_cum[:, 0:1], 0.0))
                    assert step[0] == 17
                    dve.wait_ge(t.sc, b * SN + 6)
                    does(nc.vector.tensor_tensor(t.s_a[:, :], t.s_v[:, :], t.s_e2[:, :], ALU.mult))
                    does(nc.vector.tensor_tensor_scan(t.s_dl[:, :], t.s_ones[:, :], t.s_a[:, :], 0.0, ALU.mult, ALU.add))
                    does(nc.vector.tensor_tensor(t.s_bb[:, :], t.s_dl[:, :], t.s_e1[:, :], ALU.mult))
                    assert step[0] == 20
                    dve.wait_ge(t.mm, b * MN + 5)
                    does(nc.vector.scalar_tensor_tensor(out=t.s_g[:, :], in0=t.ps_s[0][:, :], scalar=t.s_yb[:, 0:1],
                                                        in1=t.s_sz[:, :], op0=ALU.add, op1=ALU.mult))
                    assert step[0] == 21
                    dve.wait_ge(t.mm, b * MN + 6)
                    does(nc.vector.tensor_tensor(t.s_out[:, :, :], t.ps_s[1][:, :].rearrange("p (j c) -> p j c", c=C),
                                                 t.xn[:, :, :], ALU.add))
                    does(nc.vector.tensor_tensor(t.s_out[:, :, :], t.s_out[:, :, :],
                                                 t.gate_rows[:, ds(b + B, 1), 0:C].to_broadcast([P, NT, C]), ALU.mult))
                    xs = t.x[:, ds(b * NT, NT), :]
                    does(nc.vector.tensor_tensor(xs, xs, t.s_out[:, :, :], ALU.add))
                    assert step[0] == 24


def moe_global(nc, t):
    F, NF = 512, 4
    NE = EXPERTS + 1
    units = [(c, e) for c in range(NCH) for e in range(NE)]
    E8 = EXPERTS
    BITS = 30
    with ExitStack() as ctx:
        open_ffn(nc, ctx, t, 1, NF)
        open_sb(nc, ctx, t, g_hT=([P, B * T], F32), sc=([P, NTILES, E8], F32), sc_mx=([P, NTILES], F32),
                sc_sum=([P, NTILES], F32), sc_e=([P, E8, NTILES], F32), gate=([P, NTILES, NE], F32),
                gateT=([NE, B * T], F32), thr=([P, 1], I32), cand=([P, 1], I32), inc=([P, 1], I32),
                cnt=([P, 2], F32), flag=([P, E8 * NTILES], F32), rank=([P, E8 * NTILES], F32),
                tot=([P, E8 * NTILES], F32), room=([P, 1], F32), ones256=([P, E8 * NTILES], F32))
        open_sems(nc, ctx, t, "moe1_", FFN_SEMS + " lg_ps lg_done v mm gate_tr gate_ready s_exp m1")
        with nc.Block("gates") as block:
            @block.tensor
            def _(pe):
                await_loads(pe, t, "gwT")
                with pe.Fori(0, B) as b:
                    ln_tensor_transpose(nc, pe, t, b)
                    pe.wait_ge(t.hT_ready, b * NCH + NCH)
                    for c in range(NCH):
                        for j in range(4):
                            k = c * 4 + j
                            mm = nc.tensor.matmul(t.ps_o[0][:, k * E8:(k + 1) * E8], t.hid[:, 0, c, j * P:(j + 1) * P],
                                                  t.gwT[:, :], start=True, stop=True)
                    mm.then_inc(t.lg_ps, 1)
                for i in range(BITS):
                    pe.wait_ge(t.v, 7 + 3 * i)
                    nc.tensor.matmul(t.ps_o[1][:, 0:2], t.ones[:, :], t.cnt[:, :], start=True, stop=True).then_inc(t.mm, 1)
                V = 7 + 3 * BITS
                pe.wait_ge(t.v, V + 1)
                nc.tensor.matmul(t.ps_o[1][:, 0:2], t.ones[:, :], t.cnt[:, :], start=True, stop=True)
                nc.tensor.matmul(t.ps_s[0][:, 0:E8 * NTILES], t.tri[:, :], t.flag[:, :], start=True, stop=True)
                nc.tensor.matmul(t.ps_s[1][:, 0:E8 * NTILES], t.ones[:, :], t.flag[:, :], start=True, stop=True)\
                    .then_inc(t.mm, 1)
                pe.wait_ge(t.gate_ready, 1)
                for k in range(NTILES):
                    if k % 4 == 0 and k >= 8:
                        pe.wait_ge(t.m1, k // 4 - 1)
                    mm = nc.tensor.transpose(t.ps_t[k // 4 % 2][0:NE, (k % 4) * P:(k % 4 + 1) * P], t.gate[:, k, :],
                                             t.ident[:, :])
                    if k % 4 == 3:
                        mm.then_inc(t.gate_tr, 1)

            @block.vector
            def _(dve):
                n = [0]

                def does(ins):
                    n[0] += 1
                    ins.then_inc(t.v, 1)
                    dve.wait_ge(t.v, n[0])
                with dve.Fori(0, B) as b:
                    ln_vector_normalise(nc, dve, t, b)
                    ln_vector_modulate(nc, dve, t, b, 1, CB, SB, [t.hid[:, 0, c, :] for c in range(NCH)])
                    for c in range(NCH):
                        dve.wait_ge(t.hT_ready, b * NCH + (c + 1))
                        nc.vector.tensor_copy(t.g_hT[:, ds(b * T + c * CHUNK, CHUNK)], t.hid[:, 0, c, :]).then_inc(t.h_done, 1)
                    dve.wait_ge(t.lg_ps, b + 1)
                    nc.vector.tensor_copy(t.sc[:, ds(b * NT, NT), :],
                                          t.ps_o[0][:, 0:NT * E8].rearrange("p (j e) -> p j e", e=E8)).then_inc(t.lg_done, 1)
                dve.wait_ge(t.lg_done, B)
                dve.wait_ge(t.h_done, B * NCH)
                does(nc.vector.tensor_reduce(t.sc_mx[:, :], t.sc[:, :, :], AX, ALU.max))
                does(nc.vector.tensor_tensor(t.sc[:, :, :], t.sc[:, :, :], bc_last(t.sc_mx[:, :], E8), ALU.subtract))
                dve.wait_ge(t.s_exp, 1)
                does(nc.vector.tensor_reduce(t.sc_sum[:, :], t.sc[:, :, :], AX, ALU.add))
                does(nc.vector.reciprocal(t.sc_mx[:, :], t.sc_sum[:, :]))
                does(nc.vector.tensor_tensor(t.sc_e[:, :, :].rearrange("p e n -> p n e"), t.sc[:, :, :],
                                             bc_last(t.sc_mx[:, :], E8), ALU.mult))
                does(nc.vector.memset(t.cnt[:, :], 0.0))
                flat = t.sc_e[:, :, :].rearrange("p e n -> p (e n)")
                nc.vector.memset(t.ones256[:, :], 1.0).then_inc(t.act_done, 1)
                nc.vector.memset(t.thr[:, :], 0).then_inc(t.act_done, 1)
                nc.vector.memset(t.cand[:, :], 1 << (BITS - 1)).then_inc(t.act_done, 1)
                dve.wait_ge(t.act_done, 3)
                for i in range(BITS):
                    bit = 1 << (BITS - 1 - i)
                    does(nc.vector.tensor_scalar(t.flag[:, :], flat, t.cand[:, :].bitcast(F32), None, ALU.is_ge, ALU.add,
                                                 accum_out=t.cnt[:, 0:1]))
                    assert n[0] == 7 + 3 * i
                    dve.wait_ge(t.mm, i + 1)
                    does(nc.vector.tensor_scalar(t.inc[:, :], t.ps_o[1][:, 0:1], float(TOPK_ALL), float(bit),
                                                 ALU.is_ge, ALU.mult))
                    nc.vector.scalar_tensor_tensor(out=t.cand[:, :], in0=t.inc[:, :], scalar=bit >> 1, in1=t.thr[:, :],
                                                   op0=ALU.bitwise_or, op1=ALU.bitwise_or).then_inc(t.y_done, 1)
                    dve.wait_ge(t.y_done, i + 1)
                    does(nc.vector.tensor_tensor(t.thr[:, :], t.inc[:, :], t.thr[:, :], ALU.bitwise_or))
                thr = t.thr[:, :].bitcast(F32)
                does(nc.vector.tensor_scalar(t.rank[:, :], flat, thr, None, ALU.is_gt, ALU.add, accum_out=t.cnt[:, 0:1]))
                does(nc.vector.tensor_scalar(t.flag[:, :], flat, thr, None, ALU.is_equal))
                assert n[0] == 8 + 3 * BITS
                dve.wait_ge(t.mm, BITS + 1)
                does(nc.vector.tensor_scalar(t.room[:, :], t.ps_o[1][:, 0:1], -1.0, float(TOPK_ALL), ALU.mult, ALU.add))
                does(nc.vector.tensor_copy(t.tot[:, :], t.ps_s[1][:, 0:E8 * NTILES]))
                does(nc.vector.tensor_tensor_scan(t.ones256[:, :], t.ones256[:, :], t.tot[:, :], 0.0, ALU.mult, ALU.add))
                does(nc.vector.tensor_tensor(t.tot[:, :], t.ones256[:, :], t.tot[:, :], ALU.subtract))
                does(nc.vector.tensor_tensor(t.tot[:, :], t.ps_s[0][:, 0:E8 * NTILES], t.tot[:, :], ALU.add))
                does(nc.vector.scalar_tensor_tensor(out=t.tot[:, :], in0=t.tot[:, :], scalar=t.room[:, 0:1], in1=t.flag[:, :],
                                                    op0=ALU.is_lt, op1=ALU.mult))
                does(nc.vector.tensor_tensor(t.rank[:, :], t.rank[:, :], t.tot[:, :], ALU.add))
                does(nc.vector.memset(t.gate[:, :, 0:1], 1.0))
                nc.vector.tensor_tensor(t.gate[:, :, 1:NE], t.rank[:, :].rearrange("p (e n) -> p n e", e=E8),
                                        t.sc_e[:, :, :].rearrange("p e n -> p n e"), ALU.mult).then_inc(t.gate_ready, 1)
                for k in range(NTILES // 4):
                    dve.wait_ge(t.gate_tr, k + 1)
                    nc.vector.tensor_copy(t.gateT[:, k * CHUNK:(k + 1) * CHUNK], t.ps_t[k % 2][0:NE, :]).then_inc(t.m1, 1)

            @block.scalar
            def _(act):
                act.wait_ge(t.v, 2)
                nc.scalar.activation(t.sc[:, :, :], t.sc[:, :, :], ACT.Exp).then_inc(t.s_exp, 1)

            @block.gpsimd
            def _(pool):
                with pool.Fori(0, B) as b:
                    ln_pool_rstd(nc, pool, t, b)

        open_sems(nc, ctx, t, "moe1b_", "h_done act_done y_done acc_done gated_done x_done gT_here")
        open_sb(nc, ctx, t, gT=([NE, T], F32), e_hT=([P, T], F32), gb=([P, NT, NE], F32))
        with nc.Block("experts") as block:
            @block.tensor
            def _(pe):
                await_loads(pe, t, "f1_w1 f1_w2 b2_rows")

                def biases(c, j, out):
                    return nc.tensor.matmul(out, t.gT[:, c * CHUNK + j * P:c * CHUNK + (j + 1) * P], t.b2_rows[:, :],
                                            start=False, stop=True)
                with pe.Fori(0, B) as b:
                    pe.wait_ge(t.gT_here, b + 1)
                    experts_tensor(nc, pe, t, b, lambda e, f: t.f1_w1[:, e, f * P:(f + 1) * P],
                                   lambda e, f: t.f1_w2[:, e, f, :],
                                   lambda c: t.g_hT[:, ds(b * T + c * CHUNK, CHUNK)], NF, units, biases)

            @block.vector
            def _(dve):
                with dve.Fori(0, B) as b:
                    nc.vector.tensor_copy(t.gT[:, :], t.gateT[:, ds(b * T, T)]).then_inc(t.gT_here, 1)
                    experts_vector(nc, dve, t, b, units, lambda b, c, j, e: None if e == 0 else
                                   t.gate[:, ds(b * NT + (4 * c + j), 1), e:e + 1].rearrange("p a e -> p (a e)"), 1, NE)

            @block.scalar
            def _(act):
                await_loads(act, t, "b1_cols")
                with act.Fori(0, B) as b:
                    experts_scalar(nc, act, t, b, NF, units, ACT.Gelu_apprx_tanh,
                                   lambda e, f: t.b1_cols[:, e * NF + f:e * NF + f + 1])


def spiking_mlp(nc, t):
    NF = 4
    with ExitStack() as ctx:
        open_ffn(nc, ctx, t, 2, NF)
        open_sb(nc, ctx, t, f2_hT=([P, T], F32), f2_r=([P, 2, NF, CHUNK], F32), f2_y=([P, 4, C], F32),
                f2_n=([P, 4, C], F32), f2_t=([P, 4, C], F32))
        open_sems(nc, ctx, t, "mlp2_", FFN_SEMS + " sq_done v fires")
        V = 2 + 2 * (SEQ_STEPS - 1)
        with nc.Block() as block:
            @block.tensor
            def _(pe):
                await_loads(pe, t, "f2_w1 f2_w2")
                with pe.Fori(0, B) as b:
                    ln_tensor_transpose(nc, pe, t, b)
                    pe.wait_ge(t.hT_ready, b * NCH + NCH)
                    for c in range(NCH):
                        for f in range(NF):
                            if c:
                                pe.wait_ge(t.sq_done, b * (NCH * NF) + (f + 1))
                            nc.tensor.matmul(t.ps_h[f], t.f2_w1[:, f * P:(f + 1) * P], t.f2_hT[:, c * CHUNK:(c + 1) * CHUNK],
                                             start=True, stop=True).then_inc(t.h_done, 1)
                    for c in range(NCH):
                        pe.wait_ge(t.sq_done, b * (NCH * NF) + (c + 1) * NF)
                        for j in range(4):
                            for f in range(NF):
                                mm = nc.tensor.matmul(t.ps_y[c][:, j * C:(j + 1) * C], t.hid[:, c, f, j * P:(j + 1) * P],
                                                      t.f2_w2[:, f, :], start=(f == 0), stop=(f == NF - 1))
                        mm.then_inc(t.y_done, 1)

            @block.scalar
            def _(act):
                with act.Fori(0, B) as b:
                    for i in range(NCH * NF):
                        act.wait_ge(t.h_done, b * (NCH * NF) + (i + 1))
                        nc.scalar.activation(t.f2_r[:, i // NF, i % NF, :], t.ps_h[i % 4], ACT.Relu).then_inc(t.act_done, 1)

            @block.vector
            def _(dve):
                with dve.Fori(0, B) as b:
                    ln_vector_normalise(nc, dve, t, b)
                    ln_vector_modulate(nc, dve, t, b, 2, CB, SB,
                                       [t.f2_hT[:, c * CHUNK:(c + 1) * CHUNK] for c in range(NCH)])
                    for i in range(NCH * NF):
                        dve.wait_ge(t.act_done, b * (NCH * NF) + (i + 1))
                        nc.vector.tensor_tensor(t.hid[:, i // NF, i % NF, :], t.ps_h[i % 4], t.f2_r[:, i // NF, i % NF, :],
                                                ALU.mult).then_inc(t.sq_done, 1)
                    for c in range(NCH):
                        v0 = (b * NCH + c) * V
                        dve.wait_ge(t.y_done, b * NCH + (c + 1))
                        nc.vector.tensor_copy(t.f2_y[:, :, :], t.ps_y[c][:, :].rearrange("p (j c) -> p j c", c=C)).then_inc(t.v, 1)
                        dve.wait_ge(t.v, v0 + 1)
                        nc.vector.tensor_scalar(t.f2_n[:, :, :], t.f2_y[:, :, :], -1.0, None, ALU.mult).then_inc(t.v, 1)
                        nc.vector.tensor_scalar(t.acc[:, :, :], t.f2_y[:, :, :], 1.0, None, ALU.is_gt).then_inc(t.fires, 1)
                        for s in range(1, SEQ_STEPS):
                            dve.wait_ge(t.v, v0 + 2 * s)
                            nc.vector.scalar_tensor_tensor(out=t.f2_t[:, :, :], in0=t.f2_n[:, :, :], scalar=-0.9,
                                                           in1=t.f2_y[:, :, :], op0=ALU.mult, op1=ALU.add).then_inc(t.v, 1)
                            dve.wait_ge(t.v, v0 + (2 * s + 1))
                            nc.vector.scalar_tensor_tensor(out=t.f2_n[:, :, :], in0=t.f2_n[:, :, :], scalar=-1.0,
                                                           in1=t.f2_t[:, :, :], op0=ALU.is_lt, op1=ALU.subtract).then_inc(t.v, 1)
                            dve.wait_ge(t.v, v0 + (2 * s + 2))
                            dve.wait_ge(t.fires, (b * NCH + c) * SEQ_STEPS + s)
                            nc.vector.scalar_tensor_tensor(out=t.acc[:, :, :], in0=t.f2_n[:, :, :], scalar=-1.0,
                                                           in1=t.acc[:, :, :], op0=ALU.is_lt, op1=ALU.add).then_inc(t.fires, 1)
                        dve.wait_ge(t.fires, (b * NCH + c) * SEQ_STEPS + SEQ_STEPS)
                        nc.vector.tensor_scalar(t.acc[:, :, :], t.acc[:, :, :], 1.0 / SEQ_STEPS, None, ALU.mult).then_inc(t.acc_done, 1)
                        dve.wait_ge(t.acc_done, b * NCH + (c + 1))
                        ffn_residual(nc, dve, t, b, c, 2)

            @block.gpsimd
            def _(pool):
                with pool.Fori(0, B) as b:
                    ln_pool_rstd(nc, pool, t, b)


def linear_chain(nc, t, out):
    with ExitStack() as ctx:
        open_ffn(nc, ctx, t, 3, 1)
        open_sb(nc, ctx, t, f3_hT=([P, T], F32), f3_a=([P, T], F32), f3_b=([P, T], F32))
        open_sems(nc, ctx, t, "chain3_", FFN_SEMS + " m1 m2 c1 c2 stored")
        with nc.Block() as block:
            @block.sync
            def _(sp):
                with sp.Fori(0, B) as b:
                    sp.wait_ge(t.x_done, b * NCH + NCH)
                    sp.dma_start(out.rearrange("(b n p) c -> p b n c", p=P, n=NT)[:, ds(b, 1), :, :],
                                 t.x[:, ds(b * NT, NT), :].unsqueeze(1)).then_inc(t.stored, 16)
                sp.wait_ge(t.stored, 16 * B)

            @block.tensor
            def _(pe):
                await_loads(pe, t, "f3_w f3_a1 f3_a2 f3_bias")
                with pe.Fori(0, B) as b:
                    ln_tensor_transpose(nc, pe, t, b)
                    pe.wait_ge(t.hT_ready, b * NCH + NCH)
                    for w, src, ps, done, before in ((t.f3_w, t.f3_hT, t.ps_s[0], t.m1, None),
                                                     (t.f3_a1, t.f3_a, t.ps_s[1], t.m2, t.c1)):
                        if before:
                            pe.wait_ge(before, b + 1)
                        for c in range(NCH):
                            mm = nc.tensor.matmul(ps[:, c * CHUNK:(c + 1) * CHUNK], w[:, :], src[:, c * CHUNK:(c + 1) * CHUNK],
                                                  start=True, stop=True)
                        mm.then_inc(done, 1)
                    pe.wait_ge(t.c2, b + 1)
                    for c in range(NCH):
                        for j in range(4):
                            at = c * CHUNK + j * P
                            mm = nc.tensor.matmul(t.ps_y[c][:, j * C:(j + 1) * C], t.f3_b[:, at:at + P], t.f3_a2[:, :],
                                                  start=True, stop=True)
                        mm.then_inc(t.y_done, 1)

            @block.scalar
            def _(act):
                with act.Fori(0, B) as b:
                    act.wait_ge(t.m1, b + 1)
                    nc.scalar.copy(t.f3_a[:, :], t.ps_s[0][:, :]).then_inc(t.c1, 1)
                    act.wait_ge(t.m2, b + 1)
                    nc.scalar.copy(t.f3_b[:, :], t.ps_s[1][:, :]).then_inc(t.c2, 1)
                    for c in range(NCH):
                        act.wait_ge(t.h_done, b * NCH + (c + 1))
                        nc.scalar.activation(t.hid[:, c, 0, :], t.hid[:, c, 0, :], ACT.Tanh).then_inc(t.act_done, 1)

            @block.vector
            def _(dve):
                with dve.Fori(0, B) as b:
                    ln_vector_normalise(nc, dve, t, b)
                    ln_vector_modulate(nc, dve, t, b, 3, CB, SB,
                                       [t.f3_hT[:, c * CHUNK:(c + 1) * CHUNK] for c in range(NCH)])
                    for c in range(NCH):
                        dve.wait_ge(t.y_done, b * NCH + (c + 1))
                        nc.vector.tensor_tensor(t.hid[:, c, 0, :].rearrange("p (j c) -> p j c", c=C),
                                                t.ps_y[c][:, :].rearrange("p (j c) -> p j c", c=C),
                                                bc_tiles(t.f3_bias[:, :], 4), ALU.add).then_inc(t.h_done, 1)
                    for c in range(NCH):
                        dve.wait_ge(t.act_done, b * NCH + (c + 1))
                        nc.vector.tensor_copy(t.acc[:, :, :], t.hid[:, c, 0, :].rearrange("p (j c) -> p j c", c=C)).then_inc(t.acc_done, 1)
                        dve.wait_ge(t.acc_done, b * NCH + (c + 1))
                        ffn_residual(nc, dve, t, b, c, 3)

            @block.gpsimd
            def _(pool):
                with pool.Fori(0, B) as b:
                    ln_pool_rstd(nc, pool, t, b)


ALWAYS = [
    ("router", [P, EXPERTS]), ("iota8", [P, EXPERTS]),
    ("W1T", [P, C]), ("W2T", [P, C]), ("WlT", [P, C]), ("BwT", [P, 64]), ("CwT", [64, C]), ("DwT", [P, C]),
    ("dwT", [P, 64]), ("conv_w", [P, 3]), ("conv_b", [P, 1]), ("norm_w", [P, 1]), ("Avec", [64, 1]), ("Bb", [64, 1]),
    ("Cb", [P, 1]), ("Db", [P, 1]), ("db", [64, 1]),
    ("gwT", [P, EXPERTS]), ("b1_cols", [P, 9 * 4]), ("b2_rows", [9, C]),
]
LATENT = [
    ("ca_w", [P, 3, C]), ("ca_b", [P, 3]), ("bd_q", [P, 512]), ("bd_kv", [P, 512]), ("bd_o", [P, 512]),
    ("rot", [P, P]), ("wqk_rep", [P, 4, P]), ("sel_rep", [P, 4, P]), ("qlb", [P, 1]), ("kvlb_col", [P, 1]), ("kvlb_rows", [P, 512]),
    ("wqk_b", [P, 1]), ("l2ob", [P, 1]), ("cprojT", [P, C]), ("cpb_rows", [P, C]), ("cos", [P, T]), ("sin", [P, T]),
]
EXPERTS0 = [("f0_w1", [P, EXPERTS, 256]), ("f0_w2", [P, EXPERTS, 2, C])]
EXPERTS1 = [("f1_w1", [P, 9, 512]), ("f1_w2", [P, 9, 4, C])]
LATE = [
    ("w_out2", [P, 8, C]), ("f2_w1", [P, 512]), ("f2_w2", [P, 4, C]),
    ("w_out3", [P, 8, C]), ("f3_w", [P, C]), ("f3_a1", [P, C]), ("f3_a2", [P, C]), ("f3_bias", [P, C]),
]
ROW_VECTORS = {"kvlb_rows", "cpb_rows", "f3_bias"}


def open_weights(nc, ctx, t, dram, label, group):
    loads = []
    landed = ctx.enter_context(nc.semaphore(label + "_loaded"))
    t.finished.append(landed)
    for name, shape in group:
        open_sb(nc, ctx, t, **{name: (shape, F32)})
        t.loads[name] = (landed, 16 * len(group))
        dst = t[name]
        src = dram[name]
        if name in ROW_VECTORS:
            src = src.to_broadcast([P, shape[1]])
        loads.append((name, dst[tuple(slice(None) for _ in shape)], src))
    return loads


def load_weights(nc, t, label, loads):
    with nc.Block(label + "_weights") as block:
        @block.sync
        def _(sp):
            for name, dst, src in loads:
                sp.dma_start(dst, src).then_inc(t.loads[name][0], 16)
            if DEBUG:
                await_loads(sp, t, loads[0][0])


def build(nc, dram, out, last=99, first=0):
    t = Ctx()
    t["finished"] = []
    with ExitStack() as ctx:
        APART["sem"] = ctx.enter_context(nc.semaphore("waits_apart"))
        open_sb(nc, ctx, t, x=([P, NTILES, C], F32), ident=([P, P], F32), ident16=([P, P], BF16), maskp=([P, P], BF16),
                tri=([P, P], F32), ones=([P, P], F32), minus_half=([P, NT], F32), modT=([P, LAYERS * 6 * B], F32),
                gate_rows=([P, LAYERS * B, 2 * C], F32), sa_rows=([P, B, C], F32), ca_rows=([P, B, C], F32))
        t["ps_s"] = [ctx.enter_context(nc.psum_tensor(f"ps_s{i}", [P, 2 * CHUNK], F32)) for i in range(2)]
        t["ps_tt"], t["ps_oo"] = (ctx.enter_context(nc.psum_tensor(n, [P, 2 * CHUNK], F32)) for n in ("ps_t", "ps_o"))
        t["ps_t"] = [t.ps_tt[:, i * CHUNK:(i + 1) * CHUNK] for i in range(2)]
        t["ps_o"] = [t.ps_oo[:, i * CHUNK:(i + 1) * CHUNK] for i in range(2)]
        open_sems(nc, ctx, t, "", "x_loaded x_out")
        t["w_out"], t["loads"] = {}, {}
        loads = open_weights(nc, ctx, t, dram, "always", ALWAYS)
        with ExitStack() as early:
            loads += open_weights(nc, early, t, dram, "experts0", EXPERTS0)
            with ExitStack() as latent:
                loads = open_weights(nc, latent, t, dram, "latent", LATENT) + loads
                open_sb(nc, latent, t, w_lat=([P, 4, 3 * C], F32), w_out_lat=([P, 4, C], F32), lat_b=([P, 8], F32),
                        v_b_rows=([P, 4, C], F32), out_b_rows=([P, C], F32), low_copies=([P, 1], F32))
                open_sems(nc, latent, t, "", "w_out_lat_ready")
                t.w_out[0], t.loads["w_out0"] = t.w_out_lat, (t.w_out_lat_ready, 1)
                setup(nc, t, dram, loads)
                if first < 1 <= last:
                    attention(nc, t, 0, 4, 4, LatentProjection(LATENT_DIM), stage_on_chip, compose_latent)
            load_weights(nc, t, "experts1", open_weights(nc, early, t, dram, "experts1", EXPERTS1))
            if first < 2 <= last:
                moe_top2(nc, t)
            if first < 3 <= last:
                gated_scan(nc, t)
            if first < 4 <= last:
                moe_global(nc, t)
        with nc.Block("recycle") as block:
            @block.gpsimd
            def _(pool):
                for sem in t.finished:
                    pool.sem_clear(sem)
        loads = open_weights(nc, ctx, t, dram, "late", LATE)
        load_weights(nc, t, "late", loads)
        for layer in (2, 3):
            t.w_out[layer] = t[f"w_out{layer}"]
        if first < 5 <= last:
            plain = PlainProjection(64, 2, 2)
            attention(nc, t, 2, 8, 2, plain, stage_from_dram(dram["wqkv2"], len(plain.units)))
        if first < 6 <= last:
            spiking_mlp(nc, t)
        if first < 7 <= last:
            plain = PlainProjection(64, 2, 1)
            attention(nc, t, 3, 8, 2, plain, stage_from_dram(dram["wqkv3"], len(plain.units)))
        if first < 8 <= last:
            linear_chain(nc, t, out)
        else:
            with nc.Block() as block:
                @block.sync
                def _(sp):
                    await_loads(sp, t, " ".join(name for name, _, _ in loads))
                    sp.dma_start(out.rearrange("(n p) c -> p n c", p=P), t.x[:, :, :]).then_inc(t.x_out, 16)
                    sp.wait_ge(t.x_out, 16)


def block_diagonal(block, times):
    r, c = block.shape
    m = np.zeros((r * times, c * times), block.dtype)
    for i in range(times):
        m[i * r:(i + 1) * r, i * c:(i + 1) * c] = block
    return m


def four_times(block):
    m = np.zeros((P, 4, P), block.dtype)
    for h in range(4):
        m[h * 32:(h + 1) * 32, h, :] = np.concatenate([block] * 4, axis=1)
    return m


def twice(w):
    h = w.reshape(C, -1, 2, 1, 64)
    return np.concatenate([h, h], axis=3).transpose(1, 0, 2, 3, 4).reshape(-1, C, 2 * C)


def rotary_tables(latent):
    inv = (np.float32(1.0) / np.power(np.float32(10000.0), np.arange(0, latent, 2, dtype=np.float32) / np.float32(latent)))
    freqs = np.outer(np.arange(T, dtype=np.float32), inv.astype(np.float32)).astype(np.float32)
    cos = np.tile(np.repeat(np.cos(freqs), 2, axis=1).T, (4, 1)).astype(np.float32)
    sin = np.tile(np.repeat(np.sin(freqs), 2, axis=1).T, (4, 1)).astype(np.float32)
    rot = np.zeros((P, P), np.float32)
    for j in range(0, P, 2):
        rot[j + 1, j] = -1.0
        rot[j, j + 1] = 1.0
    return np.ascontiguousarray(cos), np.ascontiguousarray(sin), rot


def layout(i):
    i = {k: np.asarray(v) for k, v in i.items()}
    a = {}
    a["x"] = i["L0_attn_x"].reshape(B * T, C)
    a["cT"] = np.concatenate([i[f"L{l}_c"].T for l in range(LAYERS)], axis=1)
    a["wmod"] = np.stack([i[f"L{l}_wmod"] for l in range(LAYERS)])
    p = "L0_attn_"
    a["ca_w"] = i[p + "c_attn_w"].reshape(3, P, C).transpose(1, 0, 2)
    a["ca_b"] = i[p + "c_attn_b"].reshape(3, P).T
    a["bd_q"] = block_diagonal(i[p + "q2l_w"].T, 16)
    a["bd_kv"] = block_diagonal(i[p + "kv2l_w"].T, 16)
    a["bd_o"] = block_diagonal(i[p + "l2o_w"], 16)
    a["cos"], a["sin"], a["rot"] = rotary_tables(32)
    a["wqk_rep"], a["sel_rep"] = (four_times(m) for m in (i[p + "wqk_w"].T, np.eye(32, dtype=np.float32)))
    a["qlb"] = np.tile(i[p + "q2l_b"], 4)[:, None]
    a["kvlb_col"] = np.tile(i[p + "kv2l_b"], 4)[:, None]
    a["kvlb_rows"] = np.tile(i[p + "kv2l_b"], 16)[None, :]
    a["wqk_b"] = np.tile(i[p + "wqk_b"], 4)[:, None]
    a["l2ob"] = np.tile(i[p + "l2o_b"], 16)[:, None]
    a["cprojT"] = i[p + "cproj_w"].T
    a["cpb_rows"] = i[p + "cproj_b"][None, :]
    a["router"] = i["L0_ffn_router_w"].T
    a["iota8"] = np.tile(np.arange(EXPERTS, dtype=np.float32), (P, 1))
    a["f0_w1"] = i["L0_ffn_w1"].transpose(1, 0, 2)
    a["f0_w2"] = i["L0_ffn_w2"].reshape(EXPERTS, 2, P, C).transpose(2, 0, 1, 3)
    p = "L1_attn_"
    for name, key in (("W1T", "W1"), ("W2T", "W2"), ("WlT", "Wlast"), ("BwT", "Bw"), ("CwT", "Cw"), ("DwT", "Dw"), ("dwT", "dw")):
        a[name] = i[p + key].T
    a["conv_w"] = i[p + "conv_w"]
    for name, key in (("conv_b", "conv_b"), ("norm_w", "norm_w"), ("Avec", "A"), ("Bb", "Bb"), ("Cb", "Cb"), ("Db", "Db"), ("db", "db")):
        a[name] = i[p + key][:, None]
    p = "L1_ffn_"
    a["gwT"] = i[p + "gate_weight"].T
    b1 = np.concatenate([i[p + "bs1"][None], i[p + "b1"]])
    a["b1_cols"] = b1.reshape(9 * 4, P).T
    a["b2_rows"] = np.concatenate([i[p + "bs2"][None], i[p + "b2"]])
    a["f1_w1"] = np.concatenate([i[p + "Ws1"][None], i[p + "W1"]]).transpose(1, 0, 2)
    a["f1_w2"] = np.concatenate([i[p + "Ws2"][None], i[p + "W2"]]).reshape(9, 4, P, C).transpose(2, 0, 1, 3)
    q, k, v = np.split(i["L2_attn_W_qkv"], 3, axis=1)
    a["wqkv2"] = np.concatenate([twice(q), twice(k), v.reshape(C, 8, C).transpose(1, 0, 2)], axis=2)
    a["w_out2"] = i["L2_attn_W_out"].reshape(8, P, C).transpose(1, 0, 2)
    a["f2_w1"] = i["L2_ffn_W_fc"].T
    a["f2_w2"] = i["L2_ffn_W_proj"].T.reshape(4, P, C).transpose(1, 0, 2)
    kv = [np.repeat(np.concatenate([m.reshape(4, 64, C)] * 2, axis=1), 2, axis=0).transpose(0, 2, 1)
          for m in (i["L3_attn_Wk"], i["L3_attn_Wv"])]
    a["wqkv3"] = np.concatenate([twice(i["L3_attn_Wq"].T)] + kv, axis=2)
    a["w_out3"] = i["L3_attn_Wo"].T.reshape(8, P, C).transpose(1, 0, 2)
    a["f3_w"], a["f3_a1"], a["f3_a2"] = i["L3_ffn_weight"], i["L3_ffn_aux_weight1"], i["L3_ffn_aux_weight2"]
    a["f3_bias"] = i["L3_ffn_bias"][None, :]
    return {k: np.ascontiguousarray(v) for k, v in a.items()}


def program(nc, arrays, last=99, first=0):
    dram = {k: nc.dram_tensor("in_" + k, list(v.shape), F32, kind="ExternalInput").ap() for k, v in arrays.items()}
    out = nc.dram_tensor("out_x", [B * T, C], F32, kind="ExternalOutput").ap()
    build(nc, dram, out, last, first)


def kernel(**inputs):
    import concourse.bacc as bacc
    from concourse.bass_utils import run_bass_kernel_spmd
    arrays = layout(inputs)
    nc = bacc.Bacc("TRN2", target_bir_lowering=False, num_devices=1)
    program(nc, arrays)
    r = run_bass_kernel_spmd(nc, [{"in_" + k: v for k, v in arrays.items()}], core_ids=[0])
    return r.results[0]["out_x"].reshape(B, T, C)
```
